# Optimizing a Trainium2 kernel written in Bass

```python
import numpy as np
import jax
import jax.numpy as jnp

def _softmax(x, axis=-1):
    return jax.nn.softmax(x, axis=axis)
def _gelu(x):
    return jax.nn.gelu(x, approximate=True)
def _silu(x):
    return jax.nn.silu(x)
def _sigmoid(x):
    return jax.nn.sigmoid(x)
def _layernorm(x, axis=-1, eps=1e-5):
    m = jnp.mean(x, axis=axis, keepdims=True)
    v = jnp.var(x, axis=axis, keepdims=True)
    return (x - m) / jnp.sqrt(v + eps)
def _scatter_add(tgt, idx, src, axis=0):
    return tgt.at[idx].add(src)
def _segment_sum(src, seg, n):
    return jax.ops.segment_sum(src, seg, n)

kernel_name = 'mk_adj_resnorm_d4_adj_64_10cda7'

def setup_inputs(seed: int = 0):
    np.random.seed(seed)
    _w = jnp.asarray
    def _rec_inputs():
        import jax
        import jax.numpy as jnp
        _gk = jax.random.key(seed)
        x = -9.806e-05 + 1 * jax.random.normal(jax.random.fold_in(_gk, 1), (4096, 64), jnp.float32)
        _a = jax.random.bernoulli(jax.random.fold_in(_gk, 2), 0.0078125, (4096, 4096))
        _a = jnp.logical_or(_a, jnp.swapaxes(_a, -1, -2))
        _a = jnp.logical_or(_a, jnp.eye(4096, dtype=bool))
        _af = _a.astype(jnp.float32)
        _af = _af * jax.random.uniform(jax.random.fold_in(_gk, 3), (4096, 4096), jnp.float32, 0.05, 0.0598829)
        adj = _af
        return x, adj
    x, adj = _rec_inputs()
    def _L0_gnn_setup():
        import jax, jax.numpy as jnp
        import numpy as np
        N = 8192
        F_IN = 64
        F_OUT = 64
        K = 4
        key = jax.random.key(seed)
        k1, k2, k3 = jax.random.split(key, 3)
        x = jax.random.normal(k1, (N, F_IN), dtype=jnp.float32)
        L = jax.random.normal(k2, (N, N), dtype=jnp.float32) * (1.0 / np.sqrt(N))
        weight = jax.random.normal(k3, (K, F_IN, F_OUT), dtype=jnp.float32) * (1.0 / np.sqrt(F_IN))
        return {'x': x, 'L': L, 'weight': weight}
    _L0_gnn_all = _L0_gnn_setup()
    _L0_gnn_in = {k: v for k, v in _L0_gnn_all.items() if k in ('weight', )}
    del _L0_gnn_all

    def _L1_gnn_setup():
        import jax, jax.numpy as jnp
        import numpy as np
        N = 8192
        H = 64
        ALPHA = 0.2
        NEG_INF = -9000000000000000.0

        def gru_cell(x, h, w_ih, w_hh, b_ih, b_hh):
            gi = x @ w_ih.T + b_ih
            gh = h @ w_hh.T + b_hh
            ir, iz, inn = jnp.split(gi, 3, axis=1)
            hr, hz, hn = jnp.split(gh, 3, axis=1)
            r = jax.nn.sigmoid(ir + hr)
            z = jax.nn.sigmoid(iz + hz)
            n = jnp.tanh(inn + r * hn)
            return (1.0 - z) * n + z * h

        def gat(h, node_adj, edge_adj, W, a):
            hw = h @ W
            h_plus = (node_adj > 0).astype(hw.dtype) @ hw
            h_minus = (node_adj < 0).astype(hw.dtype) @ hw
            e_plus = jax.nn.leaky_relu(jnp.concatenate([h_plus, h_minus], axis=1) @ a, ALPHA)
            e_minus = jax.nn.leaky_relu(jnp.concatenate([h_minus, h_plus], axis=1) @ a, ALPHA)
            att = jnp.where(edge_adj > 0, e_plus, NEG_INF)
            att = jnp.where(edge_adj < 0, e_minus, att)
            att = jax.nn.softmax(att, axis=1)
            return att * edge_adj @ hw
        key = jax.random.key(seed)
        ks = jax.random.split(key, 12)
        f32 = jnp.float32
        inp = {'h': jax.random.normal(ks[0], (N, H), f32), 'node_adj': jax.random.normal(ks[1], (N, N), f32), 'edge_adj': jax.random.normal(ks[2], (N, N), f32), 'W_gat': jax.random.normal(ks[3], (H, H), f32) * (1.414 * np.sqrt(6.0 / (2 * H))), 'a_gat': jax.random.normal(ks[4], (2 * H, 1), f32) * (1.414 * np.sqrt(6.0 / (2 * H + 1))), 'w_ih_e': jax.random.normal(ks[5], (3 * H, 2 * H), f32) * 0.01, 'w_hh_e': jax.random.normal(ks[6], (3 * H, H), f32) * 0.01, 'b_ih_e': jnp.zeros((3 * H,), f32), 'b_hh_e': jnp.zeros((3 * H,), f32), 'w_ih_n': jax.random.normal(ks[7], (3 * H, H), f32) * 0.01, 'w_hh_n': jax.random.normal(ks[8], (3 * H, H), f32) * 0.01, 'b_ih_n': jnp.zeros((3 * H,), f32), 'b_hh_n': jnp.zeros((3 * H,), f32)}
        return inp
    _L1_gnn_all = _L1_gnn_setup()
    _L1_gnn_in = {k: v for k, v in _L1_gnn_all.items() if k in ('W_gat', 'a_gat', 'w_ih_e', 'w_hh_e', 'b_ih_e', 'b_hh_e', 'w_ih_n', 'w_hh_n', 'b_ih_n', 'b_hh_n', )}
    del _L1_gnn_all

    def _L2_gnn_setup():
        import jax, jax.numpy as jnp
        import numpy as np
        N, D_IN, D_OUT = (8192, 64, 64)
        MAX_NEIGH = 100
        DECAY = 0.5
        key = jax.random.key(seed)
        k1, k2, k3, k4 = jax.random.split(key, 4)
        stdv = 1.0 / np.sqrt(D_OUT)
        inputs = {'input': jax.random.normal(k1, (N, D_IN), dtype=jnp.float32), 'adj': jax.random.randint(k2, (N, N), 0, 2).astype(jnp.float32), 'weight': jax.random.uniform(k3, (D_IN, D_OUT), minval=-stdv, maxval=stdv, dtype=jnp.float32), 'bias': jax.random.uniform(k4, (D_OUT,), minval=-stdv, maxval=stdv, dtype=jnp.float32)}
        return inputs
    _L2_gnn_all = _L2_gnn_setup()
    _L2_gnn_in = {k: v for k, v in _L2_gnn_all.items() if k in ('weight', 'bias', )}
    del _L2_gnn_all

    def _L3_gnn_setup():
        import jax, jax.numpy as jnp
        import numpy as np
        CURV = 1.0
        MIN_NORM = 1e-15
        TANH_CLIP = 1.0 - 1e-05

        def _mobius_add(x, y, c):
            x2 = jnp.sum(x * x, axis=-1, keepdims=True)
            y2 = jnp.sum(y * y, axis=-1, keepdims=True)
            xy = jnp.sum(x * y, axis=-1, keepdims=True)
            num = (1.0 + 2.0 * c * xy + c * y2) * x + (1.0 - c * x2) * y
            den = 1.0 + 2.0 * c * xy + c ** 2 * x2 * y2
            return num / jnp.maximum(den, MIN_NORM)

        def _logmap(x, y, c):
            sub = _mobius_add(-x, y, c)
            sub_norm = jnp.maximum(jnp.linalg.norm(sub, axis=-1, keepdims=True), MIN_NORM)
            x2 = jnp.sum(x * x, axis=-1, keepdims=True)
            lam_x = 2.0 / jnp.maximum(1.0 - c * x2, MIN_NORM)
            sqrt_c = jnp.sqrt(c)
            arg = jnp.clip(sqrt_c * sub_norm, 0.0, TANH_CLIP)
            return 2.0 / (sqrt_c * lam_x) * jnp.arctanh(arg) * sub / sub_norm

        def _expmap(x, v, c):
            v_norm = jnp.maximum(jnp.linalg.norm(v, axis=-1, keepdims=True), MIN_NORM)
            x2 = jnp.sum(x * x, axis=-1, keepdims=True)
            lam_x = 2.0 / jnp.maximum(1.0 - c * x2, MIN_NORM)
            sqrt_c = jnp.sqrt(c)
            second = jnp.tanh(sqrt_c * lam_x * v_norm / 2.0) * v / (sqrt_c * v_norm)
            return _mobius_add(x, second, c)
        key = jax.random.key(seed)
        k1, k2, k3 = jax.random.split(key, 3)
        N, C_IN, C_OUT = (1536, 64, 64)
        x = jax.random.normal(k1, (N, C_IN), dtype=jnp.float32) * 0.03
        adj = (jax.random.uniform(k2, (N, N)) < 0.02).astype(jnp.float32)
        bound = 1.0 / np.sqrt(C_IN)
        weight = jax.random.uniform(k3, (C_IN, C_OUT), dtype=jnp.float32, minval=-bound, maxval=bound)
        bias = jnp.zeros((C_OUT,), dtype=jnp.float32)
        return {'x': x, 'adj': adj, 'weight': weight, 'bias': bias}
    _L3_gnn_all = _L3_gnn_setup()
    _L3_gnn_in = {k: v for k, v in _L3_gnn_all.items() if k in ('weight', 'bias', )}
    del _L3_gnn_all

    return {
        "x": x,
        "adj": adj,
        "L0_gnn_weight": _L0_gnn_in["weight"],
        "L1_gnn_W_gat": _L1_gnn_in["W_gat"],
        "L1_gnn_a_gat": _L1_gnn_in["a_gat"],
        "L1_gnn_w_ih_e": _L1_gnn_in["w_ih_e"],
        "L1_gnn_w_hh_e": _L1_gnn_in["w_hh_e"],
        "L1_gnn_b_ih_e": _L1_gnn_in["b_ih_e"],
        "L1_gnn_b_hh_e": _L1_gnn_in["b_hh_e"],
        "L1_gnn_w_ih_n": _L1_gnn_in["w_ih_n"],
        "L1_gnn_w_hh_n": _L1_gnn_in["w_hh_n"],
        "L1_gnn_b_ih_n": _L1_gnn_in["b_ih_n"],
        "L1_gnn_b_hh_n": _L1_gnn_in["b_hh_n"],
        "L2_gnn_weight": _L2_gnn_in["weight"],
        "L2_gnn_bias": _L2_gnn_in["bias"],
        "L3_gnn_weight": _L3_gnn_in["weight"],
        "L3_gnn_bias": _L3_gnn_in["bias"],
    }

def reference(x, adj, L0_gnn_weight, L1_gnn_W_gat, L1_gnn_a_gat, L1_gnn_w_ih_e, L1_gnn_w_hh_e, L1_gnn_b_ih_e, L1_gnn_b_hh_e, L1_gnn_w_ih_n, L1_gnn_w_hh_n, L1_gnn_b_ih_n, L1_gnn_b_hh_n, L2_gnn_weight, L2_gnn_bias, L3_gnn_weight, L3_gnn_bias):
    import jax
    import jax.numpy as jnp
    def _L0_gnn_ref(x, L, weight):
        import jax, jax.numpy as jnp
        import numpy as np
        N = 8192
        F_IN = 64
        F_OUT = 64
        K = 4
        terms = [x, L @ x]
        for _ in range(2, K):
            terms.append(2.0 * (L @ terms[-1]) - terms[-2])
        feature = jnp.stack(terms, axis=0)
        return jnp.einsum('kni,kio->no', feature, weight)

    def _L1_gnn_ref(h, node_adj, edge_adj, W_gat, a_gat, w_ih_e, w_hh_e, b_ih_e, b_hh_e, w_ih_n, w_hh_n, b_ih_n, b_hh_n):
        import jax, jax.numpy as jnp
        import numpy as np
        N = 8192
        H = 64
        ALPHA = 0.2
        NEG_INF = -9000000000000000.0

        def gru_cell(x, h, w_ih, w_hh, b_ih, b_hh):
            gi = x @ w_ih.T + b_ih
            gh = h @ w_hh.T + b_hh
            ir, iz, inn = jnp.split(gi, 3, axis=1)
            hr, hz, hn = jnp.split(gh, 3, axis=1)
            r = jax.nn.sigmoid(ir + hr)
            z = jax.nn.sigmoid(iz + hz)
            n = jnp.tanh(inn + r * hn)
            return (1.0 - z) * n + z * h

        def gat(h, node_adj, edge_adj, W, a):
            hw = h @ W
            h_plus = (node_adj > 0).astype(hw.dtype) @ hw
            h_minus = (node_adj < 0).astype(hw.dtype) @ hw
            e_plus = jax.nn.leaky_relu(jnp.concatenate([h_plus, h_minus], axis=1) @ a, ALPHA)
            e_minus = jax.nn.leaky_relu(jnp.concatenate([h_minus, h_plus], axis=1) @ a, ALPHA)
            att = jnp.where(edge_adj > 0, e_plus, NEG_INF)
            att = jnp.where(edge_adj < 0, e_minus, att)
            att = jax.nn.softmax(att, axis=1)
            return att * edge_adj @ hw
        d_node = jnp.diag(node_adj)
        d_edge = jnp.diag(edge_adj)
        A_node = node_adj - jnp.diag(d_node)
        A_edge = edge_adj - jnp.diag(d_edge)
        node_support = jnp.concatenate([(A_node > 0).astype(h.dtype) @ h, (A_node < 0).astype(h.dtype) @ h], axis=1)
        edge_output = gru_cell(node_support, h, w_ih_e, w_hh_e, b_ih_e, b_hh_e)
        edge_support = gat(h, A_node, A_edge, W_gat, a_gat)
        node_output = gru_cell(edge_support, h, w_ih_n, w_hh_n, b_ih_n, b_hh_n)
        return d_edge[:, None] * edge_output + d_node[:, None] * node_output

    def _L2_gnn_ref(input, adj, weight, bias):
        import jax, jax.numpy as jnp
        import numpy as np
        N, D_IN, D_OUT = (8192, 64, 64)
        MAX_NEIGH = 100
        DECAY = 0.5
        support = input @ weight
        mask = (adj != 0).astype(support.dtype)
        rank = jnp.cumsum(mask, axis=1)
        deg = rank[:, -1:]
        k = jnp.minimum(deg, float(MAX_NEIGH))
        pos = rank - (deg - k)
        w = mask * jnp.where(pos > 0, DECAY ** (k - pos), 0.0)
        out = w @ support + bias
        return out

    def _L3_gnn_ref(x, adj, weight, bias):
        import jax, jax.numpy as jnp
        import numpy as np
        CURV = 1.0
        MIN_NORM = 1e-15
        TANH_CLIP = 1.0 - 1e-05

        def _mobius_add(x, y, c):
            x2 = jnp.sum(x * x, axis=-1, keepdims=True)
            y2 = jnp.sum(y * y, axis=-1, keepdims=True)
            xy = jnp.sum(x * y, axis=-1, keepdims=True)
            num = (1.0 + 2.0 * c * xy + c * y2) * x + (1.0 - c * x2) * y
            den = 1.0 + 2.0 * c * xy + c ** 2 * x2 * y2
            return num / jnp.maximum(den, MIN_NORM)

        def _logmap(x, y, c):
            sub = _mobius_add(-x, y, c)
            sub_norm = jnp.maximum(jnp.linalg.norm(sub, axis=-1, keepdims=True), MIN_NORM)
            x2 = jnp.sum(x * x, axis=-1, keepdims=True)
            lam_x = 2.0 / jnp.maximum(1.0 - c * x2, MIN_NORM)
            sqrt_c = jnp.sqrt(c)
            arg = jnp.clip(sqrt_c * sub_norm, 0.0, TANH_CLIP)
            return 2.0 / (sqrt_c * lam_x) * jnp.arctanh(arg) * sub / sub_norm

        def _expmap(x, v, c):
            v_norm = jnp.maximum(jnp.linalg.norm(v, axis=-1, keepdims=True), MIN_NORM)
            x2 = jnp.sum(x * x, axis=-1, keepdims=True)
            lam_x = 2.0 / jnp.maximum(1.0 - c * x2, MIN_NORM)
            sqrt_c = jnp.sqrt(c)
            second = jnp.tanh(sqrt_c * lam_x * v_norm / 2.0) * v / (sqrt_c * v_norm)
            return _mobius_add(x, second, c)
        c = CURV
        deg = jnp.maximum(adj.sum(axis=1, keepdims=True), 1e-08)
        w = adj / deg
        log_ij = _logmap(x[:, None, :], x[None, :, :], c)
        agg = jnp.einsum('ij,ijc->ic', w, log_ij)
        transformed = agg @ weight + bias
        origin = jnp.zeros_like(transformed)
        return _expmap(origin, transformed, c)

    x = _layernorm(x + _L0_gnn_ref(x, adj, L0_gnn_weight), axis=-1)
    x = _layernorm(x + _L1_gnn_ref(x, adj, adj, L1_gnn_W_gat, L1_gnn_a_gat, L1_gnn_w_ih_e, L1_gnn_w_hh_e, L1_gnn_b_ih_e, L1_gnn_b_hh_e, L1_gnn_w_ih_n, L1_gnn_w_hh_n, L1_gnn_b_ih_n, L1_gnn_b_hh_n), axis=-1)
    x = _layernorm(x + _L2_gnn_ref(x, adj, L2_gnn_weight, L2_gnn_bias), axis=-1)
    x = _layernorm(x + _L3_gnn_ref(x, adj, L3_gnn_weight, L3_gnn_bias), axis=-1)
    return x


_drawn_inputs = setup_inputs


def setup_inputs(seed=0):
    import zlib

    import numpy as np

    out = dict(_drawn_inputs(seed))
    spreads = {'L1_gnn_b_ih_e': (0.0, 2.0),
     'L1_gnn_b_hh_e': (0.0, 2.0),
     'L1_gnn_b_ih_n': (0.0, 2.0),
     'L1_gnn_b_hh_n': (0.0, 2.0),
     'L3_gnn_bias': (0.0, 0.1)}
    factors = {'L1_gnn_W_gat': 37.8,
     'L1_gnn_w_hh_e': 64.0,
     'L1_gnn_w_ih_n': 35.82,
     'L1_gnn_w_hh_n': 200.0}
    for name, (base, spread) in spreads.items():
        noise = np.random.default_rng([zlib.crc32(name.encode()), seed]).standard_normal(out[name].shape)
        drawn = base * np.exp(spread * noise) if base else spread * noise
        out[name] = jnp.asarray(drawn.astype(out[name].dtype))
    for name, factor in factors.items():
        out[name] = (out[name] * factor).astype(out[name].dtype)
    return out
```

```python
from contextlib import ExitStack

import numpy as np

import concourse.bass as bass
from concourse import mybir

ALU = mybir.AluOpType
ACT = mybir.ActivationFunctionType
AX_X = mybir.AxisListType.X
F32 = mybir.dt.float32
BF16 = mybir.dt.bfloat16
I16 = mybir.dt.int16
U8 = mybir.dt.uint8

P = 128
N = 4096
F = 64
NB = N // P
QC = 1024
NQ = N // QC
GB = 4
NS = NB // GB
HALF = 512
CB = QC // P
RING = 4
SLOTS = NQ * NS
EPS = 1e-5
LEAK = 0.2
NEG_INF = 9.0e15
MAX_NEIGH = 100
CODE_BIAS = 8192.0
CODE_SCALE = 2.0 ** 27
TINY_Q = 2.0 ** -63
MIN_NORM = 1e-15
TANH_CLIP = 1.0 - 1e-5
LOG_CLIP = 2.0 * float(np.log(TANH_CLIP))


def adjacency_stack(nc, adjT, x, xT, cheb_w, gatWT, gat_a2, wieT, wheT, bie, bhe, winT, whnT, bin_, bhn,
                    w2, b2, w3, b3, out, upto=9):
    adj_slots = adjT.rearrange("(g k p) (q c) -> p g k q c", k=GB, p=P, c=QC)
    codes_dram = nc.dram_tensor("codes", [SLOTS, P, GB * QC], U8, kind="Internal").ap()

    ctx = ExitStack()
    with ctx:
        def sb(name, shape, dt=F32):
            return ctx.enter_context(nc.sbuf_tensor(name, shape, dt))

        def sem(name):
            return ctx.enter_context(nc.semaphore(name))

        ps = ctx.enter_context(nc.psum_tensor("ps", [P, 8, HALF], F32))

        ring = sb("ring", [P, RING, GB, QC])
        X = sb("X", [P, NB, F])
        Y = sb("Y", [P, NB, F])
        stage_f = sb("stage_f", [P, 2, GB, F + 1])
        stage_b = sb("stage_b", [P, 2, GB, 3 * F], BF16)
        turn_in = sb("turn_in", [P, QC])
        diag = sb("diag", [P, NB])
        degrees = sb("degrees", [P, NB, 2])
        edge_sum = sb("edge_sum", [P, NB])
        stats = sb("stats", [P, 10, NB])
        work = sb("work", [P, 24 * 1024])

        ident = sb("ident", [P, P])
        offdiag = sb("offdiag", [P, P])
        offdiag_b = sb("offdiag_b", [P, P], BF16)
        later_or_self = sb("later_or_self", [P, P], BF16)
        minus_ones = sb("minus_ones", [P, P], BF16)
        ones = sb("ones", [P, 32], BF16)
        ones_f = sb("ones_f", [P, 1])
        code_bias = sb("code_bias", [P, 1])
        cheb_sb = sb("cheb_sb", [P, 4, F])
        turn_w = sb("turn_w", [P, 3, 2 * F])
        w_first = sb("w_first", [F, F])
        w_edge = sb("w_edge", [P, 3 * F])
        w_score = sb("w_score", [P, 2])
        w_hid = sb("w_hid", [F + 1, 2, 4 * F])
        w_att = sb("w_att", [P, 6 * F])
        gatWT_sb = sb("gatWT_sb", [F, 2 * F])
        gat_a_sb = sb("gat_a_sb", [F, 2])
        winT_sb = sb("winT_sb", [F, 3 * F])
        bias_tmp = sb("bias_tmp", [F + 1, 4, 3 * F])
        w2_sb = sb("w2_sb", [F, F])
        w3_sb = sb("w3_sb", [F + 1, F])
        b2_sb = sb("b2_sb", [P, F])
        b3_sb = sb("b3_sb", [P, F])
        fold = sb("fold", [P, F])
        minus_two = sb("minus_two", [P, 1])

        at = [0]

        def carve(words, reset=None):
            if reset is not None:
                at[0] = reset
            a = at[0]
            at[0] += words
            assert at[0] <= 24 * 1024, at[0]
            return work[:, a:a + words]

        T1 = carve(NB * F, 0).rearrange("p (b f) -> p b f", f=F)
        T2 = carve(NB * F).rearrange("p (b f) -> p b f", f=F)
        mask = carve(2 * GB * QC // 2).bitcast(BF16).rearrange("p (t k c) -> p t k c", t=2, k=GB)
        later = carve(2 * GB * QC // 2).bitcast(BF16).rearrange("p (t k c) -> p t k c", t=2, k=GB)
        codes = carve(2 * GB * QC // 4).bitcast(U8).rearrange("p (t k c) -> p t k c", t=2, k=GB)
        xT_sb = carve(N)[0:F, :]
        count_in = codes.rearrange("p t k c -> p (t k c)")[0:F, 0:4 * QC].bitcast(F32)

        row_sum = mask[:, 0].rearrange("p k c -> p (k c)")[:, 0:2 * QC].bitcast(F32)

        more = carve(2 * 2 * QC // 2, 0).bitcast(BF16).rearrange("p (t k c) -> p t k c", t=2, k=2)
        less = carve(2 * 2 * QC // 2).bitcast(BF16).rearrange("p (t k c) -> p t k c", t=2, k=2)
        negs = carve(2 * 2 * QC).rearrange("p (t k c) -> p t k c", t=2, k=2)
        hid = carve(CB * 8 * F).rearrange("p (c g n) -> p c g n", c=CB, g=2)
        att = carve(CB * (6 * F + 2)).rearrange("p (c n) -> p c n", c=CB)
        parts = carve(NB * 3 * F // 2).bitcast(BF16).rearrange("p (b n) -> p b n", n=3 * F)
        weighted_in = carve(QC)
        hT = carve(QC)[0:F + 1, :]
        x_q = carve(CB * F).rearrange("p (c f) -> p c f", f=F)
        own = carve(GB * P).rearrange("p (k c) -> p k c", k=GB)
        gate = carve(CB * 2 * F).rearrange("p (c g f) -> p c g f", c=CB, g=2)
        small = carve(16 * 2 * CB).rearrange("p (i c n) -> p i c n", i=16, c=CB)

        code_in = carve(4 * QC, 0).bitcast(U8).rearrange("p (r k c) -> p r k c", r=4, k=GB)
        decay = carve(4 * QC).bitcast(I16).rearrange("p (t k c) -> p t k c", t=2, k=GB)
        support = carve(NB * F).rearrange("p (b f) -> p b f", f=F)
        assert at[0] <= 2048 * 2 + 4096 + CB * 8 * F + CB * (6 * F + 2)
        h2T = carve(2 * QC, at[0] + 4096)[0:F, :].rearrange("p (t c) -> p t c", t=2)

        UT = carve(N, 0)[0:F + 2, :]
        VT = carve(N)[0:F + 2, :]
        x_ext = carve(NB * (F + 1)).rearrange("p (b f) -> p b f", f=F + 1)
        stat_q = carve(2 * GB * P)[0:F + 2, :].rearrange("p (t c) -> p t c", t=2)
        stat_d = carve(2 * GB * P)[0:F + 2, :].rearrange("p (t c) -> p t c", t=2)
        dist = carve(3 * 2 * QC).rearrange("p (u a c) -> p u a c", u=3, a=2)
        logs = carve(2 * 2 * QC).rearrange("p (u a c) -> p u a c", u=2, a=2)
        U = carve(NB * (F + 2), at[0] - 5 * 2 * QC).rearrange("p (b f) -> p b f", f=F + 2)
        V_ = carve(NB * (F + 2)).rearrange("p (b f) -> p b f", f=F + 2)
        aggT = carve(2 * QC, at[0])[0:F, :].rearrange("p (t c) -> p t c", t=2)

        split_rest = [Y[:], support]

        def own_blocks(slot, s):
            first = slot[:, 0, s * GB * P:(s * GB + 1) * P]
            return bass.AP(first.tensor, first.offset, [first.ap[0], (QC + P, GB), (1, P)])

        block = ctx.enter_context(nc.Block())

        loaded = [sem(f"loaded{r}") for r in range(RING)]
        ring_used = sem("ring_used")
        load_turns = sem("load_turns")
        stage_turns = sem("stage_turns")
        turn_turns = sem("turn_turns")
        consts_in = sem("consts_in")
        x_in = sem("x_in")
        pool_steps = sem("pool_steps")
        consts_made = sem("consts_made")
        weights_made = sem("weights_made")
        first_ready = sem("first_ready")
        first_read = sem("first_read")
        staged = [sem(f"staged{p}") for p in range(3)]
        signs_ready = [sem(f"signs_ready{p}") for p in range(2)]
        dve_signs = [sem(f"dve_signs{p}") for p in range(2)]
        rank_ready = sem("rank_ready")
        codes_made = sem("codes_made")
        codes_stored = [sem(f"codes_stored{t}") for t in range(2)]
        product_ready = [sem(f"product_ready{p}") for p in range(3)]
        product_copied = [sem(f"product_copied{p}") for p in range(3)]
        turned = [sem(f"turned{p}") for p in range(3)]
        turn_read = [sem(f"turn_read{p}") for p in range(3)]
        counts_ready = sem("counts_ready")
        counts_copied = sem("counts_copied")
        counts_turned = sem("counts_turned")
        counts_read = sem("counts_read")
        turn_steps = [sem(f"turn_steps{p}") for p in range(3)]
        norm_steps = [sem(f"norm_steps{l}") for l in range(4)]
        norm_root = [sem(f"norm_root{l}") for l in range(4)]
        normed = [sem(f"normed{l}") for l in range(4)]
        out_stored = sem("out_stored")
        row_steps = sem("row_steps")
        row_ready = sem("row_ready")
        rows_turned = sem("rows_turned")
        rows_read = sem("rows_read")
        gat_ready = sem("gat_ready")
        parts_steps = [sem(f"parts_steps{l}") for l in (1, 2)]
        parts_act = [sem(f"parts_act{l}") for l in (1, 2)]
        parts_ready = [sem(f"parts_ready{l}") for l in (1, 2)]
        staged_parts = [sem(f"staged_parts{l}") for l in (1, 2)]
        diag_cut = sem("diag_cut")
        diag_steps = sem("diag_steps")
        negs_made = sem("negs_made")
        signs_made = sem("signs_made")
        rect_ready = sem("rect_ready")
        pair_used = sem("pair_used")
        sums_copied = sem("sums_copied")
        x_q_ready = sem("x_q_ready")
        hT_ready = sem("hT_ready")
        hT_copied = sem("hT_copied")
        hid_ready = sem("hid_ready")
        att_ready = sem("att_ready")
        hid_read = sem("hid_read")
        att_read = sem("att_read")
        gate_steps = sem("gate_steps")
        gate_act = sem("gate_act")
        layer1_sum = sem("layer1_sum")
        code_loaded = [sem(f"code_loaded{r}") for r in range(4)]
        decay_used = sem("decay_used")
        decay_dve = sem("decay_dve")
        decay_act = sem("decay_act")
        h2T_ready = sem("h2T_ready")
        h2T_copied = sem("h2T_copied")
        support_ready = sem("support_ready")
        support_read = sem("support_read")
        sum2_copied = sem("sum2_copied")
        sum2_turned = sem("sum2_turned")
        sum2_read = sem("sum2_read")
        ext_steps = sem("ext_steps")
        ext_ready = sem("ext_ready")
        uv_ready = sem("uv_ready")
        uv_copied = sem("uv_copied")
        staged_ext = sem("staged_ext")
        staged_qd = sem("staged_qd")
        dist_ready = sem("dist_ready")
        clamped = sem("clamped")
        logs_made = sem("logs_made")
        log_pairs = sem("log_pairs")
        clipped = sem("clipped")
        atanh_steps = sem("atanh_steps")
        atanh_ready = sem("atanh_ready")
        final_steps = sem("final_steps")
        weighted = sem("weighted")
        gathered = sem("gathered")
        agg_copied = sem("agg_copied")
        agg_turned = sem("agg_turned")
        agg_read = sem("agg_read")
        tail_steps = sem("tail_steps")
        tail_act = sem("tail_act")
        aggT_ready = sem("aggT_ready")
        aggT_copied = sem("aggT_copied")
        moved_ready = sem("moved_ready")

        N_PUTS = 19
        G_SCORES = 10
        G_SUMS = 22
        G_NEW = 25
        GATE_STEPS = 30
        TAIL_NORM = NQ + 2
        TAIL_AGG = 12

        def source_group(p, q, s):
            if p == 0:
                return NS - 1 - s
            if p in (1, 3):
                return (q * 2 + s) % NS
            return s

        def block_order(p):
            return (3, 2, 1, 0) if p == 0 else (0, 1, 2, 3)

        @block.sync
        def _(sp):
            def load(p, q, s):
                r = s % RING
                g = source_group(p, q, s)
                src = adj_slots[:, bass.ds(g, 1), :, bass.ds(q, 1), :].rearrange("p a k b c -> p (a k) (b c)")
                sp.dma_start(ring[:, r], src).then_inc(loaded[r], 16)

            def wait_then_load(p, q, s, used, value):
                sp.wait_ge(used, value)
                if not isinstance(q, int):
                    sp.sem_inc(load_turns, 1)
                load(p, q, s)

            for s in range(RING):
                load(0, 0, s)
            for s in range(RING, NS):
                wait_then_load(0, 0, s, ring_used, s - RING + 1)
            with sp.Fori(1, NQ) as q:
                for s in range(NS):
                    wait_then_load(0, q, s, ring_used, q * NS + (s - RING + 1))
            for p in (1, 2):
                with sp.Fori(0, NQ) as q:
                    for s in range(NS):
                        wait_then_load(p, q, s, ring_used, q * NS + (p * SLOTS + s - RING + 1))
            if upto < 1:
                return
            for s in range(NS):
                if s < RING:
                    wait_then_load(3, 0, s, ring_used, 3 * SLOTS + s - RING + 1)
                else:
                    wait_then_load(3, 0, s, pair_used, 2 + 2 * (s - RING + 1))
            with sp.Fori(1, NQ) as q:
                for s in range(NS):
                    wait_then_load(3, q, s, pair_used, q * (2 * NS) + (2 + 2 * (s - RING + 1)))
            if upto < 2:
                return
            for t in range(2):
                sp.wait_ge(codes_stored[t], NQ * NS // 2 * 16)
            sp.wait_ge(normed[1], 1)

            def load_codes(q, s):
                r = s % RING
                src = codes_dram[bass.ds(q * NS + s, 1)].rearrange("a p n -> p (a n)")
                sp.dma_start(code_in[:, r].rearrange("p k c -> p (k c)"), src).then_inc(code_loaded[r], 16)

            for s in range(NS):
                if s >= RING:
                    sp.wait_ge(decay_dve, s - RING + 1)
                    sp.wait_ge(decay_act, s - RING + 1)
                load_codes(0, s)
            with sp.Fori(1, NQ) as q:
                for s in range(NS):
                    sp.wait_ge(decay_dve, q * NS + (s - RING + 1))
                    sp.wait_ge(decay_act, q * NS + (s - RING + 1))
                    sp.sem_inc(load_turns, 1)
                    load_codes(q, s)
            if upto < 3:
                return
            for s in range(NS):
                if s < RING:
                    wait_then_load(4, 0, s, pair_used, 2 + 2 * (SLOTS + s - RING + 1))
                else:
                    wait_then_load(4, 0, s, gathered, GB * (s - RING + 1))
            with sp.Fori(1, NQ) as q:
                for s in range(NS):
                    wait_then_load(4, q, s, gathered, q * (GB * NS) + GB * (s - RING + 1))

        @block.gpsimd
        def _(pool):
            steps = [0]

            def step(ins):
                steps[0] += 1
                ins.then_inc(pool_steps, 1)
                pool.wait_ge(pool_steps, steps[0])

            def diagonal(ap, base, fill, width):
                step(nc.gpsimd.affine_select(out=ap, in_=ap, compare_op=ALU.not_equal, fill=fill, base=base,
                                             pattern=[[-1, width]], channel_multiplier=1))

            step(nc.gpsimd.memset(ident[:], 0.0))
            diagonal(ident[:], 0, 1.0, P)
            step(nc.gpsimd.memset(offdiag[:], 1.0))
            diagonal(offdiag[:], 0, 0.0, P)
            step(nc.gpsimd.memset(offdiag_b[:], 1.0))
            diagonal(offdiag_b[:], 0, 0.0, P)
            step(nc.gpsimd.memset(fold[:], 0.0))
            diagonal(fold[:], 0, 1.0, F)
            diagonal(fold[:], -F, 1.0, F)
            step(nc.gpsimd.memset(minus_ones[:], -1.0))
            step(nc.gpsimd.memset(ones[:], 1.0))
            step(nc.gpsimd.memset(ones_f[:], 1.0))
            step(nc.gpsimd.memset(code_bias[:], MAX_NEIGH - CODE_BIAS))
            step(nc.gpsimd.memset(later_or_self[:], -1.0))
            step(nc.gpsimd.affine_select(out=later_or_self[:], in_=later_or_self[:], compare_op=ALU.is_gt, fill=0.0,
                                         base=0, pattern=[[-1, P]], channel_multiplier=1))
            diagonal(later_or_self[:], 0, CODE_BIAS, P)
            step(nc.gpsimd.memset(minus_two[0:F], -2.0))
            step(nc.gpsimd.memset(minus_two[F:P], 1.0))
            pool.sem_inc(consts_made, 1)

            def stage(p, src, done):
                with pool.Fori(0, NQ) as q:
                    for s in range(NS):
                        g = source_group(p, q, s)
                        if p == 0 and s < 2:
                            pool.wait_ge(ring_used, q * NS)
                        else:
                            pool.wait_ge(ring_used, p * SLOTS + q * NS + s - 1)
                        pool.sem_inc(stage_turns, 1)
                        nc.gpsimd.tensor_copy(stage_f[:, s % 2, :, 0:F],
                                              src[:, bass.ds(g * GB, GB), :]).then_inc(done, 1)

            pool.wait_ge(x_in, 32)
            stage(0, X, staged[0])
            pool.wait_ge(turn_read[0], NQ)
            stage(1, T1, staged[1])
            pool.wait_ge(turn_read[1], NQ)
            stage(2, T2, staged[2])
            if upto < 1:
                return

            pool.wait_ge(parts_ready[0], 1)
            with pool.Fori(0, NQ) as q:
                for s in range(NS):
                    g = source_group(3, q, s)
                    pool.wait_ge(pair_used, q * (2 * NS) + 2 * s)
                    pool.sem_inc(stage_turns, 1)
                    nc.gpsimd.tensor_copy(stage_f[:, s % 2, :, 0:F],
                                          X[:, bass.ds(g * GB, GB), :]).then_inc(staged_parts[0], 1)
                    nc.gpsimd.tensor_copy(stage_b[:, s % 2], parts[:, bass.ds(g * GB, GB), :]).then_inc(
                        staged_parts[0], 1)
                pool.wait_ge(layer1_sum, q)
                pool.sem_inc(stage_turns, 1)
                nc.gpsimd.tensor_copy(x_q, X[:, bass.ds(q * CB, CB), :]).then_inc(x_q_ready, 1)
            if upto < 2:
                return

            pool.wait_ge(parts_ready[1], 1)
            with pool.Fori(0, NQ) as q:
                for s in range(NS):
                    pool.wait_ge(decay_used, q * NS + s)
                    pool.sem_inc(stage_turns, 1)
                    nc.gpsimd.tensor_copy(stage_b[:, s % 2], parts[:, s * GB:(s + 1) * GB, :]).then_inc(
                        staged_parts[1], 1)
            if upto < 3:
                return

            pool.wait_ge(ext_ready, 1)
            with pool.Fori(0, NQ) as q:
                for u in range(GB * NS):
                    n = q * (GB * NS) + u
                    if u == 0 or u % GB == GB - 1 and u < GB * (NS - 1):
                        s = 0 if u == 0 else u // GB + 1
                        pool.wait_ge(gathered, q * (GB * NS) + max(s - 1, 0) * GB)
                        pool.sem_inc(stage_turns, 1)
                        nc.gpsimd.tensor_copy(stage_f[:, s % 2], x_ext[:, s * GB:(s + 1) * GB, :]).then_inc(
                            staged_ext, 1)
                    pool.wait_ge(logs_made, n + 1)
                    pool.wait_ge(weighted, n + 1)
                    a, b = logs[:, u % 2, 0, :], logs[:, u % 2, 1, :]
                    lq, ld = dist[:, u % 3, 0, :], dist[:, u % 3, 1, :]
                    nc.gpsimd.tensor_tensor(a, lq, ld, ALU.subtract).then_inc(log_pairs, 1)
                    nc.gpsimd.tensor_tensor(b, lq, ld, ALU.add).then_inc(log_pairs, 1)

        @block.tensor
        def _(pe):
            pe.wait_ge(weights_made, 1)
            pe.wait_ge(x_in, 32)
            for n in range(4):
                for c in range(8):
                    b = n * 8 + c
                    mm = nc.tensor.matmul(ps[:, n, c * F:(c + 1) * F], xT_sb[:, b * P:(b + 1) * P], w_first[:],
                                          start=True, stop=True)
                mm.then_inc(first_ready, 1)
            nc.tensor.matmul(ps[:, 4, 0:2], gatWT_sb[:], gat_a_sb[:], start=True, stop=True)
            nc.tensor.matmul(ps[:, 5, 0:3 * F], gatWT_sb[:], winT_sb[:], start=True, stop=True).then_inc(gat_ready, 1)
            pe.wait_ge(first_read, 5)

            for p in range(3):
                with pe.Fori(0, NQ) as q:
                    for s in range(NS):
                        r, t = s % RING, s % 2
                        pe.wait_ge(loaded[r], (q * 2 + (p * 8 + s // RING + 1)) * 16)
                        pe.wait_ge(staged[p], q * NS + s + 1)
                        order = block_order(p)
                        if p == 0:
                            for j, k in enumerate(order):
                                pe.wait_ge(signs_ready[0], q * (GB * NS) + (s * GB + j + 1))
                                for h in range(2):
                                    cols = slice(h * HALF, (h + 1) * HALF)
                                    pe.wait_ge(codes_made, q * (2 * GB * NS) + ((s * GB + j) * 2 + h))
                                    nc.tensor.matmul(ps[:, 6 + h, :], later_or_self[:], mask[:, t, k, cols],
                                                     start=True, stop=False)
                                    nc.tensor.matmul(ps[:, 6 + h, :], minus_ones[:], later[:, t, j, cols],
                                                     start=False, stop=True).then_inc(rank_ready, 1)
                        if p == 1:
                            pe.wait_ge(signs_ready[1], q * NS + s + 1)
                            if s == 0:
                                pe.wait_ge(counts_read, q)
                            for k in range(GB):
                                for h in range(2):
                                    cols = slice(h * HALF, (h + 1) * HALF)
                                    st, sp_ = s == 0 and k == 0, s == NS - 1 and k == GB - 1
                                    nc.tensor.matmul(ps[0:32, 6 + h, :], ones[:], mask[:, t, k, cols],
                                                     start=st, stop=sp_)
                                    nc.tensor.matmul(ps[32:64, 6 + h, :], ones[:], later[:, t, k, cols],
                                                     start=st, stop=sp_)
                        for pair in range(2):
                            if p == 2 and pair == 1:
                                pe.wait_ge(row_steps, q * (GB * NS) + GB * (s + 1))
                            ka, kb = order[2 * pair:2 * pair + 2]
                            first, last = s == 0 and pair == 0, s == NS - 1 and pair == 1
                            for h in range(2):
                                cols = slice(h * HALF, (h + 1) * HALF)
                                nc.tensor.matmul(ps[0:F, h, :], stage_f[:, t, ka, 0:F], ring[:, r, ka, cols],
                                                 start=first, stop=last)
                                mm = nc.tensor.matmul(ps[F:2 * F, h, :], stage_f[:, t, kb, 0:F], ring[:, r, kb, cols],
                                                      start=first, stop=last)
                        mm.then_inc(ring_used, 1)
                    pe.wait_ge(product_copied[p], (q + 1) * 2)
                    pe.wait_ge(turn_read[p], q)
                    if p:
                        pe.wait_ge(turn_read[p - 1], NQ)
                    for c in range(CB):
                        mm = nc.tensor.matmul(ps[:, 4 + c // 4, (c % 4) * P:(c % 4 + 1) * P],
                                              turn_in[:, c * P:(c + 1) * P], turn_w[:, p, :], start=True, stop=True)
                    mm.then_inc(turned[p], 1)
                    if p == 1:
                        pe.wait_ge(counts_copied, q + 1)
                        for c in range(CB):
                            mm = nc.tensor.matmul(ps[:, 6, 2 * c:2 * c + 2], count_in[:, c * P:(c + 1) * P],
                                                  ident[0:F, 0:F:32], start=True, stop=True)
                        mm.then_inc(counts_turned, 1)
                    if p == 2:
                        pe.wait_ge(row_ready, q + 1)
                        pe.wait_ge(rows_read, q)
                        for c in range(CB):
                            mm = nc.tensor.matmul(ps[:, 6, c:c + 1], row_sum[:, c * P:(c + 1) * P], ones_f[:],
                                                  start=True, stop=True)
                        mm.then_inc(rows_turned, 1)
            if upto < 1:
                return

            pe.sem_inc(pair_used, 2)
            pe.wait_ge(turn_read[2], NQ)
            pe.wait_ge(rows_read, NQ)
            with pe.Fori(0, NQ) as q:
                for s in range(NS):
                    r, t = s % RING, s % 2
                    pe.wait_ge(staged_parts[0], q * (2 * NS) + 2 * (s + 1))
                    for pair in range(2):
                        pe.wait_ge(rect_ready, q * (2 * NS) + (2 * s + pair + 1))
                        for i in range(2):
                            k = 2 * pair + i
                            first = s == 0 and k == 0
                            last = s == NS - 1 and k == GB - 1
                            for h in range(2):
                                cols = slice(h * HALF, (h + 1) * HALF)
                                nc.tensor.matmul(ps[0:F, h, :], stage_f[:, t, k, 0:F], ring[:, r, k, cols],
                                                 start=first, stop=last)
                                nc.tensor.matmul(ps[F:P, h, :], stage_f[:, t, k, 0:F], negs[:, pair, i, cols],
                                                 start=first, stop=last)
                                for m in range(3):
                                    part = stage_b[:, t, k, m * F:(m + 1) * F]
                                    nc.tensor.matmul(ps[0:F, 2 + h, :], part, more[:, pair, i, cols],
                                                     start=first and m == 0, stop=last and m == 2)
                                    mm = nc.tensor.matmul(ps[F:P, 2 + h, :], part, less[:, pair, i, cols],
                                                          start=first and m == 0, stop=last and m == 2)
                        mm.then_inc(pair_used, 1)
                pe.wait_ge(x_q_ready, q + 1)
                pe.wait_ge(hid_read, q * CB)
                pe.wait_ge(att_read, q * CB)
                pe.sem_inc(turn_turns, 1)
                for c in range(CB):
                    mm = nc.tensor.transpose(ps[0:F, 4 + c // 4, (c % 4) * P:(c % 4 + 1) * P], x_q[:, c, :], ident[:])
                mm.then_inc(hT_ready, 1)
                pe.wait_ge(hT_copied, q + 1)
                pe.wait_ge(sums_copied, q * 4 + 4)
                for c in range(CB):
                    a, b = 4 + 2 * (c % 2), 5 + 2 * (c % 2)
                    cols = slice(c * P, (c + 1) * P)
                    if c >= 2:
                        pe.wait_ge(hid_read, q * CB + (c - 1))
                        pe.wait_ge(att_read, q * CB + (c - 1))
                    nc.tensor.matmul(ps[:, a, :], hT[:, cols], w_hid[:].rearrange("p g n -> p (g n)"),
                                     start=True, stop=False)
                    nc.tensor.matmul(ps[:, a, 0:3 * F], turn_in[:, cols], w_edge[:], start=False, stop=True).then_inc(
                        hid_ready, 1)
                    nc.tensor.matmul(ps[:, b, 0:6 * F], weighted_in[:, cols], w_att[:], start=True, stop=True)
                    nc.tensor.matmul(ps[:, b, 6 * F:6 * F + 2], turn_in[:, cols], w_score[:],
                                     start=True, stop=True).then_inc(att_ready, 1)
            if upto < 2:
                return

            pe.wait_ge(normed[1], 1)
            pe.wait_ge(hid_read, NB)
            pe.wait_ge(att_read, NB)
            for n in range(NQ):
                if n >= 2:
                    pe.wait_ge(h2T_copied, n - 1)
                for c in range(CB):
                    bank = 2 * (n % 2) + c // 4
                    mm = nc.tensor.transpose(ps[0:F, bank, (c % 4) * P:(c % 4 + 1) * P], X[:, n * CB + c, :], ident[:])
                mm.then_inc(h2T_ready, 1)
                pe.wait_ge(h2T_copied, n + 1)
                for c in range(CB):
                    mm = nc.tensor.matmul(ps[:, 4 + n, c * F:(c + 1) * F], h2T[:, n % 2, c * P:(c + 1) * P], w2_sb[:],
                                          start=True, stop=True)
                mm.then_inc(support_ready, 1)
            pe.wait_ge(support_read, NQ)
            with pe.Fori(0, NQ) as q:
                for s in range(NS):
                    t = s % 2
                    pe.wait_ge(staged_parts[1], q * NS + s + 1)
                    pe.wait_ge(decay_dve, q * NS + s + 1)
                    pe.wait_ge(decay_act, q * NS + s + 1)
                    for k in range(GB):
                        for h in range(2):
                            w = decay[:, t, k, h * HALF:(h + 1) * HALF].bitcast(BF16)
                            nc.tensor.matmul(ps[:, h, :], stage_b[:, t, k, 0:2 * F], w,
                                             start=s == 0 and k == 0, stop=False)
                    for k in (0, 2):
                        for h in range(2):
                            for i in range(2):
                                w = decay[:, t, k + i, h * HALF:(h + 1) * HALF].bitcast(BF16)
                                mm = nc.tensor.matmul(ps[i * F:(i + 1) * F, h, :], stage_b[:, t, k + i, 2 * F:3 * F], w,
                                                      start=False, stop=s == NS - 1 and k == 2)
                    mm.then_inc(decay_used, 1)
                pe.wait_ge(sum2_copied, q * 2 + 2)
                pe.wait_ge(sum2_read, q)
                for c in range(CB):
                    mm = nc.tensor.matmul(ps[:, 4, c * F:(c + 1) * F], turn_in[:, c * P:(c + 1) * P], fold[:],
                                          start=True, stop=True)
                mm.then_inc(sum2_turned, 1)
            if upto < 3:
                return

            pe.wait_ge(ext_ready, 1)
            pe.wait_ge(sum2_read, NQ)
            for n in range(2 * NQ):
                src = (U, V_)[n % 2]
                if n >= 2:
                    pe.wait_ge(uv_copied, n - 1)
                for c in range(CB):
                    bank = 2 * (n % 2) + c // 4
                    mm = nc.tensor.transpose(ps[0:F + 2, bank, (c % 4) * P:(c % 4 + 1) * P],
                                             src[:, n // 2 * CB + c, :], ident[:])
                mm.then_inc(uv_ready, 1)
            pe.wait_ge(uv_copied, 2 * NQ)
            LAG = 3
            with pe.Fori(0, NQ) as q:
                for u in range(GB * NS + LAG):
                    if u < GB * NS:
                        s, k = u // GB, u % GB
                        if k == 0:
                            pe.wait_ge(staged_qd, q * (2 * NS) + 2 * (s + 1))
                        for h in range(2):
                            pe.wait_ge(clamped, q * (4 * GB * NS) + (4 * u + 2 * (h + 1)))
                            cols = bass.ds(q * QC + h * HALF, HALF)
                            nc.tensor.matmul(ps[:, h, :], stat_q[:, s % 2, k * P:(k + 1) * P], UT[:, cols],
                                             start=True, stop=True)
                            nc.tensor.matmul(ps[:, 2 + h, :], stat_d[:, s % 2, k * P:(k + 1) * P], UT[:, cols],
                                             start=True, stop=True).then_inc(dist_ready, 1)
                    if u >= LAG:
                        v = u - LAG
                        s, k = v // GB, v % GB
                        if k == 0:
                            pe.wait_ge(staged_ext, q * NS + s + 1)
                        pe.wait_ge(weighted, q * (GB * NS) + (v + 1 + 2))
                        for h in range(2):
                            mm = nc.tensor.matmul(ps[0:F + 1, 4 + h, :], stage_f[:, s % 2, k, :],
                                                  ring[:, s % RING, k, h * HALF:(h + 1) * HALF],
                                                  start=v == 0, stop=v == GB * NS - 1)
                        mm.then_inc(gathered, 1)
                pe.wait_ge(agg_copied, q * 2 + 2)
                pe.wait_ge(agg_read, q)
                for c in range(CB):
                    bank, at_ = 6 + c // 4, (c % 4) * (F + 1)
                    mm = nc.tensor.matmul(ps[:, bank, at_:at_ + F + 1], turn_in[0:F + 1, c * P:(c + 1) * P],
                                          ident[0:F + 1, 0:F + 1], start=True, stop=True)
                mm.then_inc(agg_turned, 1)
            pe.wait_ge(tail_steps, TAIL_AGG)
            for n in range(NQ):
                if n >= 2:
                    pe.wait_ge(aggT_copied, n - 1)
                for c in range(CB):
                    bank = 2 * (n % 2) + c // 4
                    mm = nc.tensor.transpose(ps[0:F, bank, (c % 4) * P:(c % 4 + 1) * P], Y[:, n * CB + c, :], ident[:])
                mm.then_inc(aggT_ready, 1)
                pe.wait_ge(aggT_copied, n + 1)
                for c in range(CB):
                    mm = nc.tensor.matmul(ps[:, 4 + n, c * F:(c + 1) * F], aggT[:, n % 2, c * P:(c + 1) * P],
                                          w3_sb[0:F, :], start=True, stop=True)
                mm.then_inc(moved_ready, 1)

        def copy_product(act, p, q):
            act.wait_ge(ring_used, (q + 1) * NS + p * SLOTS)
            act.wait_ge(turned[p], q)
            nc.scalar.activation(turn_in[:, HALF:QC], ps[:, 1, :], ACT.Copy).then_inc(product_copied[p], 1)

        def split_act(act, i, src, scale):
            for m in range(3):
                act.wait_ge(parts_steps[i], m)
                if m == 0:
                    act.wait_ge(normed[i], 1)
                rest = src[:] if m == 0 else split_rest[i]
                nc.scalar.activation(parts[:, :, m * F:(m + 1) * F], rest, ACT.Copy).then_inc(parts_act[i], 1)

        def norm_act(act, l):
            act.wait_ge(norm_steps[l], 6)
            nc.scalar.activation(stats[:, 4, :], stats[:, 3, :], ACT.Sqrt).then_inc(norm_root[l], 1)

        @block.scalar
        def _(act):
            def put(dst, src):
                act.dma_start(dst, src).then_inc(consts_in, 16)

            act.dma_start(X[:], x).then_inc(x_in, 16)
            act.dma_start(xT_sb, xT).then_inc(x_in, 16)
            cheb = cheb_w.rearrange("k i o -> i k o")
            put(cheb_sb[0:F], cheb)
            put(cheb_sb[F:P], cheb)
            put(gatWT_sb[:, 0:F], gatWT)
            put(gatWT_sb[:, F:2 * F], gatWT)
            put(gat_a_sb[:], gat_a2)
            put(winT_sb[:], winT)
            put(w_edge[:], wieT)
            for g, (wT, b_in, b_hid) in enumerate(((wheT, bie, bhe), (whnT, bin_, bhn))):
                put(w_hid[0:F, g, 0:2 * F], wT[:, 0:2 * F])
                put(w_hid[0:F, g, 3 * F:4 * F], wT[:, 2 * F:3 * F])
                put(bias_tmp[F:F + 1, 2 * g, :], b_in)
                put(bias_tmp[F:F + 1, 2 * g + 1, :], b_hid)
            put(w2_sb[:], w2)
            put(w3_sb[0:F, :], w3)
            put(b2_sb[:], b2.partition_broadcast(P) if False else b2.broadcast_to([P, F]))
            put(b3_sb[:], b3.broadcast_to([P, F]))
            act.sem_inc(codes_made, 1)

            with act.Fori(0, NQ) as q:
                for s in range(NS):
                    t = s % 2
                    act.wait_ge(codes_stored[t], (q * (NS // 2) + s // 2) * 16)
                    for j, k in enumerate(block_order(0)):
                        for h in range(2):
                            act.wait_ge(rank_ready, q * (2 * GB * NS) + ((s * GB + j) * 2 + h + 1))
                            nc.scalar.activation(codes[:, t, k, h * HALF:(h + 1) * HALF], ps[:, 6 + h, :], ACT.Relu,
                                                 bias=code_bias[:], scale=1.0).then_inc(codes_made, 1)
                    act.wait_ge(codes_made, q * (2 * GB * NS) + ((s + 1) * GB * 2 + 1))
                    act.dma_start(codes_dram[bass.ds(q * NS + (NS - 1 - s), 1)].rearrange("a p n -> p (a n)"),
                                  codes[:, t].rearrange("p k c -> p (k c)")).then_inc(codes_stored[t], 16)
                copy_product(act, 0, q)

            act.wait_ge(codes_stored[0], NQ * NS // 2 * 16)
            act.wait_ge(codes_stored[1], NQ * NS // 2 * 16)
            with act.Fori(0, NQ) as q:
                copy_product(act, 1, q)
                act.wait_ge(counts_turned, q)
                nc.scalar.activation(count_in, ps[0:F, 6:8, :], ACT.Copy).then_inc(counts_copied, 1)
            with act.Fori(0, NQ) as q:
                copy_product(act, 2, q)
            norm_act(act, 0)
            if upto < 1:
                return

            split_act(act, 0, X, 1.0)
            act.preload_act_table_set("exp_and_others")
            with act.Fori(0, NQ) as q:
                for s in range(NS):
                    act.wait_ge(loaded[s % RING], (q * 2 + (24 + s // RING + 1)) * 16)
                    if s < 2:
                        act.wait_ge(diag_cut, q * 2 + s + 1)
                    for pair in range(2):
                        act.wait_ge(pair_used, q * (2 * NS) + (2 * s + pair + 1))
                        nc.scalar.activation(negs[:, pair], ring[:, s % RING, 2 * pair:2 * pair + 2, :], ACT.Relu,
                                             scale=-1.0).then_inc(negs_made, 1)
                act.wait_ge(pair_used, q * (2 * NS) + (2 * NS + 2))
                act.wait_ge(att_ready, q * CB)
                nc.scalar.activation(turn_in[:, HALF:QC], ps[:, 3, :], ACT.Copy).then_inc(sums_copied, 1)
                nc.scalar.activation(weighted_in[:, HALF:QC], ps[:, 1, :], ACT.Copy).then_inc(sums_copied, 1)
                act.wait_ge(hT_ready, q + 1)
                nc.scalar.activation(hT[0:F, :], ps[0:F, 4:6, :], ACT.Copy).then_inc(hT_copied, 1)
                for c in range(CB):
                    act.wait_ge(hid_ready, q * CB + c + 1)
                    if c == 0:
                        act.wait_ge(layer1_sum, q)
                    nc.scalar.activation(hid[:, c].rearrange("p g n -> p (g n)"), ps[:, 4 + 2 * (c % 2), :],
                                         ACT.Copy).then_inc(hid_read, 1)
                act.wait_ge(gate_steps, q * GATE_STEPS + G_SCORES)
                nc.scalar.activation(small[:, 4], small[:, 2], ACT.Exp).then_inc(gate_act, 1)
                nc.scalar.activation(small[:, 5, :, 0], small[:, 3, :, 1], ACT.Exp).then_inc(gate_act, 1)
                act.wait_ge(gate_steps, q * GATE_STEPS + G_SUMS)
                act.wait_ge(hid_read, q * CB + CB)
                rz = hid[:, :, :, 0:2 * F].rearrange("p c g n -> p (c g) n")
                nc.scalar.activation(rz, rz, ACT.Tanh, scale=0.5).then_inc(gate_act, 1)
                act.wait_ge(gate_steps, q * GATE_STEPS + G_NEW)
                nc.scalar.activation(gate[:], gate[:], ACT.Tanh).then_inc(gate_act, 1)
            norm_act(act, 1)
            if upto < 2:
                return

            for n in range(NQ):
                act.wait_ge(h2T_ready, n + 1)
                if n >= 2:
                    act.wait_ge(support_ready, n - 1)
                nc.scalar.activation(h2T[:, n % 2, :], ps[0:F, 2 * (n % 2):2 * (n % 2) + 2, :], ACT.Copy).then_inc(
                    h2T_copied, 1)
                act.wait_ge(support_ready, n + 1)
                nc.scalar.activation(support[:, n * CB:(n + 1) * CB, :].rearrange("p c f -> p (c f)"), ps[:, 4 + n, :],
                                     ACT.Copy, scale=CODE_SCALE).then_inc(support_read, 1)
            act.wait_ge(support_read, NQ)
            split_act(act, 1, support, 1.0)
            with act.Fori(0, NQ) as q:
                for s in range(NS):
                    act.wait_ge(code_loaded[s % RING], (q * 2 + (s // RING + 1)) * 16)
                    act.wait_ge(decay_used, q * NS + (s - 1) if s >= 2 else q * NS)
                    nc.scalar.activation(decay[:, s % 2, 3, :], code_in[:, s % RING, 3, :], ACT.Copy,
                                         scale=128.0).then_inc(decay_act, 1)
                act.wait_ge(decay_used, q * NS + NS)
                act.wait_ge(sum2_turned, q)
                nc.scalar.activation(turn_in[:, HALF:QC], ps[:, 1, :], ACT.Copy).then_inc(sum2_copied, 1)
            norm_act(act, 2)
            if upto < 3:
                return

            for n in range(2 * NQ):
                act.wait_ge(uv_ready, n + 1)
                dst = (UT, VT)[n % 2]
                nc.scalar.activation(dst[:, n // 2 * QC:(n // 2 + 1) * QC],
                                     ps[0:F + 2, 2 * (n % 2):2 * (n % 2) + 2, :], ACT.Copy).then_inc(uv_copied, 1)
            act.wait_ge(uv_copied, 2 * NQ)
            act.preload_act_table_set("natural_log_exp_and_others")

            def stage_qd(q, s):
                act.wait_ge(dist_ready, q * (2 * GB * NS) + max(s - 1, 0) * 2 * GB)
                cols = slice(s * GB * P, (s + 1) * GB * P)
                nc.scalar.activation(stat_q[:, s % 2, :], VT[:, cols], ACT.Copy,
                                     scale=minus_two[0:F + 2, :]).then_inc(staged_qd, 1)
                nc.scalar.activation(stat_d[:, s % 2, :], UT[:, cols], ACT.Copy,
                                     scale=minus_two[0:F + 2, :]).then_inc(staged_qd, 1)

            with act.Fori(0, NQ) as q:
                stage_qd(q, 0)
                for u in range(GB * NS + 1):
                    n = q * (GB * NS)
                    if u < GB * NS:
                        act.wait_ge(clamped, q * (4 * GB * NS) + (4 * u + 8))
                        both = dist[:, u % 3].rearrange("p a c -> p (a c)")
                        nc.scalar.activation(both, both, ACT.Ln).then_inc(logs_made, 1)
                        if u % GB == GB - 2 and u < GB * (NS - 1):
                            stage_qd(q, u // GB + 1)
                    if u >= 1:
                        v = u - 1
                        size, rest = logs[:, v % 2, 0, :], logs[:, v % 2, 1, :]
                        act.wait_ge(clipped, n + (v + 1))
                        nc.scalar.activation(size, size, ACT.Exp, scale=0.5).then_inc(atanh_steps, 1)
                        act.wait_ge(log_pairs, q * (2 * GB * NS) + 2 * (v + 1))
                        nc.scalar.activation(rest, rest, ACT.Exp, scale=-0.5)
                        act.wait_ge(atanh_steps, n + (v + 1))
                        nc.scalar.activation(dist[:, v % 3, 0, :], size, ACT.Ln, bias=1.0, scale=1.0)
                        nc.scalar.activation(dist[:, v % 3, 1, :], size, ACT.Ln, bias=1.0, scale=-1.0).then_inc(
                            atanh_ready, 1)
                act.wait_ge(gathered, n + GB * NS)
                act.wait_ge(agg_turned, q)
                nc.scalar.activation(turn_in[0:F + 1, HALF:QC], ps[0:F + 1, 5, :], ACT.Copy).then_inc(agg_copied, 1)
            for n in range(NQ):
                act.wait_ge(aggT_ready, n + 1)
                if n >= 2:
                    act.wait_ge(moved_ready, n - 1)
                nc.scalar.activation(aggT[:, n % 2, :], ps[0:F, 2 * (n % 2):2 * (n % 2) + 2, :], ACT.Copy).then_inc(
                    aggT_copied, 1)
            act.wait_ge(tail_steps, TAIL_AGG + TAIL_NORM)
            nc.scalar.activation(stats[:, 1, :], stats[:, 0, :], ACT.Sqrt).then_inc(tail_act, 1)
            act.wait_ge(tail_steps, TAIL_AGG + TAIL_NORM + 1)
            nc.scalar.activation(stats[:, 3, :], stats[:, 2, :], ACT.Tanh).then_inc(tail_act, 1)
            norm_act(act, 3)

        @block.vector
        def _(dve):
            V = nc.vector

            def steps_on(s, base=0):
                n = [0]

                def step(ins):
                    n[0] += 1
                    ins.then_inc(s, 1)
                    dve.wait_ge(s, base + n[0])
                return step

            def norm(l):
                step = steps_on(norm_steps[l])
                wide = [P, NB, F]
                step(V.tensor_reduce(stats[:, 0, :], Y[:], AX_X, ALU.add))
                step(V.tensor_scalar(stats[:, 1, :], stats[:, 0, :], 1.0 / F, None, ALU.mult))
                step(V.tensor_tensor(Y[:], Y[:], stats[:, 1, :].unsqueeze(2).broadcast_to(wide), ALU.subtract))
                step(V.tensor_tensor(X[:], Y[:], Y[:], ALU.mult))
                step(V.tensor_reduce(stats[:, 2, :], X[:], AX_X, ALU.add))
                step(V.tensor_scalar(stats[:, 3, :], stats[:, 2, :], 1.0 / F, EPS, ALU.mult, ALU.add))
                dve.wait_ge(norm_root[l], 1)
                step(V.reciprocal(stats[:, 5, :], stats[:, 4, :]))
                V.tensor_tensor(X[:], Y[:], stats[:, 5, :].unsqueeze(2).broadcast_to(wide),
                                ALU.mult).then_inc(normed[l], 1)

            dve.wait_ge(consts_in, N_PUTS * 16)
            dve.wait_ge(consts_made, 1)
            for p in range(3):
                V.tensor_copy(turn_w[:, p, 0:F], fold[:])
            V.tensor_tensor(w_first[:], cheb_sb[0:F, 0, :], cheb_sb[0:F, 2, :], ALU.subtract)
            V.tensor_tensor(turn_w[:, 0, F:P], cheb_sb[:, 1, :], cheb_sb[:, 3, :], ALU.subtract)
            V.tensor_scalar(turn_w[:, 1, F:P], cheb_sb[:, 2, :], 2.0, None, ALU.mult)
            V.tensor_scalar(turn_w[:, 2, F:P], cheb_sb[:, 3, :], 2.0, None, ALU.mult)
            for g in range(2):
                V.memset(w_hid[0:F, g, 2 * F:3 * F], 0.0)
                b_in, b_hid = bias_tmp[F:F + 1, 2 * g, :], bias_tmp[F:F + 1, 2 * g + 1, :]
                V.tensor_tensor(w_hid[F:F + 1, g, 0:2 * F], b_in[:, 0:2 * F], b_hid[:, 0:2 * F], ALU.add)
                V.tensor_copy(w_hid[F:F + 1, g, 2 * F:3 * F], b_in[:, 2 * F:3 * F])
                V.tensor_copy(w_hid[F:F + 1, g, 3 * F:4 * F], b_hid[:, 2 * F:3 * F])
            V.memset(w_att[0:F, 3 * F:6 * F], 0.0)
            V.memset(w_att[F:P, 0:3 * F], 0.0)
            dve.drain().then_inc(weights_made, 1)

            dve.wait_ge(x_in, 32)
            for n in range(4):
                dve.wait_ge(first_ready, n + 1)
                V.tensor_tensor(Y[:, n * 8:(n + 1) * 8, :], ps[:, n, :].rearrange("p (c f) -> p c f", f=F),
                                X[:, n * 8:(n + 1) * 8, :], ALU.add).then_inc(first_read, 1)
            dve.wait_ge(gat_ready, 1)
            V.tensor_copy(w_score[0:F, :], ps[0:F, 4, 0:2])
            V.tensor_copy(w_score[F:P, 0:1], ps[F:P, 4, 1:2])
            V.tensor_copy(w_score[F:P, 1:2], ps[F:P, 4, 0:1])
            V.tensor_copy(w_att[0:F, 0:3 * F], ps[0:F, 5, 0:3 * F])
            V.tensor_scalar(w_att[F:P, 3 * F:6 * F], ps[F:P, 5, 0:3 * F], -1.0, None, ALU.mult)
            dve.drain().then_inc(first_read, 1)
            dve.wait_ge(first_read, 5)

            def turn(p, q):
                dve.wait_ge(ring_used, (q + 1) * NS + p * SLOTS)
                dve.wait_ge(turned[p], q)
                V.tensor_copy(turn_in[:, 0:HALF], ps[:, 0, :]).then_inc(product_copied[p], 1)
                dve.wait_ge(turned[p], q + 1)
                turned_rows = ps[:, 4:6, :].rearrange("p a (c f) -> p (a c) f", f=2 * F)
                blocks = bass.ds(q * CB, CB)
                if p == 0:
                    V.tensor_copy(T1[:, blocks, :], turned_rows[:, :, 0:F])
                if p == 1:
                    V.scalar_tensor_tensor(T2[:, blocks, :], turned_rows[:, :, 0:F], 2.0, X[:, blocks, :],
                                           ALU.mult, ALU.subtract)
                V.tensor_tensor(Y[:, blocks, :], turned_rows[:, :, F:2 * F], Y[:, blocks, :],
                                ALU.add).then_inc(turn_read[p], 1)

            with dve.Fori(0, NQ) as q:
                for s in range(NS):
                    r, t = s % RING, s % 2
                    dve.wait_ge(loaded[r], (q * 2 + (s // RING + 1)) * 16)
                    dve.wait_ge(ring_used, q * NS + max(s - 1, 0) if s < 2 else q * NS + s - 1)
                    V.tensor_scalar(mask[:, t], ring[:, r], 0.0, None, ALU.not_equal).then_inc(dve_signs[0], 1)
                    for j in range(GB):
                        if s == 0 and j == 0:
                            V.memset(later[:, t, 0], 0.0).then_inc(signs_ready[0], 1)
                            dve.wait_ge(dve_signs[0], q * NS + s + 1)
                            continue
                        k_seen = block_order(0)[(j - 1) % GB]
                        t_seen = t if j else 1 - t
                        dve.wait_ge(dve_signs[0], q * NS + s + 1)
                        dve.wait_ge(signs_ready[0], q * (GB * NS) + (s * GB + j))
                        V.tensor_tensor(later[:, t, j], later[:, t_seen, (j - 1) % GB], mask[:, t_seen, k_seen],
                                        ALU.add).then_inc(signs_ready[0], 1)
                turn(0, q)
            dve.wait_ge(turn_read[0], NQ)
            with dve.Fori(0, NQ) as q:
                for s in range(NS):
                    r, t = s % RING, s % 2
                    dve.wait_ge(loaded[r], (q * 2 + (8 + s // RING + 1)) * 16)
                    dve.wait_ge(ring_used, q * NS + (SLOTS + s - 1))
                    above = V.tensor_scalar(mask[:, t], ring[:, r], 0.0, None, ALU.is_gt)
                    below = V.tensor_scalar(later[:, t], ring[:, r], 0.0, None, ALU.is_lt)
                    if s < 2:
                        above.then_inc(dve_signs[1], 1)
                        below.then_inc(dve_signs[1], 1)
                        dve.wait_ge(dve_signs[1], q * 4 + 2 * (s + 1))
                        cut = offdiag_b[:].unsqueeze(1).broadcast_to([P, GB, P])
                        for part in (mask, later):
                            mine = own_blocks(part[:, t], s)
                            below = V.tensor_tensor(mine, mine, cut, ALU.mult)
                    below.then_inc(signs_ready[1], 1)
                turn(1, q)
                dve.wait_ge(counts_turned, q + 1)
                V.tensor_copy(degrees[:, bass.ds(q * CB, CB), :],
                              ps[:, 6, 0:2 * CB].rearrange("p (c n) -> p c n", n=2)).then_inc(counts_read, 1)
            dve.wait_ge(turn_read[1], NQ)
            with dve.Fori(0, NQ) as q:
                for s in range(NS):
                    dve.wait_ge(loaded[s % RING], (q * 2 + (16 + s // RING + 1)) * 16)
                    if s == 0:
                        dve.wait_ge(rows_turned, q)
                    for k in range(GB):
                        dve.wait_ge(row_steps, q * (GB * NS) + (s * GB + k))
                        edges = ring[:, s % RING, k, :]
                        if s == 0 and k == 0:
                            V.tensor_copy(row_sum, edges).then_inc(row_steps, 1)
                        else:
                            V.tensor_tensor(row_sum, row_sum, edges, ALU.add).then_inc(row_steps, 1)
                dve.wait_ge(row_steps, (q + 1) * (GB * NS))
                dve.sem_inc(row_ready, 1)
                turn(2, q)
                dve.wait_ge(rows_turned, q + 1)
                V.tensor_copy(edge_sum[:, bass.ds(q * CB, CB)], ps[:, 6, 0:CB]).then_inc(rows_read, 1)
            dve.wait_ge(turn_read[2], NQ)
            norm(0)
            if upto < 1:
                return

            def split(i, src):
                for m in range(2):
                    dve.wait_ge(parts_act[i], m + 1)
                    rest = src if m == 0 else split_rest[i]
                    V.tensor_tensor(split_rest[i], rest, parts[:, :, m * F:(m + 1) * F],
                                    ALU.subtract).then_inc(parts_steps[i], 1)
                    dve.wait_ge(parts_steps[i], m + 1)
                dve.wait_ge(parts_act[i], 3)
                dve.sem_inc(parts_ready[i], 1)

            dve.wait_ge(normed[0], 1)
            split(0, X[:])
            V.memset(hT[F:F + 1, :], 1.0)
            with dve.Fori(0, NQ) as q:
                for s in range(NS):
                    r = s % RING
                    dve.wait_ge(loaded[r], (q * 2 + (24 + s // RING + 1)) * 16)
                    if s < 2:
                        mine = own_blocks(ring[:, r], s)
                        base = q * 4 + 2 * s
                        V.tensor_tensor(own, mine, ident[:].unsqueeze(1).broadcast_to([P, GB, P]),
                                        ALU.mult).then_inc(diag_steps, 1)
                        dve.wait_ge(diag_steps, base + 1)
                        V.tensor_reduce(diag[:, bass.ds(q * CB + s * GB, GB)], own, AX_X, ALU.add).then_inc(
                            diag_steps, 1)
                        V.tensor_tensor(mine, mine, offdiag[:].unsqueeze(1).broadcast_to([P, GB, P]),
                                        ALU.mult).then_inc(diag_cut, 1)
                        dve.wait_ge(diag_cut, q * 2 + s + 1)
                        dve.wait_ge(diag_steps, base + 2)
                    for pair in range(2):
                        m = 2 * s + pair
                        edges = ring[:, r, 2 * pair:2 * pair + 2, :]
                        dve.wait_ge(pair_used, q * (2 * NS) + (m + 1))
                        V.tensor_scalar(more[:, pair], edges, 0.0, None, ALU.is_gt)
                        V.tensor_scalar(less[:, pair], edges, 0.0, None, ALU.is_lt)
                        dve.wait_ge(negs_made, q * (2 * NS) + (m + 1))
                        V.tensor_scalar(edges, edges, 0.0, None, ALU.max).then_inc(rect_ready, 1)
                dve.wait_ge(pair_used, q * (2 * NS) + (2 * NS + 2))
                dve.wait_ge(att_ready, q * CB)
                V.tensor_copy(turn_in[:, 0:HALF], ps[:, 2, :]).then_inc(sums_copied, 1)
                V.tensor_copy(weighted_in[:, 0:HALF], ps[:, 0, :]).then_inc(sums_copied, 1)
                for c in range(CB):
                    dve.wait_ge(att_ready, q * CB + c + 1)
                    V.tensor_copy(att[:, c, :], ps[:, 5 + 2 * (c % 2), 0:6 * F + 2]).then_inc(att_read, 1)
                dve.wait_ge(att_read, q * CB + CB)

                count = [0]

                def step(ins):
                    count[0] += 1
                    ins.then_inc(gate_steps, 1)
                    dve.wait_ge(gate_steps, q * GATE_STEPS + count[0])

                blocks = bass.ds(q * CB, CB)
                pairs = [P, CB, 2]
                scores = att[:, :, 6 * F:6 * F + 2]
                num, present, e, top, ex, ex0, z, wt = (small[:, i] for i in (0, 1, 2, 3, 4, 5, 6, 7))
                step(V.tensor_copy(num, degrees[:, blocks, :]))
                step(V.tensor_scalar(present, num, 0.0, None, ALU.is_gt))
                step(V.scalar_tensor_tensor(e, scores, LEAK, scores, ALU.mult, ALU.max))
                step(V.tensor_tensor(e, e, present, ALU.mult))
                step(V.tensor_scalar(present, present, NEG_INF, -NEG_INF, ALU.mult, ALU.add))
                step(V.tensor_tensor(e, e, present, ALU.add))
                step(V.tensor_reduce(top[:, :, 0], e, AX_X, ALU.max))
                step(V.tensor_scalar(top[:, :, 0], top[:, :, 0], -NEG_INF, None, ALU.max))
                step(V.tensor_tensor(e, e, top[:, :, 0:1].broadcast_to(pairs), ALU.subtract))
                step(V.tensor_scalar(top[:, :, 1], top[:, :, 0], -1.0, -NEG_INF, ALU.mult, ALU.add))
                assert count[0] == G_SCORES
                step(V.tensor_reduce(z[:, :, 0], num, AX_X, ALU.add))
                step(V.tensor_scalar(z[:, :, 0], z[:, :, 0], -1.0, float(N), ALU.mult, ALU.add))
                dve.wait_ge(gate_act, q * 4 + 2)
                step(V.tensor_tensor(z[:, :, 0], z[:, :, 0], ex0[:, :, 0], ALU.mult))
                step(V.tensor_tensor(wt, ex, num, ALU.mult))
                step(V.tensor_reduce(z[:, :, 1], wt, AX_X, ALU.add))
                step(V.tensor_tensor(z[:, :, 0], z[:, :, 0], z[:, :, 1], ALU.add))
                step(V.reciprocal(z[:, :, 1], z[:, :, 0]))
                step(V.tensor_tensor(wt, ex, z[:, :, 1:2].broadcast_to(pairs), ALU.mult))
                third = [P, CB, 3 * F]
                step(V.tensor_tensor(att[:, :, 0:3 * F], att[:, :, 0:3 * F], wt[:, :, 0:1].broadcast_to(third),
                                     ALU.mult))
                step(V.tensor_tensor(att[:, :, 3 * F:6 * F], att[:, :, 3 * F:6 * F], wt[:, :, 1:2].broadcast_to(third),
                                     ALU.mult))
                step(V.tensor_tensor(att[:, :, 0:3 * F], att[:, :, 0:3 * F], att[:, :, 3 * F:6 * F], ALU.add))
                dve.wait_ge(hid_read, q * CB + CB)
                step(V.tensor_tensor(hid[:, :, 1, 0:3 * F], hid[:, :, 1, 0:3 * F], att[:, :, 0:3 * F], ALU.add))
                assert count[0] == G_SUMS
                rz = hid[:, :, :, 0:2 * F].rearrange("p c g n -> p (c g) n")
                reset, update, new_in, new_hid = (hid[:, :, :, i * F:(i + 1) * F] for i in range(4))
                dve.wait_ge(gate_act, q * 4 + 3)
                step(V.tensor_scalar(rz, rz, 0.5, 0.5, ALU.mult, ALU.add))
                step(V.tensor_tensor(gate, reset, new_hid, ALU.mult))
                step(V.tensor_tensor(gate, gate, new_in, ALU.add))
                assert count[0] == G_NEW
                dve.wait_ge(gate_act, q * 4 + 4)
                hidden = x_q.unsqueeze(2).broadcast_to([P, CB, 2, F])
                step(V.tensor_tensor(new_hid, hidden, gate, ALU.subtract))
                step(V.tensor_tensor(new_hid, new_hid, update, ALU.mult))
                step(V.tensor_tensor(gate, gate, new_hid, ALU.add))
                step(V.tensor_tensor(gate[:, :, 0, :], gate[:, :, 0, :], gate[:, :, 1, :], ALU.add))
                step(V.tensor_tensor(gate[:, :, 0, :], gate[:, :, 0, :],
                                     diag[:, blocks].unsqueeze(2).broadcast_to([P, CB, F]), ALU.mult))
                assert count[0] == GATE_STEPS
                V.tensor_tensor(Y[:, blocks, :], gate[:, :, 0, :], x_q, ALU.add).then_inc(layer1_sum, 1)
            dve.wait_ge(layer1_sum, NQ)
            norm(1)
            if upto < 2:
                return

            dve.wait_ge(support_read, NQ)
            split(1, support)
            with dve.Fori(0, NQ) as q:
                for s in range(NS):
                    dve.wait_ge(code_loaded[s % RING], (q * 2 + (s // RING + 1)) * 16)
                    dve.wait_ge(decay_used, q * NS + (s - 1) if s >= 2 else q * NS)
                    V.tensor_scalar(decay[:, s % 2, 0:3, :], code_in[:, s % RING, 0:3, :], 128.0, None,
                                    ALU.mult).then_inc(decay_dve, 1)
                dve.wait_ge(decay_used, q * NS + NS)
                dve.wait_ge(sum2_turned, q)
                V.tensor_copy(turn_in[:, 0:HALF], ps[:, 0, :]).then_inc(sum2_copied, 1)
                dve.wait_ge(sum2_turned, q + 1)
                blocks = bass.ds(q * CB, CB)
                V.tensor_tensor(Y[:, blocks, :], ps[:, 4, :].rearrange("p (c f) -> p c f", f=F), X[:, blocks, :],
                                ALU.add).then_inc(sum2_read, 1)
            dve.wait_ge(sum2_read, NQ)
            V.tensor_tensor(Y[:], Y[:], b2_sb[:].unsqueeze(1).broadcast_to([P, NB, F]), ALU.add).then_inc(sum2_read, 1)
            dve.wait_ge(sum2_read, NQ + 1)
            norm(2)
            if upto < 3:
                return

            dve.wait_ge(normed[2], 1)
            step = steps_on(ext_steps)
            norm2 = stats[:, 6, :]
            step(V.tensor_tensor(Y[:], X[:], X[:], ALU.mult))
            step(V.tensor_reduce(norm2, Y[:], AX_X, ALU.add))
            for rows, a, b in ((U, F, F + 1), (V_, F + 1, F)):
                step(V.tensor_copy(rows[:, :, 0:F], X[:]))
                step(V.tensor_copy(rows[:, :, a:a + 1], norm2.unsqueeze(2)))
                step(V.memset(rows[:, :, b:b + 1], 1.0))
            step(V.tensor_copy(x_ext[:, :, 0:F], X[:]))
            step(V.tensor_scalar(x_ext[:, :, F:F + 1], norm2.unsqueeze(2), 1.0, None, ALU.add))
            dve.sem_inc(ext_ready, 1)
            dve.sem_inc(clamped, 4)
            dve.sem_inc(weighted, 2)
            dve.wait_ge(uv_copied, 2 * NQ)
            with dve.Fori(0, NQ) as q:
                for u in range(GB * NS + 2):
                    if u < GB * NS:
                        dve.wait_ge(weighted, q * (GB * NS) + (max(u - 2, 0) + 2))
                        for h in range(2):
                            dve.wait_ge(dist_ready, q * (2 * GB * NS) + (2 * u + h + 1))
                            cols = slice(h * HALF, (h + 1) * HALF)
                            V.tensor_scalar(dist[:, u % 3, 0, cols], ps[:, h, :], TINY_Q, None, ALU.max).then_inc(
                                clamped, 1)
                            V.tensor_scalar(dist[:, u % 3, 1, cols], ps[:, 2 + h, :], MIN_NORM, None,
                                            ALU.max).then_inc(clamped, 1)
                    if 1 <= u <= GB * NS:
                        v = u - 1
                        dve.wait_ge(log_pairs, q * (2 * GB * NS) + (2 * v + 1))
                        V.tensor_scalar(logs[:, v % 2, 0, :], logs[:, v % 2, 0, :], LOG_CLIP, None,
                                        ALU.min).then_inc(clipped, 1)
                    if u >= 2:
                        v = u - 2
                        dve.wait_ge(atanh_ready, q * (GB * NS) + (v + 1))
                        a, b = dist[:, v % 3, 0, :], dist[:, v % 3, 1, :]
                        V.tensor_tensor(a, a, b, ALU.subtract).then_inc(final_steps, 1)
                        dve.wait_ge(final_steps, q * (2 * GB * NS) + (2 * v + 1))
                        V.tensor_tensor(a, a, logs[:, v % 2, 1, :], ALU.mult).then_inc(final_steps, 1)
                        dve.wait_ge(final_steps, q * (2 * GB * NS) + (2 * v + 2))
                        edges = ring[:, v // GB % RING, v % GB, :]
                        if v % GB == 0:
                            dve.wait_ge(loaded[v // GB % RING], (q * 2 + (32 + v // GB // RING + 1)) * 16)
                        V.tensor_tensor(edges, edges, a, ALU.mult).then_inc(weighted, 1)
                dve.wait_ge(gathered, q * (GB * NS) + GB * NS)
                dve.wait_ge(agg_turned, q)
                V.tensor_copy(turn_in[0:F + 1, 0:HALF], ps[0:F + 1, 4, :]).then_inc(agg_copied, 1)
                dve.wait_ge(agg_turned, q + 1)
                sums = [ps[:, 6 + i, 0:4 * (F + 1)].rearrange("p (c f) -> p c f", f=F + 1) for i in range(2)]
                for i in range(2):
                    V.tensor_copy(Y[:, bass.ds(q * CB + 4 * i, 4), :], sums[i][:, :, 0:F])
                V.tensor_copy(stats[:, 7, bass.ds(q * CB, 4)], sums[0][:, :, F])
                V.tensor_copy(stats[:, 7, bass.ds(q * CB + 4, 4)], sums[1][:, :, F]).then_inc(agg_read, 1)
            dve.wait_ge(agg_read, NQ)
            step = steps_on(tail_steps)
            wide = [P, NB, F]
            room = dist[:].rearrange("p u a c -> p (u a c)")[:, 0:NB * F].rearrange("p (b f) -> p b f", f=F)
            s_dot, s_own, s_b, s_kappa = (stats[:, i, :] for i in (0, 1, 2, 3))
            step(V.tensor_tensor(room, X[:], Y[:], ALU.mult))
            step(V.tensor_reduce(s_dot, room, AX_X, ALU.add))
            step(V.scalar_tensor_tensor(s_own, s_dot, 2.0, stats[:, 7, :], ALU.mult, ALU.subtract))
            step(V.tensor_scalar(s_b, norm2, -1.0, 1.0, ALU.mult, ALU.add))
            step(V.tensor_tensor(room, X[:], s_own.unsqueeze(2).broadcast_to(wide), ALU.mult))
            step(V.tensor_tensor(Y[:], Y[:], s_b.unsqueeze(2).broadcast_to(wide), ALU.mult))
            step(V.tensor_tensor(Y[:], Y[:], room, ALU.add))
            step(V.tensor_scalar(s_b, s_b, MIN_NORM, 0.5, ALU.max, ALU.mult))
            step(V.tensor_scalar(s_dot, edge_sum[:], 1e-8, None, ALU.max))
            step(V.reciprocal(s_own, s_dot))
            step(V.tensor_tensor(s_kappa, s_b, s_own, ALU.mult))
            step(V.tensor_tensor(Y[:], Y[:], s_kappa.unsqueeze(2).broadcast_to(wide), ALU.mult))
            for n in range(NQ):
                dve.wait_ge(moved_ready, n + 1)
                step(V.tensor_tensor(room[:, n * CB:(n + 1) * CB, :], ps[:, 4 + n, :].rearrange("p (c f) -> p c f", f=F),
                                     b3_sb[:].unsqueeze(1).broadcast_to([P, CB, F]), ALU.add))
            step(V.tensor_tensor(Y[:], room, room, ALU.mult))
            step(V.tensor_reduce(stats[:, 0, :], Y[:], AX_X, ALU.add))
            dve.wait_ge(tail_act, 1)
            step(V.tensor_scalar(stats[:, 2, :], stats[:, 1, :], MIN_NORM, None, ALU.max))
            dve.wait_ge(tail_act, 2)
            step(V.reciprocal(stats[:, 4, :], stats[:, 2, :]))
            step(V.tensor_tensor(stats[:, 5, :], stats[:, 3, :], stats[:, 4, :], ALU.mult))
            step(V.tensor_tensor(room, room, stats[:, 5, :].unsqueeze(2).broadcast_to(wide), ALU.mult))
            step(V.tensor_tensor(Y[:], X[:], room, ALU.add))
            norm(3)

        @block.sync
        def _(sp):
            sp.wait_ge(normed[min(upto, 3)], 1)
            sp.dma_start(out, X[:]).then_inc(out_stored, 16)
            sp.wait_ge(out_stored, 16)


def lay_out(x, adj, L0_gnn_weight, L1_gnn_W_gat, L1_gnn_a_gat, L1_gnn_w_ih_e, L1_gnn_w_hh_e, L1_gnn_b_ih_e,
            L1_gnn_b_hh_e, L1_gnn_w_ih_n, L1_gnn_w_hh_n, L1_gnn_b_ih_n, L1_gnn_b_hh_n, L2_gnn_weight, L2_gnn_bias,
            L3_gnn_weight, L3_gnn_bias):
    def turn(a):
        return np.ascontiguousarray(np.asarray(a).T)

    def nodes(a):
        return np.ascontiguousarray(np.asarray(a).reshape(NB, P, F).transpose(1, 0, 2))

    def row(a):
        return np.ascontiguousarray(np.asarray(a).reshape(1, -1))

    return {
        "adjT": turn(adj), "x": nodes(x), "xT": turn(x),
        "cheb_w": np.ascontiguousarray(L0_gnn_weight),
        "gatWT": turn(L1_gnn_W_gat), "gat_a2": turn(np.asarray(L1_gnn_a_gat).reshape(2, F)),
        "wieT": turn(L1_gnn_w_ih_e), "wheT": turn(L1_gnn_w_hh_e), "bie": row(L1_gnn_b_ih_e), "bhe": row(L1_gnn_b_hh_e),
        "winT": turn(L1_gnn_w_ih_n), "whnT": turn(L1_gnn_w_hh_n), "bin": row(L1_gnn_b_ih_n), "bhn": row(L1_gnn_b_hh_n),
        "w2": np.ascontiguousarray(L2_gnn_weight), "b2": row(L2_gnn_bias),
        "w3": np.ascontiguousarray(L3_gnn_weight), "b3": row(L3_gnn_bias),
    }


def kernel(**inputs):
    from concourse import bacc
    from concourse.bass_utils import run_bass_kernel_spmd

    nc = bacc.Bacc("TRN2", target_bir_lowering=False, num_devices=1)
    arrays = {f"in_{k}": a for k, a in lay_out(**inputs).items()}
    aps = [nc.dram_tensor(k, a.shape, mybir.dt.from_np(a.dtype), kind="ExternalInput").ap()
           for k, a in arrays.items()]
    out = nc.dram_tensor("out_nodes", (P, NB, F), F32, kind="ExternalOutput").ap()
    adjacency_stack(nc, *aps, out)
    result = run_bass_kernel_spmd(nc, [arrays], core_ids=[0])
    return result.results[0]["out_nodes"].transpose(1, 0, 2).reshape(N, F)
```

```python
from contextlib import ExitStack

import numpy as np

import concourse.bass as bass
from concourse import mybir

ALU = mybir.AluOpType
ACT = mybir.ActivationFunctionType
AX_X = mybir.AxisListType.X
F32 = mybir.dt.float32
BF16 = mybir.dt.bfloat16
I16 = mybir.dt.int16
U8 = mybir.dt.uint8

P = 128
N = 4096
F = 64
NB = N // P
QC = 1024
NQ = N // QC
GB = 4
NS = NB // GB
HALF = 512
CB = QC // P
RING = 4
SLOTS = NQ * NS
EPS = 1e-5
LEAK = 0.2
NEG_INF = 9.0e15
MAX_NEIGH = 100
CODE_BIAS = 8192.0
CODE_SCALE = 2.0 ** 27
TINY_Q = 2.0 ** -63
MIN_NORM = 1e-15
TANH_CLIP = 1.0 - 1e-5


def adjacency_stack(nc, adjT, x, xT, cheb_w, gatWT, gat_a2, wieT, wheT, bie, bhe, winT, whnT, bin_, bhn,
                    w2, b2, w3, b3, out):
    adj_slots = adjT.rearrange("(g k p) (q c) -> p g k q c", k=GB, p=P, c=QC)
    codes_dram = nc.dram_tensor("codes", [SLOTS, P, GB * QC], U8, kind="Internal").ap()

    ctx = ExitStack()
    with ctx:
        def sb(name, shape, dt=F32):
            return ctx.enter_context(nc.sbuf_tensor(name, shape, dt))

        def sem(name):
            return ctx.enter_context(nc.semaphore(name))

        ps = ctx.enter_context(nc.psum_tensor("ps", [P, 8, HALF], F32))

        WORK = 26 * 1024

        ring = sb("ring", [P, RING, GB, QC])
        X = sb("X", [P, NB, F])
        Y = sb("Y", [P, NB, F])
        stage_f = sb("stage_f", [P, 2, GB, F + 1])
        stage_words = sb("stage_words", [P, 2 * GB * P])
        stage_b = stage_words[:, 0:2 * GB * 3 * F // 2].bitcast(BF16).rearrange("p (t k n) -> p t k n", t=2, k=GB)
        stat = stage_words[0:F + 2, :].rearrange("p (t c) -> p t c", t=2)
        turn_in = sb("turn_in", [P, QC])
        diag = sb("diag", [P, NB])
        degrees = sb("degrees", [P, NB, 2])
        edge_sum = sb("edge_sum", [P, NB])
        stats = sb("stats", [P, 10, NB])
        work = sb("work", [P, WORK])

        ident = sb("ident", [P, P])
        offdiag = sb("offdiag", [P, P])
        offdiag_b = sb("offdiag_b", [P, P], BF16)
        later_or_self = sb("later_or_self", [P, P], BF16)
        minus_ones = sb("minus_ones", [P, P], BF16)
        ones = sb("ones", [P, 32], BF16)
        ones_f = sb("ones_f", [P, 1])
        code_bias = sb("code_bias", [P, 1])
        cheb_sb = sb("cheb_sb", [P, 4, F])
        turn_w = sb("turn_w", [P, 3, 2 * F])
        w_first = sb("w_first", [F, F])
        w_edge = sb("w_edge", [P, 3 * F])
        w_score = sb("w_score", [P, 2])
        w_hid = sb("w_hid", [F + 1, 2, 4 * F])
        w_att = sb("w_att", [P, 6 * F])
        gatWT_sb = sb("gatWT_sb", [F, 2 * F])
        gat_a_sb = sb("gat_a_sb", [F, 2])
        winT_sb = sb("winT_sb", [F, 3 * F])
        w2_sb = sb("w2_sb", [F, F])
        w3_sb = sb("w3_sb", [F + 1, F])
        b2_sb = sb("b2_sb", [P, F])
        b3_sb = sb("b3_sb", [P, F])
        fold = sb("fold", [P, F])
        minus_two = sb("minus_two", [P, 1])

        at = [0]

        def carve(words, reset=None):
            if reset is not None:
                at[0] = reset
            a = at[0]
            at[0] += words
            assert at[0] <= WORK, at[0]
            return work[:, a:a + words]

        T1 = carve(NB * F, 0).rearrange("p (b f) -> p b f", f=F)
        T2 = carve(NB * F).rearrange("p (b f) -> p b f", f=F)
        mask = carve(2 * GB * QC // 2).bitcast(BF16).rearrange("p (t k c) -> p t k c", t=2, k=GB)
        later = carve(2 * GB * QC // 2).bitcast(BF16).rearrange("p (t k c) -> p t k c", t=2, k=GB)
        codes = carve(2 * GB * QC // 4).bitcast(U8).rearrange("p (t k c) -> p t k c", t=2, k=GB)
        xT_sb = carve(N)[0:F, :]
        bias_tmp = carve(4 * 3 * F)[0:F + 1, :].rearrange("p (i n) -> p i n", i=4)
        count_in = codes.rearrange("p t k c -> p (t k c)")[0:F, 0:4 * QC].bitcast(F32)

        row_out = mask[:, 1].rearrange("p k c -> p (k c)")[:, 0:2 * QC].bitcast(F32)
        row_sum = mask[:, 0].rearrange("p k c -> p (k c)")[:, 0:2 * QC].bitcast(F32)

        more = carve(2 * 2 * QC // 2, 0).bitcast(BF16).rearrange("p (t k c) -> p t k c", t=2, k=2)
        less = carve(2 * 2 * QC // 2).bitcast(BF16).rearrange("p (t k c) -> p t k c", t=2, k=2)
        negs = carve(2 * 2 * QC).rearrange("p (t k c) -> p t k c", t=2, k=2)
        hid = carve(CB * 8 * F).rearrange("p (c g n) -> p c g n", c=CB, g=2)
        att = carve(CB * (6 * F + 2)).rearrange("p (c n) -> p c n", c=CB)
        parts = carve(NB * 3 * F // 2).bitcast(BF16).rearrange("p (b n) -> p b n", n=3 * F)
        weighted_in = carve(QC)
        hT = carve(QC)[0:F + 1, :]
        x_q = carve(CB * F).rearrange("p (c f) -> p c f", f=F)
        own = carve(GB * P).rearrange("p (k c) -> p k c", k=GB)
        gate = carve(CB * 2 * F).rearrange("p (c g f) -> p c g f", c=CB, g=2)
        small = carve(16 * 2 * CB).rearrange("p (i c n) -> p i c n", i=16, c=CB)

        code_in = carve(4 * QC, 0).bitcast(U8).rearrange("p (r k c) -> p r k c", r=4, k=GB)
        decay = carve(4 * QC).bitcast(I16).rearrange("p (t k c) -> p t k c", t=2, k=GB)
        support = carve(NB * F).rearrange("p (b f) -> p b f", f=F)
        assert at[0] <= 2048 * 2 + 4096 + CB * 8 * F + CB * (6 * F + 2)
        h2T = carve(2 * QC, at[0] + 4096)[0:F, :].rearrange("p (t c) -> p t c", t=2)

        UT = carve(N, 0)[0:F + 2, :]
        VT = carve(N)[0:F + 2, :]
        aggT = carve(N)[0:F + 1, :]
        near = carve(4 * QC).rearrange("p (u c) -> p u c", u=4)
        both = carve(4 * QC).rearrange("p (u c) -> p u c", u=4)
        scale = carve(4 * QC).rearrange("p (u c) -> p u c", u=4)
        denom = carve(2 * QC).rearrange("p (u c) -> p u c", u=2)
        U = carve(NB * (F + 2), at[0] - 14 * QC).rearrange("p (b f) -> p b f", f=F + 2)
        V_ = carve(NB * (F + 2)).rearrange("p (b f) -> p b f", f=F + 2)
        moveT = carve(2 * QC, at[0])[0:F, :].rearrange("p (t c) -> p t c", t=2)
        stage_m = Y[:].rearrange("p b f -> p (b f)")[:, 0:2 * CB * (F + 1)].rearrange(
            "p (t c f) -> p t c f", t=2, c=CB)
        mirror_f = turn_in[:].rearrange("p (h c) -> p h c", h=2)

        split_rest = [Y[:], support]

        def own_blocks(slot, s):
            first = slot[:, 0, s * GB * P:(s * GB + 1) * P]
            return bass.AP(first.tensor, first.offset, [first.ap[0], (QC + P, GB), (1, P)])

        ROUND = 2 * CB
        UNITS = NQ * ROUND + 2 * CB

        class Unit:
            def __init__(self, n, J, I, k, off, direct_load, mirror_load, quad, offs, adds, free, targets_buffer=0,
                         targets_free=None):
                self.n = n
                self.J, self.I = J, I
                self.k = k
                self.off = off
                self.direct_load = direct_load
                self.mirror_load = mirror_load
                self.quad = quad
                self.offs = offs
                self.adds = adds
                self.free = free
                self.targets_buffer = targets_buffer
                self.targets_free = targets_free

            def has(self, back):
                return not isinstance(self.n, int) or self.n >= back

            def has_off(self, back):
                return not isinstance(self.offs, int) or self.offs >= back

        def round_unit(J, u):
            if u < 0:
                J, u = J - 1, u + ROUND
            off = u >= CB
            I = ((J + 1) % NQ if off else J)
            free = (J * 4 + 1, J * 4) if off else (J * 4 - 1, None)
            return Unit(J * ROUND + u, J, I, u % CB, off, J * 2 + int(off), J, J * 4 + u // GB,
                        J * CB + (u - CB) if off else None, J * 4, free, 0, J * CB)

        def tail_unit(n):
            if n < NQ * ROUND:
                return round_unit(NQ - 1, n - (NQ - 1) * ROUND)
            if n >= UNITS:
                return None
            J, k = divmod(n - NQ * ROUND, CB)
            adds = 4 * NQ - 1 + 3 * J
            return Unit(n, J, J + 2, k, True, 2 * NQ + J, NQ + J, n // GB, NQ * CB + J * CB + k, adds,
                        (adds, adds + 1), 1 - J, NQ * CB)

        ADDS = 4 * NQ + 6
        DEPTH = 4

        def run_units(eng, step):
            for t in range(ROUND):
                step(lambda lag, t=t: round_unit(0, t - lag) if t >= lag else None)
            with eng.Fori(1, NQ) as J:
                for t in range(ROUND):
                    step(lambda lag, t=t: round_unit(J, t - lag))
            for t in range(NQ * ROUND, UNITS + DEPTH):
                step(lambda lag, t=t: tail_unit(t - lag))

        def quarters(eng, work, settle=None):
            work(0, True)
            with eng.Fori(1, NQ) as q:
                work(q, False)
            if settle:
                settle()

        block = ctx.enter_context(nc.Block())

        loaded = [sem(f"loaded{r}") for r in range(RING)]
        ring_used = sem("ring_used")
        load_turns = sem("load_turns")
        stage_turns = sem("stage_turns")
        turn_turns = sem("turn_turns")
        consts_in = sem("consts_in")
        x_in = sem("x_in")
        pool_steps = sem("pool_steps")
        consts_made = sem("consts_made")
        weights_made = sem("weights_made")
        first_ready = sem("first_ready")
        first_read = sem("first_read")
        staged = [sem(f"staged{p}") for p in range(3)]
        signs_ready = [sem(f"signs_ready{p}") for p in range(2)]
        dve_signs = [sem(f"dve_signs{p}") for p in range(2)]
        rank_ready = sem("rank_ready")
        codes_made = sem("codes_made")
        codes_stored = [sem(f"codes_stored{t}") for t in range(2)]
        product_ready = [sem(f"product_ready{p}") for p in range(3)]
        product_copied = [sem(f"product_copied{p}") for p in range(3)]
        turned = [sem(f"turned{p}") for p in range(3)]
        turn_read = [sem(f"turn_read{p}") for p in range(3)]
        counts_copied = sem("counts_copied")
        counts_turned = sem("counts_turned")
        counts_read = sem("counts_read")
        turn_steps = [sem(f"turn_steps{p}") for p in range(3)]
        norm_steps = [sem(f"norm_steps{l}") for l in range(4)]
        norm_root = [sem(f"norm_root{l}") for l in range(4)]
        normed = [sem(f"normed{l}") for l in range(4)]
        out_stored = sem("out_stored")
        row_steps = sem("row_steps")
        row_ready = sem("row_ready")
        rows_turned = sem("rows_turned")
        rows_read = sem("rows_read")
        gat_ready = sem("gat_ready")
        parts_steps = [sem(f"parts_steps{l}") for l in (1, 2)]
        parts_act = [sem(f"parts_act{l}") for l in (1, 2)]
        parts_ready = [sem(f"parts_ready{l}") for l in (1, 2)]
        staged_parts = [sem(f"staged_parts{l}") for l in (1, 2)]
        diag_cut = sem("diag_cut")
        diag_steps = sem("diag_steps")
        negs_made = sem("negs_made")
        rect_ready = sem("rect_ready")
        pair_used = sem("pair_used")
        sums_copied = sem("sums_copied")
        x_q_ready = sem("x_q_ready")
        hT_ready = sem("hT_ready")
        hT_copied = sem("hT_copied")
        hid_ready = sem("hid_ready")
        att_ready = sem("att_ready")
        hid_read = sem("hid_read")
        att_read = sem("att_read")
        gate_steps = sem("gate_steps")
        gate_act = sem("gate_act")
        layer1_sum = sem("layer1_sum")
        code_loaded = [sem(f"code_loaded{r}") for r in range(4)]
        decay_used = sem("decay_used")
        decay_dve = sem("decay_dve")
        decay_act = sem("decay_act")
        h2T_ready = sem("h2T_ready")
        h2T_copied = sem("h2T_copied")
        support_ready = sem("support_ready")
        support_read = sem("support_read")
        sum2_copied = sem("sum2_copied")
        sum2_turned = sem("sum2_turned")
        sum2_read = sem("sum2_read")
        ext_steps = sem("ext_steps")
        ext_ready = sem("ext_ready")
        uv_ready = sem("uv_ready")
        uv_copied = sem("uv_copied")
        staged_rows = sem("staged_rows")
        staged_mirror = sem("staged_mirror")
        staged_stat = sem("staged_stat")
        dist_ready = sem("dist_ready")
        clamped = sem("clamped")
        logs_made = sem("logs_made")
        log_pairs = sem("log_pairs")
        norms_made = sem("norms_made")
        clipped = sem("clipped")
        halves_made = sem("halves_made")
        atanh_made = sem("atanh_made")
        atanh_diag = sem("atanh_diag")
        g_made = sem("g_made")
        weighted = sem("weighted")
        g_turned = sem("g_turned")
        mirror_weighted = sem("mirror_weighted")
        gathered = sem("gathered")
        mirrored = sem("mirrored")
        agg_added = sem("agg_added")
        plus_made = sem("plus_made")
        agg_turned = sem("agg_turned")
        agg_read = sem("agg_read")
        tail_steps = sem("tail_steps")
        tail_act = sem("tail_act")
        moveT_ready = sem("moveT_ready")
        moveT_copied = sem("moveT_copied")
        moved_ready = sem("moved_ready")

        N_PUTS = 19
        G_SCORES = 10
        G_SUMS = 22
        G_NEW = 25
        GATE_STEPS = 30
        TAIL_NORM = NQ + 2
        TAIL_AGG = 12

        def source_group(p, q, s):
            if p == 0:
                return NS - 1 - s
            if p in (1, 3):
                return (q * 2 + s) % NS
            return s

        def block_order(p):
            return (3, 2, 1, 0) if p == 0 else (0, 1, 2, 3)

        @block.sync
        def _(sp):
            for credited in (*turn_read, *turned, counts_turned, layer1_sum, att_ready, sum2_turned, sum2_read):
                sp.sem_inc(credited, 1)

            def load(p, q, s):
                r = s % RING
                g = source_group(p, q, s)
                src = adj_slots[:, bass.ds(g, 1), :, bass.ds(q, 1), :].rearrange("p a k b c -> p (a k) (b c)")
                sp.dma_start(ring[:, r], src).then_inc(loaded[r], 16)

            def wait_then_load(p, q, s, used, value):
                sp.wait_ge(used, value)
                if not isinstance(q, int):
                    sp.sem_inc(load_turns, 1)
                load(p, q, s)

            load(0, 0, 0)
            sp.dma_start(xT_sb, xT).then_inc(x_in, 16)
            sp.wait_ge(x_in, 32)
            sp.wait_ge(consts_in, N_PUTS * 16)
            for s in range(1, RING):
                load(0, 0, s)
            for s in range(RING, NS):
                wait_then_load(0, 0, s, ring_used, s - RING + 1)
            with sp.Fori(1, NQ) as q:
                for s in range(NS):
                    wait_then_load(0, q, s, ring_used, q * NS + (s - RING + 1))
            for p in (1, 2):
                with sp.Fori(0, NQ) as q:
                    for s in range(NS):
                        wait_then_load(p, q, s, ring_used, q * NS + (p * SLOTS + s - RING + 1))
            for s in range(NS):
                if s < RING:
                    wait_then_load(3, 0, s, ring_used, 3 * SLOTS + s - RING + 1)
                else:
                    wait_then_load(3, 0, s, pair_used, 2 + 2 * (s - RING + 1))
            with sp.Fori(1, NQ) as q:
                for s in range(NS):
                    wait_then_load(3, q, s, pair_used, q * (2 * NS) + (2 + 2 * (s - RING + 1)))
            for t in range(2):
                sp.wait_ge(codes_stored[t], NQ * NS // 2 * 16)
            sp.wait_ge(normed[1], 1)

            def load_codes(q, s):
                r = s % RING
                src = codes_dram[bass.ds(q * NS + s, 1)].rearrange("a p n -> p (a n)")
                sp.dma_start(code_in[:, r].rearrange("p k c -> p (k c)"), src).then_inc(code_loaded[r], 16)

            for s in range(NS):
                if s >= RING:
                    sp.wait_ge(decay_dve, s - RING + 1)
                    sp.wait_ge(decay_act, s - RING + 1)
                load_codes(0, s)
            with sp.Fori(1, NQ) as q:
                for s in range(NS):
                    sp.wait_ge(decay_dve, q * NS + (s - RING + 1))
                    sp.wait_ge(decay_act, q * NS + (s - RING + 1))
                    sp.sem_inc(load_turns, 1)
                    load_codes(q, s)
            def load_pair(J, I, r):
                rows, cols = (J, I) if r < 2 else (I, J)
                src = adj_slots[:, bass.ds(rows * 2 + r % 2, 1), :, bass.ds(cols, 1), :].rearrange(
                    "p a k b c -> p (a k) (b c)")
                sp.dma_start(ring[:, r], src).then_inc(loaded[r], 16)

            for r in (0, 1):
                sp.wait_ge(pair_used, 2 + 2 * (SLOTS - RING + r + 1))
                load_pair(0, 0, r)
            for r in (2, 3):
                sp.wait_ge(pair_used, 2 + 2 * (SLOTS - RING + r + 1))
                load_pair(0, 1, r)
            for r in (0, 1):
                sp.wait_ge(gathered, GB * (r + 1))
                load_pair(0, 1, r)
            with sp.Fori(1, NQ) as J:
                for r in (0, 1):
                    sp.wait_ge(gathered, J * ROUND + (GB * (r + 1) - CB))
                    sp.sem_inc(load_turns, 1)
                    load_pair(J, J, r)
                for r in (2, 3):
                    sp.wait_ge(mirror_weighted, J * (2 * CB) + (r - 3))
                    sp.sem_inc(load_turns, 1)
                    load_pair(J, (J + 1) % NQ, r)
                for r in (0, 1):
                    sp.wait_ge(gathered, J * ROUND + GB * (r + 1))
                    sp.sem_inc(load_turns, 1)
                    load_pair(J, (J + 1) % NQ, r)
            for J in range(2):
                base = NQ * ROUND + J * CB
                for r in (0, 2, 3, 1):
                    if r < 2:
                        sp.wait_ge(gathered, base - CB + GB * (r + 1))
                    else:
                        sp.wait_ge(mirror_weighted, (NQ + J) * 2 * CB + (r - 3))
                    load_pair(J, J + 2, r)

        @block.gpsimd
        def _(pool):
            steps = [0]

            def step(ins):
                steps[0] += 1
                ins.then_inc(pool_steps, 1)
                pool.wait_ge(pool_steps, steps[0])

            def diagonal(ap, base, fill, width):
                step(nc.gpsimd.affine_select(out=ap, in_=ap, compare_op=ALU.not_equal, fill=fill, base=base,
                                             pattern=[[-1, width]], channel_multiplier=1))

            step(nc.gpsimd.memset(ident[:], 0.0))
            diagonal(ident[:], 0, 1.0, P)
            step(nc.gpsimd.memset(offdiag[:], 1.0))
            diagonal(offdiag[:], 0, 0.0, P)
            step(nc.gpsimd.memset(offdiag_b[:], 1.0))
            diagonal(offdiag_b[:], 0, 0.0, P)
            step(nc.gpsimd.memset(fold[:], 0.0))
            diagonal(fold[:], 0, 1.0, F)
            diagonal(fold[:], -F, 1.0, F)
            step(nc.gpsimd.memset(minus_ones[:], -1.0))
            step(nc.gpsimd.memset(ones[:], 1.0))
            step(nc.gpsimd.memset(ones_f[:], 1.0))
            step(nc.gpsimd.memset(code_bias[:], MAX_NEIGH - CODE_BIAS))
            step(nc.gpsimd.memset(later_or_self[:], -1.0))
            step(nc.gpsimd.affine_select(out=later_or_self[:], in_=later_or_self[:], compare_op=ALU.is_gt, fill=0.0,
                                         base=0, pattern=[[-1, P]], channel_multiplier=1))
            diagonal(later_or_self[:], 0, CODE_BIAS, P)
            step(nc.gpsimd.memset(minus_two[0:F], -2.0))
            step(nc.gpsimd.memset(minus_two[F:P], 1.0))
            pool.sem_inc(consts_made, 1)

            def stage(p, src, done):
                def work(q, first):
                    for s in range(NS):
                        g = source_group(p, q, s)
                        if not (first and p == 0 and s < 2):
                            pool.wait_ge(ring_used, p * SLOTS + q * NS + s - 1)
                        pool.sem_inc(stage_turns, 1)
                        nc.gpsimd.tensor_copy(stage_f[:, s % 2, :, 0:F],
                                              src[:, bass.ds(g * GB, GB), :]).then_inc(done, 1)
                quarters(pool, work)

            pool.wait_ge(x_in, 32)
            stage(0, X, staged[0])
            pool.wait_ge(turn_read[0], NQ + 1)
            stage(1, T1, staged[1])
            pool.wait_ge(turn_read[1], NQ + 1)
            stage(2, T2, staged[2])

            pool.wait_ge(parts_ready[0], 1)
            def stage_x(n):
                pool.wait_ge(layer1_sum, n)
                pool.sem_inc(stage_turns, 1)
                nc.gpsimd.tensor_copy(x_q, X[:, bass.ds((n - 1) * CB, CB), :]).then_inc(x_q_ready, 1)

            def work(q, first):
                for s in range(NS):
                    g = source_group(3, q, s)
                    if not (first and s == 0):
                        pool.wait_ge(pair_used, q * (2 * NS) + 2 * s)
                    pool.sem_inc(stage_turns, 1)
                    nc.gpsimd.tensor_copy(stage_f[:, s % 2, :, 0:F],
                                          X[:, bass.ds(g * GB, GB), :]).then_inc(staged_parts[0], 1)
                    nc.gpsimd.tensor_copy(stage_b[:, s % 2], parts[:, bass.ds(g * GB, GB), :]).then_inc(
                        staged_parts[0], 1)
                    if s == 1 and not first:
                        stage_x(q)
            quarters(pool, work, lambda: stage_x(NQ))

            pool.wait_ge(parts_ready[1], 1)
            def work(q, first):
                for s in range(NS):
                    if not (first and s < 2):
                        pool.wait_ge(decay_used, q * NS + s - 1)
                    pool.sem_inc(stage_turns, 1)
                    nc.gpsimd.tensor_copy(stage_b[:, s % 2], parts[:, s * GB:(s + 1) * GB, :]).then_inc(
                        staged_parts[1], 1)
            quarters(pool, work)

            pool.wait_ge(ext_ready, 1)
            norm_plus = stats[:, 8, :]

            def unit_step(at):
                u = at(0)
                if u:
                    if u.k % GB == 0:
                        if u.has(2 * GB):
                            pool.wait_ge(gathered, (u.quad - 1) * GB)
                            pool.sem_inc(stage_turns, 1)
                        t = u.k // GB
                        blocks = bass.ds(u.J * CB + u.k, GB)
                        nc.gpsimd.tensor_copy(stage_f[:, t, :, 0:F], X[:, blocks, :]).then_inc(staged_rows, 1)
                        nc.gpsimd.tensor_copy(stage_f[:, t, :, F], norm_plus[:, blocks]).then_inc(staged_rows, 1)
                    if u.off and u.k == 0:
                        m = u.targets_buffer
                        if not m and u.has_off(1):
                            pool.wait_ge(mirrored, 2 * u.targets_free)
                            pool.sem_inc(stage_turns, 1)
                        blocks = bass.ds(u.I * CB, CB)
                        nc.gpsimd.tensor_copy(stage_m[:, m, :, 0:F], X[:, blocks, :]).then_inc(staged_mirror, 1)
                        nc.gpsimd.tensor_copy(stage_m[:, m, :, F], norm_plus[:, blocks]).then_inc(staged_mirror, 1)
                    pool.wait_ge(logs_made, u.n + 1)
                    if u.has(4):
                        v = at(4)
                        pool.wait_ge(weighted, v.n + 1)
                        if v.off:
                            pool.wait_ge(g_turned, v.offs * 2 + 2)
                    lq, ld = near[:, u.k % 4], denom[:, u.k % 2]
                    nc.gpsimd.tensor_tensor(both[:, u.k % 4], lq, ld, ALU.subtract).then_inc(log_pairs, 1)
                    nc.gpsimd.tensor_tensor(scale[:, u.k % 4], lq, ld, ALU.add).then_inc(log_pairs, 1)
                v = at(1)
                if v and v.off:
                    pool.wait_ge(halves_made, v.n + 1)
                    nc.gpsimd.tensor_tensor(near[:, v.k % 4], near[:, v.k % 4], both[:, v.k % 4],
                                            ALU.subtract).then_inc(atanh_made, 1)

            run_units(pool, unit_step)

        @block.tensor
        def _(pe):
            pe.wait_ge(weights_made, 1)
            pe.wait_ge(x_in, 32)
            for n in range(4):
                for c in range(8):
                    b = n * 8 + c
                    mm = nc.tensor.matmul(ps[:, n, c * F:(c + 1) * F], xT_sb[:, b * P:(b + 1) * P], w_first[:],
                                          start=True, stop=True)
                mm.then_inc(first_ready, 1)
            nc.tensor.matmul(ps[:, 4, 0:2], gatWT_sb[:], gat_a_sb[:], start=True, stop=True)
            nc.tensor.matmul(ps[:, 5, 0:3 * F], gatWT_sb[:], winT_sb[:], start=True, stop=True).then_inc(gat_ready, 1)
            pe.wait_ge(first_read, 5)

            def rank(q, s, j, k):
                pe.wait_ge(signs_ready[0], q * (GB * NS) + (s * GB + j + 1))
                for h in range(2):
                    cols = slice(h * HALF, (h + 1) * HALF)
                    pe.wait_ge(codes_made, q * (2 * GB * NS) + ((s * GB + j) * 2 + h))
                    nc.tensor.matmul(ps[:, 6 + h, :], later_or_self[:], mask[:, s % 2, k, cols],
                                     start=True, stop=False)
                    nc.tensor.matmul(ps[:, 6 + h, :], minus_ones[:], later[:, s % 2, j, cols],
                                     start=False, stop=True).then_inc(rank_ready, 1)

            def count(q, s, k):
                for h in range(2):
                    cols = slice(h * HALF, (h + 1) * HALF)
                    st, sp_ = s == 0 and k == 0, s == NS - 1 and k == GB - 1
                    nc.tensor.matmul(ps[0:32, 6 + h, :], ones[:], mask[:, s % 2, k, cols], start=st, stop=sp_)
                    nc.tensor.matmul(ps[32:64, 6 + h, :], ones[:], later[:, s % 2, k, cols], start=st, stop=sp_)

            def turn(p, n):
                pe.wait_ge(product_copied[p], n * 2)
                pe.wait_ge(turn_read[p], n)
                if p:
                    pe.wait_ge(turn_read[p - 1], NQ + 1)
                for c in range(CB):
                    mm = nc.tensor.matmul(ps[:, 4 + c // 4, (c % 4) * P:(c % 4 + 1) * P],
                                          turn_in[:, c * P:(c + 1) * P], turn_w[:, p, :], start=True, stop=True)
                mm.then_inc(turned[p], 1)
                if p == 1:
                    pe.wait_ge(counts_copied, n)
                    for c in range(CB):
                        mm = nc.tensor.matmul(ps[:, 2, 2 * c:2 * c + 2], count_in[:, c * P:(c + 1) * P],
                                              ident[0:F, 0:F:32], start=True, stop=True)
                    mm.then_inc(counts_turned, 1)
                if p == 2:
                    pe.wait_ge(row_ready, n)
                    for c in range(CB):
                        mm = nc.tensor.matmul(ps[:, 2, c:c + 1], row_out[:, c * P:(c + 1) * P], ones_f[:],
                                              start=True, stop=True)
                    mm.then_inc(rows_turned, 1)

            for p in range(3):
                def work(q, first):
                    for s in range(NS):
                        r, t = s % RING, s % 2
                        pe.wait_ge(loaded[r], (q * 2 + (p * 8 + s // RING + 1)) * 16)
                        pe.wait_ge(staged[p], q * NS + s + 1)
                        if p == 1:
                            pe.wait_ge(signs_ready[1], q * NS + s + 1)
                            if s == 0 and not first:
                                pe.wait_ge(counts_copied, q)
                        order = block_order(p)
                        for i in range(GB):
                            if p == 0:
                                rank(q, s, i, order[i])
                            if p == 1:
                                count(q, s, i)
                            if p == 2 and i == 2:
                                pe.wait_ge(row_steps, q * (GB * NS) + GB * (s + 1))
                            if s == 0 and i == 0 and not first:
                                pe.wait_ge(product_copied[p], q * 2)
                            pair, h = i // 2, i % 2
                            ka, kb = order[2 * pair:2 * pair + 2]
                            start, stop = s == 0 and pair == 0, s == NS - 1 and pair == 1
                            cols = slice(h * HALF, (h + 1) * HALF)
                            nc.tensor.matmul(ps[0:F, h, :], stage_f[:, t, ka, 0:F], ring[:, r, ka, cols],
                                             start=start, stop=stop)
                            mm = nc.tensor.matmul(ps[F:2 * F, h, :], stage_f[:, t, kb, 0:F], ring[:, r, kb, cols],
                                                  start=start, stop=stop)
                        mm.then_inc(ring_used, 1)
                        if s == 1 and not first:
                            turn(p, q)
                quarters(pe, work, lambda: turn(p, NQ))

            pe.sem_inc(pair_used, 2)
            pe.wait_ge(turn_read[2], NQ + 1)
            pe.wait_ge(rows_read, NQ)

            def project(n):
                pe.wait_ge(x_q_ready, n)
                pe.wait_ge(sums_copied, n * 4)
                pe.sem_inc(turn_turns, 1)
                for c in range(CB):
                    mm = nc.tensor.transpose(ps[0:F, 4 + c // 4, (c % 4) * P:(c % 4 + 1) * P], x_q[:, c, :], ident[:])
                mm.then_inc(hT_ready, 1)
                pe.wait_ge(hT_copied, n)
                for c in range(CB):
                    a, b = 4 + 2 * (c % 2), 5 + 2 * (c % 2)
                    cols = slice(c * P, (c + 1) * P)
                    if c >= 2:
                        pe.wait_ge(hid_read, (n - 1) * CB + (c - 1))
                        pe.wait_ge(att_read, (n - 1) * CB + (c - 1))
                    nc.tensor.matmul(ps[:, a, :], hT[:, cols], w_hid[:].rearrange("p g n -> p (g n)"),
                                     start=True, stop=False)
                    nc.tensor.matmul(ps[:, a, 0:3 * F], turn_in[:, cols], w_edge[:], start=False, stop=True).then_inc(
                        hid_ready, 1)
                    nc.tensor.matmul(ps[:, b, 0:6 * F], weighted_in[:, cols], w_att[:], start=True, stop=True)
                    nc.tensor.matmul(ps[:, b, 6 * F:6 * F + 2], turn_in[:, cols], w_score[:],
                                     start=True, stop=True).then_inc(att_ready, 1)

            def work(q, first):
                for s in range(NS):
                    r, t = s % RING, s % 2
                    pe.wait_ge(staged_parts[0], q * (2 * NS) + 2 * (s + 1))
                    for pair in range(2):
                        pe.wait_ge(rect_ready, q * (2 * NS) + (2 * s + pair + 1))
                        if s == 0 and pair == 0 and not first:
                            pe.wait_ge(sums_copied, q * 4)
                        for i in range(2):
                            k = 2 * pair + i
                            start = s == 0 and k == 0
                            stop = s == NS - 1 and k == GB - 1
                            for h in range(2):
                                cols = slice(h * HALF, (h + 1) * HALF)
                                nc.tensor.matmul(ps[0:F, h, :], stage_f[:, t, k, 0:F], ring[:, r, k, cols],
                                                 start=start, stop=stop)
                                nc.tensor.matmul(ps[F:P, h, :], stage_f[:, t, k, 0:F], negs[:, pair, i, cols],
                                                 start=start, stop=stop)
                                for m in range(3):
                                    part = stage_b[:, t, k, m * F:(m + 1) * F]
                                    nc.tensor.matmul(ps[0:F, 2 + h, :], part, more[:, pair, i, cols],
                                                     start=start and m == 0, stop=stop and m == 2)
                                    mm = nc.tensor.matmul(ps[F:P, 2 + h, :], part, less[:, pair, i, cols],
                                                          start=start and m == 0, stop=stop and m == 2)
                        mm.then_inc(pair_used, 1)
                    if s == 1 and not first:
                        project(q)

            quarters(pe, work, lambda: project(NQ))

            pe.wait_ge(normed[1], 1)
            pe.wait_ge(hid_read, NB)
            pe.wait_ge(att_read, NB)
            for n in range(NQ):
                if n >= 2:
                    pe.wait_ge(h2T_copied, n - 1)
                for c in range(CB):
                    bank = 2 * (n % 2) + c // 4
                    mm = nc.tensor.transpose(ps[0:F, bank, (c % 4) * P:(c % 4 + 1) * P], X[:, n * CB + c, :], ident[:])
                mm.then_inc(h2T_ready, 1)
                pe.wait_ge(h2T_copied, n + 1)
                for c in range(CB):
                    mm = nc.tensor.matmul(ps[:, 4 + n, c * F:(c + 1) * F], h2T[:, n % 2, c * P:(c + 1) * P], w2_sb[:],
                                          start=True, stop=True)
                mm.then_inc(support_ready, 1)
            pe.wait_ge(support_read, NQ)
            def fold_sums(n):
                pe.wait_ge(sum2_copied, n * 2)
                pe.wait_ge(sum2_read, n)
                for c in range(CB):
                    mm = nc.tensor.matmul(ps[:, 4, c * F:(c + 1) * F], turn_in[:, c * P:(c + 1) * P], fold[:],
                                          start=True, stop=True)
                mm.then_inc(sum2_turned, 1)

            def work(q, first):
                for s in range(NS):
                    t = s % 2
                    pe.wait_ge(staged_parts[1], q * NS + s + 1)
                    pe.wait_ge(decay_dve, q * NS + s + 1)
                    pe.wait_ge(decay_act, q * NS + s + 1)
                    if s == 0 and not first:
                        pe.wait_ge(sum2_copied, q * 2)
                    for k in range(GB):
                        for h in range(2):
                            w = decay[:, t, k, h * HALF:(h + 1) * HALF].bitcast(BF16)
                            nc.tensor.matmul(ps[:, h, :], stage_b[:, t, k, 0:2 * F], w,
                                             start=s == 0 and k == 0, stop=False)
                    for k in (0, 2):
                        for h in range(2):
                            for i in range(2):
                                w = decay[:, t, k + i, h * HALF:(h + 1) * HALF].bitcast(BF16)
                                mm = nc.tensor.matmul(ps[i * F:(i + 1) * F, h, :], stage_b[:, t, k + i, 2 * F:3 * F], w,
                                                      start=False, stop=s == NS - 1 and k == 2)
                    mm.then_inc(decay_used, 1)
                    if s == 1 and not first:
                        fold_sums(q)

            quarters(pe, work, lambda: fold_sums(NQ))

            pe.wait_ge(ext_ready, 1)
            pe.wait_ge(sum2_read, NQ + 1)
            for n in range(2 * NQ):
                src = (U, V_)[n % 2]
                if n >= 2:
                    pe.wait_ge(uv_copied, n - 1)
                for c in range(CB):
                    bank = 2 * (n % 2) + c // 4
                    mm = nc.tensor.transpose(ps[0:F + 2, bank, (c % 4) * P:(c % 4 + 1) * P],
                                             src[:, n // 2 * CB + c, :], ident[:])
                mm.then_inc(uv_ready, 1)
            pe.wait_ge(uv_copied, 2 * NQ)

            def mirror_products(v, h):
                for c in range(GB):
                    mm = nc.tensor.matmul(ps[0:F + 1, 7, v.k % GB * P:(v.k % GB + 1) * P],
                                          stage_m[:, v.targets_buffer, h * GB + c, :],
                                          mirror_f[:, h, c * P:(c + 1) * P],
                                          start=h == 0 and c == 0, stop=h == 1 and c == GB - 1)
                mm.then_inc(mirrored, 1)

            def turn_g(v, h):
                pe.sem_inc(turn_turns, 1)
                for c in range(GB):
                    mm = nc.tensor.transpose(ps[:, 6, c * P:(c + 1) * P],
                                             both[:, v.k % 4, (h * GB + c) * P:(h * GB + c + 1) * P], ident[:])
                mm.then_inc(g_turned, 1)

            def unit_step(at):
                u = at(0)
                if u:
                    if u.k % GB == 0:
                        pe.wait_ge(staged_stat, u.quad + 1)
                    t = u.k // GB
                    for h in range(2):
                        cols = bass.ds(u.I * QC + h * HALF, HALF)
                        if h == 0 and u.has(1):
                            pe.wait_ge(clamped, 2 * u.n - 1)
                        mm = nc.tensor.matmul(ps[:, h, :], stat[:, t, u.k % GB * P:(u.k % GB + 1) * P], VT[:, cols],
                                              start=True, stop=True)
                    mm.then_inc(dist_ready, 1)
                    for h in range(2):
                        cols = bass.ds(u.I * QC + h * HALF, HALF)
                        if h == 0 and u.has(1):
                            pe.wait_ge(clamped, 2 * u.n)
                        mm = nc.tensor.matmul(ps[:, 2 + h, :], stat[:, t, u.k % GB * P:(u.k % GB + 1) * P],
                                              UT[:, cols], start=True, stop=True)
                    mm.then_inc(dist_ready, 1)
                v = at(4)
                if v and v.off:
                    pe.wait_ge(mirror_weighted, v.offs * 2 + 2)
                    mirror_products(v, 1)
                v = at(3)
                if v and v.off:
                    pe.wait_ge(g_made, v.n + 1)
                    if v.has_off(1):
                        pe.wait_ge(mirror_weighted, v.offs * 2)
                    turn_g(v, 0)
                if v:
                    pe.wait_ge(weighted, v.n + 1)
                    if v.k % GB == 0:
                        pe.wait_ge(staged_rows, 2 * (v.quad + 1))
                    if v.k == 0 and v.has(1):
                        pe.wait_ge(agg_added, v.free[0])
                    for h in range(2):
                        mm = nc.tensor.matmul(ps[0:F + 1, 4 + h, :], stage_f[:, v.k // GB, v.k % GB, :],
                                              ring[:, v.k // GB, v.k % GB, h * HALF:(h + 1) * HALF],
                                              start=v.k == 0, stop=v.k == CB - 1)
                    mm.then_inc(gathered, 1)
                if v and v.off:
                    pe.wait_ge(mirror_weighted, v.offs * 2 + 1)
                    turn_g(v, 1)
                    if v.k == 0:
                        pe.wait_ge(staged_mirror, 2 * (v.mirror_load + 1))
                        if v.has_off(1):
                            pe.wait_ge(agg_added, v.free[1])
                    elif v.k == GB:
                        pe.wait_ge(agg_added, v.adds + 2)
                    mirror_products(v, 0)

            run_units(pe, unit_step)
            pe.wait_ge(agg_added, ADDS)
            for b in range(NB):
                mm = nc.tensor.matmul(ps[:, b // GB, b % GB * (F + 1):(b % GB + 1) * (F + 1)],
                                      aggT[:, b * P:(b + 1) * P], ident[0:F + 1, 0:F + 1], start=True, stop=True)
            mm.then_inc(agg_turned, 1)
            pe.wait_ge(tail_steps, TAIL_AGG)
            for n in range(NQ):
                if n >= 2:
                    pe.wait_ge(moveT_copied, n - 1)
                for c in range(CB):
                    bank = 2 * (n % 2) + c // 4
                    mm = nc.tensor.transpose(ps[0:F, bank, (c % 4) * P:(c % 4 + 1) * P], Y[:, n * CB + c, :], ident[:])
                mm.then_inc(moveT_ready, 1)
                pe.wait_ge(moveT_copied, n + 1)
                for c in range(CB):
                    mm = nc.tensor.matmul(ps[:, 4 + n, c * F:(c + 1) * F], moveT[:, n % 2, c * P:(c + 1) * P],
                                          w3_sb[0:F, :], start=True, stop=True)
                mm.then_inc(moved_ready, 1)

        def copy_product(act, p, n):
            act.wait_ge(ring_used, n * NS + p * SLOTS)
            act.wait_ge(turned[p], n)
            nc.scalar.activation(turn_in[:, HALF:QC], ps[:, 1, :], ACT.Copy).then_inc(product_copied[p], 1)

        def split_act(act, i, src, scale):
            for m in range(3):
                act.wait_ge(parts_steps[i], m)
                if m == 0:
                    act.wait_ge(normed[i], 1)
                rest = src[:] if m == 0 else split_rest[i]
                nc.scalar.activation(parts[:, :, m * F:(m + 1) * F], rest, ACT.Copy).then_inc(parts_act[i], 1)

        def norm_act(act, l):
            act.wait_ge(norm_steps[l], 6)
            nc.scalar.activation(stats[:, 4, :], stats[:, 3, :], ACT.Sqrt).then_inc(norm_root[l], 1)

        @block.scalar
        def _(act):
            def put(dst, src):
                act.dma_start(dst, src).then_inc(consts_in, 16)

            act.dma_start(X[:], x).then_inc(x_in, 16)
            cheb = cheb_w.rearrange("k i o -> i k o")
            put(cheb_sb[0:F], cheb)
            put(cheb_sb[F:P], cheb)
            put(gatWT_sb[:, 0:F], gatWT)
            put(gatWT_sb[:, F:2 * F], gatWT)
            put(gat_a_sb[:], gat_a2)
            put(winT_sb[:], winT)
            put(w_edge[:], wieT)
            for g, (wT, b_in, b_hid) in enumerate(((wheT, bie, bhe), (whnT, bin_, bhn))):
                put(w_hid[0:F, g, 0:2 * F], wT[:, 0:2 * F])
                put(w_hid[0:F, g, 3 * F:4 * F], wT[:, 2 * F:3 * F])
                put(bias_tmp[F:F + 1, 2 * g, :], b_in)
                put(bias_tmp[F:F + 1, 2 * g + 1, :], b_hid)
            put(w2_sb[:], w2)
            put(w3_sb[0:F, :], w3)
            put(b2_sb[:], b2.broadcast_to([P, F]))
            put(b3_sb[:], b3.broadcast_to([P, F]))
            act.sem_inc(codes_made, 1)

            def code_work(q, first):
                for s in range(NS):
                    t = s % 2
                    if not (first and s < 2):
                        act.wait_ge(codes_stored[t], (q * (NS // 2) + s // 2) * 16)
                    for j, k in enumerate(block_order(0)):
                        if s == 0 and j == 1 and not first:
                            copy_product(act, 0, q)
                        for h in range(2):
                            act.wait_ge(rank_ready, q * (2 * GB * NS) + ((s * GB + j) * 2 + h + 1))
                            nc.scalar.activation(codes[:, t, k, h * HALF:(h + 1) * HALF], ps[:, 6 + h, :], ACT.Relu,
                                                 bias=code_bias[:], scale=1.0).then_inc(codes_made, 1)
                    act.wait_ge(codes_made, q * (2 * GB * NS) + ((s + 1) * GB * 2 + 1))
                    act.dma_start(codes_dram[bass.ds(q * NS + (NS - 1 - s), 1)].rearrange("a p n -> p (a n)"),
                                  codes[:, t].rearrange("p k c -> p (k c)")).then_inc(codes_stored[t], 16)

            quarters(act, code_work, lambda: copy_product(act, 0, NQ))
            act.wait_ge(codes_stored[0], NQ * NS // 2 * 16)
            act.wait_ge(codes_stored[1], NQ * NS // 2 * 16)
            with act.Fori(1, NQ + 1) as n:
                act.wait_ge(ring_used, n * NS + SLOTS)
                act.wait_ge(counts_turned, n)
                nc.scalar.activation(count_in, ps[0:F, 6:8, :], ACT.Copy).then_inc(counts_copied, 1)
                copy_product(act, 1, n)
            with act.Fori(1, NQ + 1) as n:
                copy_product(act, 2, n)
            norm_act(act, 0)

            split_act(act, 0, X, 1.0)
            act.preload_act_table_set("exp_and_others")

            def copy_sums(n):
                act.wait_ge(pair_used, n * (2 * NS) + 2)
                act.wait_ge(att_ready, (n - 1) * CB + 1)
                nc.scalar.activation(turn_in[:, HALF:QC], ps[:, 3, :], ACT.Copy).then_inc(sums_copied, 1)
                nc.scalar.activation(weighted_in[:, HALF:QC], ps[:, 1, :], ACT.Copy).then_inc(sums_copied, 1)

            def copy_hidden(n):
                act.wait_ge(hT_ready, n)
                nc.scalar.activation(hT[0:F, :], ps[0:F, 4:6, :], ACT.Copy).then_inc(hT_copied, 1)
                for c in range(CB):
                    act.wait_ge(hid_ready, (n - 1) * CB + (c + 1))
                    if c == 0:
                        act.wait_ge(layer1_sum, n)
                    nc.scalar.activation(hid[:, c].rearrange("p g n -> p (g n)"), ps[:, 4 + 2 * (c % 2), :],
                                         ACT.Copy).then_inc(hid_read, 1)

            def gate_part(n, i):
                if i == 0:
                    act.wait_ge(gate_steps, (n - 1) * GATE_STEPS + G_SCORES)
                    nc.scalar.activation(small[:, 4], small[:, 2], ACT.Exp).then_inc(gate_act, 1)
                    nc.scalar.activation(small[:, 5, :, 0], small[:, 3, :, 1], ACT.Exp).then_inc(gate_act, 1)
                if i == 1:
                    act.wait_ge(gate_steps, (n - 1) * GATE_STEPS + G_SUMS)
                    act.wait_ge(hid_read, n * CB)
                    rz = hid[:, :, :, 0:2 * F].rearrange("p c g n -> p (c g) n")
                    nc.scalar.activation(rz, rz, ACT.Tanh, scale=0.5).then_inc(gate_act, 1)
                if i == 2:
                    act.wait_ge(gate_steps, (n - 1) * GATE_STEPS + G_NEW)
                    nc.scalar.activation(gate[:], gate[:], ACT.Tanh).then_inc(gate_act, 1)

            def sign_work(q, first):
                for s in range(NS):
                    act.wait_ge(loaded[s % RING], (q * 2 + (24 + s // RING + 1)) * 16)
                    if s < 2:
                        act.wait_ge(diag_cut, q * 2 + s + 1)
                    for pair in range(2):
                        act.wait_ge(pair_used, q * (2 * NS) + (2 * s + pair + 1))
                        nc.scalar.activation(negs[:, pair], ring[:, s % RING, 2 * pair:2 * pair + 2, :], ACT.Relu,
                                             scale=-1.0).then_inc(negs_made, 1)
                        if s == 0 and pair == 0 and not first:
                            copy_sums(q)
                        if s == 2 and pair == 0 and not first:
                            copy_hidden(q)
                    if s in (4, 5, 6) and not first:
                        gate_part(q, s - 4)

            def settle():
                copy_sums(NQ)
                copy_hidden(NQ)
                for i in range(3):
                    gate_part(NQ, i)

            quarters(act, sign_work, settle)
            norm_act(act, 1)

            for n in range(NQ):
                act.wait_ge(h2T_ready, n + 1)
                if n >= 2:
                    act.wait_ge(support_ready, n - 1)
                nc.scalar.activation(h2T[:, n % 2, :], ps[0:F, 2 * (n % 2):2 * (n % 2) + 2, :], ACT.Copy).then_inc(
                    h2T_copied, 1)
                act.wait_ge(support_ready, n + 1)
                nc.scalar.activation(support[:, n * CB:(n + 1) * CB, :].rearrange("p c f -> p (c f)"), ps[:, 4 + n, :],
                                     ACT.Copy, scale=CODE_SCALE).then_inc(support_read, 1)
            act.wait_ge(support_read, NQ)
            split_act(act, 1, support, 1.0)

            def copy_sums2(n):
                act.wait_ge(decay_used, n * NS)
                act.wait_ge(sum2_turned, n)
                nc.scalar.activation(turn_in[:, HALF:QC], ps[:, 1, :], ACT.Copy).then_inc(sum2_copied, 1)

            def decay_work(q, first):
                for s in range(NS):
                    act.wait_ge(code_loaded[s % RING], (q * 2 + (s // RING + 1)) * 16)
                    if not (first and s < 2):
                        act.wait_ge(decay_used, q * NS + s - 1)
                    nc.scalar.activation(decay[:, s % 2, 3, :], code_in[:, s % RING, 3, :], ACT.Copy,
                                         scale=128.0).then_inc(decay_act, 1)
                    if s == 0 and not first:
                        copy_sums2(q)

            quarters(act, decay_work, lambda: copy_sums2(NQ))
            norm_act(act, 2)

            for n in range(2 * NQ):
                act.wait_ge(uv_ready, n + 1)
                dst = (UT, VT)[n % 2]
                nc.scalar.activation(dst[:, n // 2 * QC:(n // 2 + 1) * QC],
                                     ps[0:F + 2, 2 * (n % 2):2 * (n % 2) + 2, :], ACT.Copy).then_inc(uv_copied, 1)
            act.wait_ge(uv_copied, 2 * NQ)
            act.preload_act_table_set("natural_log_exp_and_others")

            def stage_stat(J, k):
                nc.scalar.activation(stat[:, k // GB, :], UT[:, bass.ds(J * QC + k * P, GB * P)], ACT.Copy,
                                     scale=minus_two[0:F + 2, :]).then_inc(staged_stat, 1)

            def unit_step(at):
                v = at(1)
                if v:
                    act.wait_ge(log_pairs, 2 * v.n + 1)
                    size, rest, a = both[:, v.k % 4], scale[:, v.k % 4], near[:, v.k % 4]
                    nc.scalar.activation(size, size, ACT.Exp, scale=0.5).then_inc(norms_made, 1)
                u = at(0)
                if u:
                    act.wait_ge(clamped, 2 * u.n + 1)
                    nc.scalar.activation(near[:, u.k % 4], near[:, u.k % 4], ACT.Ln)
                    act.wait_ge(clamped, 2 * u.n + 2)
                    nc.scalar.activation(denom[:, u.k % 2], denom[:, u.k % 2], ACT.Ln).then_inc(logs_made, 1)
                if v:
                    act.wait_ge(clipped, v.n + 1)
                    act.wait_ge(log_pairs, 2 * v.n + 2)
                    nc.scalar.activation(a, size, ACT.Ln, bias=1.0, scale=1.0).then_inc(plus_made, 1)
                    nc.scalar.activation(rest, rest, ACT.Exp, scale=-0.5)
                    act.wait_ge(plus_made, v.n + 1)
                    nc.scalar.activation(size, size, ACT.Ln, bias=1.0, scale=-1.0).then_inc(halves_made, 1)
                if u and u.k % GB == 1 and (u.k == 1 or not (isinstance(u.n, int) and u.n > UNITS - CB)):
                    if u.has(GB):
                        act.wait_ge(dist_ready, 2 * GB * u.quad)
                        act.sem_inc(stage_turns, 1)
                    if u.k == 1:
                        stage_stat(u.J, GB)
                    elif not u.off:
                        stage_stat(u.J, 0)
                    else:
                        stage_stat((u.J + 1) % NQ, 0)

            stage_stat(0, 0)
            run_units(act, unit_step)
            for n in range(NQ):
                act.wait_ge(moveT_ready, n + 1)
                if n >= 2:
                    act.wait_ge(moved_ready, n - 1)
                nc.scalar.activation(moveT[:, n % 2, :], ps[0:F, 2 * (n % 2):2 * (n % 2) + 2, :], ACT.Copy).then_inc(
                    moveT_copied, 1)
            act.wait_ge(tail_steps, TAIL_AGG + TAIL_NORM)
            nc.scalar.activation(stats[:, 1, :], stats[:, 0, :], ACT.Sqrt).then_inc(tail_act, 1)
            act.wait_ge(tail_steps, TAIL_AGG + TAIL_NORM + 1)
            nc.scalar.activation(stats[:, 3, :], stats[:, 2, :], ACT.Tanh).then_inc(tail_act, 1)
            norm_act(act, 3)

        @block.vector
        def _(dve):
            V = nc.vector

            def steps_on(s, base=0):
                n = [0]

                def step(ins):
                    n[0] += 1
                    ins.then_inc(s, 1)
                    dve.wait_ge(s, base + n[0])
                return step

            def norm(l):
                step = steps_on(norm_steps[l])
                wide = [P, NB, F]
                step(V.tensor_reduce(stats[:, 0, :], Y[:], AX_X, ALU.add))
                step(V.tensor_scalar(stats[:, 1, :], stats[:, 0, :], 1.0 / F, None, ALU.mult))
                step(V.tensor_tensor(Y[:], Y[:], stats[:, 1, :].unsqueeze(2).broadcast_to(wide), ALU.subtract))
                step(V.tensor_tensor(X[:], Y[:], Y[:], ALU.mult))
                step(V.tensor_reduce(stats[:, 2, :], X[:], AX_X, ALU.add))
                step(V.tensor_scalar(stats[:, 3, :], stats[:, 2, :], 1.0 / F, EPS, ALU.mult, ALU.add))
                dve.wait_ge(norm_root[l], 1)
                step(V.reciprocal(stats[:, 5, :], stats[:, 4, :]))
                V.tensor_tensor(X[:], Y[:], stats[:, 5, :].unsqueeze(2).broadcast_to(wide),
                                ALU.mult).then_inc(normed[l], 1)

            dve.wait_ge(consts_in, N_PUTS * 16)
            dve.wait_ge(consts_made, 1)
            for p in range(3):
                V.tensor_copy(turn_w[:, p, 0:F], fold[:])
            V.tensor_tensor(w_first[:], cheb_sb[0:F, 0, :], cheb_sb[0:F, 2, :], ALU.subtract)
            V.tensor_tensor(turn_w[:, 0, F:P], cheb_sb[:, 1, :], cheb_sb[:, 3, :], ALU.subtract)
            V.tensor_scalar(turn_w[:, 1, F:P], cheb_sb[:, 2, :], 2.0, None, ALU.mult)
            V.tensor_scalar(turn_w[:, 2, F:P], cheb_sb[:, 3, :], 2.0, None, ALU.mult)
            for g in range(2):
                V.memset(w_hid[0:F, g, 2 * F:3 * F], 0.0)
                b_in, b_hid = bias_tmp[F:F + 1, 2 * g, :], bias_tmp[F:F + 1, 2 * g + 1, :]
                V.tensor_tensor(w_hid[F:F + 1, g, 0:2 * F], b_in[:, 0:2 * F], b_hid[:, 0:2 * F], ALU.add)
                V.tensor_copy(w_hid[F:F + 1, g, 2 * F:3 * F], b_in[:, 2 * F:3 * F])
                V.tensor_copy(w_hid[F:F + 1, g, 3 * F:4 * F], b_hid[:, 2 * F:3 * F])
            V.memset(w_att[0:F, 3 * F:6 * F], 0.0)
            V.memset(w_att[F:P, 0:3 * F], 0.0)
            dve.drain().then_inc(weights_made, 1)

            dve.wait_ge(x_in, 32)
            for n in range(4):
                dve.wait_ge(first_ready, n + 1)
                V.tensor_tensor(Y[:, n * 8:(n + 1) * 8, :], ps[:, n, :].rearrange("p (c f) -> p c f", f=F),
                                X[:, n * 8:(n + 1) * 8, :], ALU.add).then_inc(first_read, 1)
            dve.wait_ge(gat_ready, 1)
            V.tensor_copy(w_score[0:F, :], ps[0:F, 4, 0:2])
            V.tensor_copy(w_score[F:P, 0:1], ps[F:P, 4, 1:2])
            V.tensor_copy(w_score[F:P, 1:2], ps[F:P, 4, 0:1])
            V.tensor_copy(w_att[0:F, 0:3 * F], ps[0:F, 5, 0:3 * F])
            V.tensor_scalar(w_att[F:P, 3 * F:6 * F], ps[F:P, 5, 0:3 * F], -1.0, None, ALU.mult)
            dve.drain().then_inc(first_read, 1)
            dve.wait_ge(first_read, 5)

            def copy_product_dve(p, n):
                dve.wait_ge(ring_used, n * NS + p * SLOTS)
                dve.wait_ge(turned[p], n)
                V.tensor_copy(turn_in[:, 0:HALF], ps[:, 0, :]).then_inc(product_copied[p], 1)

            def read_turned(p, n):
                dve.wait_ge(turned[p], n + 1)
                turned_rows = ps[:, 4:6, :].rearrange("p a (c f) -> p (a c) f", f=2 * F)
                blocks = bass.ds((n - 1) * CB, CB)
                if p == 0:
                    V.tensor_copy(T1[:, blocks, :], turned_rows[:, :, 0:F])
                if p == 1:
                    V.scalar_tensor_tensor(T2[:, blocks, :], turned_rows[:, :, 0:F], 2.0, X[:, blocks, :],
                                           ALU.mult, ALU.subtract)
                V.tensor_tensor(Y[:, blocks, :], turned_rows[:, :, F:2 * F], Y[:, blocks, :],
                                ALU.add).then_inc(turn_read[p], 1)
                if p == 1:
                    dve.wait_ge(counts_turned, n + 1)
                    V.tensor_copy(degrees[:, blocks, :],
                                  ps[:, 2, 0:2 * CB].rearrange("p (c n) -> p c n", n=2)).then_inc(counts_read, 1)
                if p == 2:
                    dve.wait_ge(rows_turned, n)
                    V.tensor_copy(edge_sum[:, blocks], ps[:, 2, 0:CB]).then_inc(rows_read, 1)

            def settle(p):
                copy_product_dve(p, NQ)
                read_turned(p, NQ)

            def rank_work(q, first):
                for s in range(NS):
                    r, t = s % RING, s % 2
                    dve.wait_ge(loaded[r], (q * 2 + (s // RING + 1)) * 16)
                    if not (first and s < 2):
                        dve.wait_ge(ring_used, q * NS + s - 1)
                    V.tensor_scalar(mask[:, t], ring[:, r], 0.0, None, ALU.not_equal).then_inc(dve_signs[0], 1)
                    for j in range(GB):
                        if s == 0 and j == 0:
                            V.memset(later[:, t, 0], 0.0).then_inc(signs_ready[0], 1)
                            dve.wait_ge(dve_signs[0], q * NS + s + 1)
                            continue
                        k_seen = block_order(0)[(j - 1) % GB]
                        t_seen = t if j else 1 - t
                        dve.wait_ge(dve_signs[0], q * NS + s + 1)
                        dve.wait_ge(signs_ready[0], q * (GB * NS) + (s * GB + j))
                        V.tensor_tensor(later[:, t, j], later[:, t_seen, (j - 1) % GB], mask[:, t_seen, k_seen],
                                        ALU.add).then_inc(signs_ready[0], 1)
                        if s == 0 and j == 1 and not first:
                            copy_product_dve(0, q)
                    if s == 2 and not first:
                        read_turned(0, q)

            def sign_work(q, first):
                for s in range(NS):
                    r, t = s % RING, s % 2
                    dve.wait_ge(loaded[r], (q * 2 + (8 + s // RING + 1)) * 16)
                    dve.wait_ge(ring_used, q * NS + (SLOTS + s - 1))
                    above = V.tensor_scalar(mask[:, t], ring[:, r], 0.0, None, ALU.is_gt)
                    below = V.tensor_scalar(later[:, t], ring[:, r], 0.0, None, ALU.is_lt)
                    if s < 2:
                        above.then_inc(dve_signs[1], 1)
                        below.then_inc(dve_signs[1], 1)
                        dve.wait_ge(dve_signs[1], q * 4 + 2 * (s + 1))
                        cut = offdiag_b[:].unsqueeze(1).broadcast_to([P, GB, P])
                        for part in (mask, later):
                            mine = own_blocks(part[:, t], s)
                            below = V.tensor_tensor(mine, mine, cut, ALU.mult)
                    below.then_inc(signs_ready[1], 1)
                    if s == 0 and not first:
                        copy_product_dve(1, q)
                    if s == 2 and not first:
                        read_turned(1, q)

            def row_work(q, first):
                for s in range(NS):
                    dve.wait_ge(loaded[s % RING], (q * 2 + (16 + s // RING + 1)) * 16)
                    if s == 0 and not first:
                        dve.wait_ge(row_ready, q)
                    for k in range(GB):
                        edges = ring[:, s % RING, k, :]
                        if s == 0 and k == 0:
                            V.tensor_copy(row_sum, edges).then_inc(row_steps, 1)
                            if not first:
                                copy_product_dve(2, q)
                        else:
                            dve.wait_ge(row_steps, q * (GB * NS) + (s * GB + k))
                            V.tensor_tensor(row_sum, row_sum, edges, ALU.add).then_inc(row_steps, 1)
                    if s == 2 and not first:
                        read_turned(2, q)
                dve.wait_ge(row_steps, (q + 1) * (GB * NS))
                if not first:
                    dve.wait_ge(rows_turned, q)
                V.tensor_copy(row_out, row_sum).then_inc(row_ready, 1)

            for p, work in enumerate((rank_work, sign_work, row_work)):
                quarters(dve, work, lambda: settle(p))
                dve.wait_ge(turn_read[p], NQ + 1)
            norm(0)

            def split(i, src):
                for m in range(2):
                    dve.wait_ge(parts_act[i], m + 1)
                    rest = src if m == 0 else split_rest[i]
                    V.tensor_tensor(split_rest[i], rest, parts[:, :, m * F:(m + 1) * F],
                                    ALU.subtract).then_inc(parts_steps[i], 1)
                    dve.wait_ge(parts_steps[i], m + 1)
                dve.wait_ge(parts_act[i], 3)
                dve.sem_inc(parts_ready[i], 1)

            dve.wait_ge(normed[0], 1)
            split(0, X[:])
            V.memset(hT[F:F + 1, :], 1.0)

            def copy_sums(n):
                dve.wait_ge(pair_used, n * (2 * NS) + 2)
                dve.wait_ge(att_ready, (n - 1) * CB + 1)
                V.tensor_copy(turn_in[:, 0:HALF], ps[:, 2, :]).then_inc(sums_copied, 1)
                V.tensor_copy(weighted_in[:, 0:HALF], ps[:, 0, :]).then_inc(sums_copied, 1)

            def copy_attention(n):
                for c in range(CB):
                    dve.wait_ge(att_ready, (n - 1) * CB + (c + 1) + 1)
                    V.tensor_copy(att[:, c, :], ps[:, 5 + 2 * (c % 2), 0:6 * F + 2]).then_inc(att_read, 1)
                dve.wait_ge(att_read, n * CB)

            def gate_part(n, i):
                count = [(0, G_SCORES, G_SUMS, G_NEW)[i]]

                def step(ins):
                    count[0] += 1
                    ins.then_inc(gate_steps, 1)
                    dve.wait_ge(gate_steps, (n - 1) * GATE_STEPS + count[0])

                blocks = bass.ds((n - 1) * CB, CB)
                pairs = [P, CB, 2]
                scores = att[:, :, 6 * F:6 * F + 2]
                num, present, e, top, ex, ex0, z, wt = (small[:, i] for i in (0, 1, 2, 3, 4, 5, 6, 7))
                rz = hid[:, :, :, 0:2 * F].rearrange("p c g n -> p (c g) n")
                reset, update, new_in, new_hid = (hid[:, :, :, i * F:(i + 1) * F] for i in range(4))
                if i == 0:
                    step(V.tensor_copy(num, degrees[:, blocks, :]))
                    step(V.tensor_scalar(present, num, 0.0, None, ALU.is_gt))
                    step(V.scalar_tensor_tensor(e, scores, LEAK, scores, ALU.mult, ALU.max))
                    step(V.tensor_tensor(e, e, present, ALU.mult))
                    step(V.tensor_scalar(present, present, NEG_INF, -NEG_INF, ALU.mult, ALU.add))
                    step(V.tensor_tensor(e, e, present, ALU.add))
                    step(V.tensor_reduce(top[:, :, 0], e, AX_X, ALU.max))
                    step(V.tensor_scalar(top[:, :, 0], top[:, :, 0], -NEG_INF, None, ALU.max))
                    step(V.tensor_tensor(e, e, top[:, :, 0:1].broadcast_to(pairs), ALU.subtract))
                    step(V.tensor_scalar(top[:, :, 1], top[:, :, 0], -1.0, -NEG_INF, ALU.mult, ALU.add))
                    assert count[0] == G_SCORES
                if i == 1:
                    step(V.tensor_reduce(z[:, :, 0], num, AX_X, ALU.add))
                    step(V.tensor_scalar(z[:, :, 0], z[:, :, 0], -1.0, float(N), ALU.mult, ALU.add))
                    dve.wait_ge(gate_act, (n - 1) * 4 + 2)
                    step(V.tensor_tensor(z[:, :, 0], z[:, :, 0], ex0[:, :, 0], ALU.mult))
                    step(V.tensor_tensor(wt, ex, num, ALU.mult))
                    step(V.tensor_reduce(z[:, :, 1], wt, AX_X, ALU.add))
                    step(V.tensor_tensor(z[:, :, 0], z[:, :, 0], z[:, :, 1], ALU.add))
                    step(V.reciprocal(z[:, :, 1], z[:, :, 0]))
                    step(V.tensor_tensor(wt, ex, z[:, :, 1:2].broadcast_to(pairs), ALU.mult))
                    third = [P, CB, 3 * F]
                    step(V.tensor_tensor(att[:, :, 0:3 * F], att[:, :, 0:3 * F], wt[:, :, 0:1].broadcast_to(third),
                                         ALU.mult))
                    step(V.tensor_tensor(att[:, :, 3 * F:6 * F], att[:, :, 3 * F:6 * F], wt[:, :, 1:2].broadcast_to(third),
                                         ALU.mult))
                    step(V.tensor_tensor(att[:, :, 0:3 * F], att[:, :, 0:3 * F], att[:, :, 3 * F:6 * F], ALU.add))
                    dve.wait_ge(hid_read, n * CB)
                    step(V.tensor_tensor(hid[:, :, 1, 0:3 * F], hid[:, :, 1, 0:3 * F], att[:, :, 0:3 * F], ALU.add))
                    assert count[0] == G_SUMS
                if i == 2:
                    dve.wait_ge(gate_act, (n - 1) * 4 + 3)
                    step(V.tensor_scalar(rz, rz, 0.5, 0.5, ALU.mult, ALU.add))
                    step(V.tensor_tensor(gate, reset, new_hid, ALU.mult))
                    step(V.tensor_tensor(gate, gate, new_in, ALU.add))
                    assert count[0] == G_NEW
                if i == 3:
                    dve.wait_ge(gate_act, (n - 1) * 4 + 4)
                    hidden = x_q.unsqueeze(2).broadcast_to([P, CB, 2, F])
                    step(V.tensor_tensor(new_hid, hidden, gate, ALU.subtract))
                    step(V.tensor_tensor(new_hid, new_hid, update, ALU.mult))
                    step(V.tensor_tensor(gate, gate, new_hid, ALU.add))
                    step(V.tensor_tensor(gate[:, :, 0, :], gate[:, :, 0, :], gate[:, :, 1, :], ALU.add))
                    step(V.tensor_tensor(gate[:, :, 0, :], gate[:, :, 0, :],
                                         diag[:, blocks].unsqueeze(2).broadcast_to([P, CB, F]), ALU.mult))
                    assert count[0] == GATE_STEPS
                    V.tensor_tensor(Y[:, blocks, :], gate[:, :, 0, :], x_q, ALU.add).then_inc(layer1_sum, 1)

            def sign_work(q, first):
                for s in range(NS):
                    r = s % RING
                    dve.wait_ge(loaded[r], (q * 2 + (24 + s // RING + 1)) * 16)
                    if s < 2:
                        mine = own_blocks(ring[:, r], s)
                        base = q * 4 + 2 * s
                        V.tensor_tensor(own, mine, ident[:].unsqueeze(1).broadcast_to([P, GB, P]),
                                        ALU.mult).then_inc(diag_steps, 1)
                        dve.wait_ge(diag_steps, base + 1)
                        V.tensor_reduce(diag[:, bass.ds(q * CB + s * GB, GB)], own, AX_X, ALU.add).then_inc(
                            diag_steps, 1)
                        V.tensor_tensor(mine, mine, offdiag[:].unsqueeze(1).broadcast_to([P, GB, P]),
                                        ALU.mult).then_inc(diag_cut, 1)
                        dve.wait_ge(diag_cut, q * 2 + s + 1)
                        dve.wait_ge(diag_steps, base + 2)
                    for pair in range(2):
                        m = 2 * s + pair
                        edges = ring[:, r, 2 * pair:2 * pair + 2, :]
                        dve.wait_ge(pair_used, q * (2 * NS) + (m + 1))
                        V.tensor_scalar(more[:, pair], edges, 0.0, None, ALU.is_gt)
                        V.tensor_scalar(less[:, pair], edges, 0.0, None, ALU.is_lt)
                        dve.wait_ge(negs_made, q * (2 * NS) + (m + 1))
                        V.tensor_scalar(edges, edges, 0.0, None, ALU.max).then_inc(rect_ready, 1)
                        if s == 0 and pair == 0 and not first:
                            copy_sums(q)
                        if s == 2 and pair == 0 and not first:
                            copy_attention(q)
                    if s in (3, 5, 6, 7) and not first:
                        gate_part(q, (3, 5, 6, 7).index(s))

            def settle():
                copy_sums(NQ)
                copy_attention(NQ)
                for i in range(4):
                    gate_part(NQ, i)

            quarters(dve, sign_work, settle)
            dve.wait_ge(layer1_sum, NQ + 1)
            norm(1)

            dve.wait_ge(support_read, NQ)
            split(1, support)

            def copy_sums2(n):
                dve.wait_ge(decay_used, n * NS)
                dve.wait_ge(sum2_turned, n)
                V.tensor_copy(turn_in[:, 0:HALF], ps[:, 0, :]).then_inc(sum2_copied, 1)

            def read_sums2(n):
                dve.wait_ge(sum2_turned, n + 1)
                blocks = bass.ds((n - 1) * CB, CB)
                V.tensor_tensor(Y[:, blocks, :], ps[:, 4, :].rearrange("p (c f) -> p c f", f=F), X[:, blocks, :],
                                ALU.add).then_inc(sum2_read, 1)

            def decay_work(q, first):
                for s in range(NS):
                    dve.wait_ge(code_loaded[s % RING], (q * 2 + (s // RING + 1)) * 16)
                    if not (first and s < 2):
                        dve.wait_ge(decay_used, q * NS + s - 1)
                    V.tensor_scalar(decay[:, s % 2, 0:3, :], code_in[:, s % RING, 0:3, :], 128.0, None,
                                    ALU.mult).then_inc(decay_dve, 1)
                    if s == 0 and not first:
                        copy_sums2(q)
                    if s == 3 and not first:
                        read_sums2(q)

            def settle2():
                copy_sums2(NQ)
                read_sums2(NQ)

            quarters(dve, decay_work, settle2)
            dve.wait_ge(sum2_read, NQ + 1)
            V.tensor_tensor(Y[:], Y[:], b2_sb[:].unsqueeze(1).broadcast_to([P, NB, F]), ALU.add).then_inc(sum2_read, 1)
            dve.wait_ge(sum2_read, NQ + 1 + 1)
            norm(2)

            dve.wait_ge(normed[2], 1)
            step = steps_on(ext_steps)
            norm2 = stats[:, 6, :]
            step(V.tensor_tensor(Y[:], X[:], X[:], ALU.mult))
            step(V.tensor_reduce(norm2, Y[:], AX_X, ALU.add))
            for rows, a, b in ((U, F, F + 1), (V_, F + 1, F)):
                step(V.tensor_copy(rows[:, :, 0:F], X[:]))
                step(V.tensor_copy(rows[:, :, a:a + 1], norm2.unsqueeze(2)))
                step(V.memset(rows[:, :, b:b + 1], 1.0))
            step(V.tensor_scalar(stats[:, 8, :], norm2, 1.0, None, ALU.add))
            step(V.memset(aggT, 0.0))
            dve.sem_inc(ext_ready, 1)
            dve.wait_ge(uv_copied, 2 * NQ)

            def mirror_weights(v, h):
                dve.wait_ge(g_turned, v.offs * 2 + h + 1)
                if v.has_off(1):
                    dve.wait_ge(mirrored, v.offs * 2 + h - 1)
                if v.k == 0:
                    dve.wait_ge(loaded[2 + h], (32 + v.mirror_load + 1) * 16)
                V.tensor_tensor(mirror_f[:, h, :].rearrange("p (b c) -> p b c", c=P),
                                ps[:, 6, :].rearrange("p (b c) -> p b c", c=P),
                                ring[:, 2 + h, :, v.k * P:(v.k + 1) * P], ALU.mult).then_inc(mirror_weighted, 1)

            def add(cols, sums, before):
                if not (isinstance(before, int) and before == 0):
                    dve.wait_ge(agg_added, before)
                V.tensor_tensor(aggT[:, cols], aggT[:, cols], sums, ALU.add).then_inc(agg_added, 1)

            def unit_step(at):
                v = at(4)
                if v and v.off:
                    mirror_weights(v, 1)
                u = at(0)
                if u:
                    if u.has(4):
                        dve.wait_ge(g_made, u.n - 3)
                    dve.wait_ge(dist_ready, 2 * u.n + 1)
                    V.tensor_scalar(near[:, u.k % 4], ps[:, 0:2, :].rearrange("p h c -> p (h c)"), TINY_Q, None,
                                    ALU.max).then_inc(clamped, 1)
                    if u.has(2):
                        dve.wait_ge(log_pairs, 2 * u.n - 2)
                    dve.wait_ge(dist_ready, 2 * u.n + 2)
                    V.tensor_scalar(denom[:, u.k % 2], ps[:, 2:4, :].rearrange("p h c -> p (h c)"), MIN_NORM, None,
                                    ALU.max).then_inc(clamped, 1)
                v = at(1)
                if v:
                    dve.wait_ge(norms_made, v.n + 1)
                    V.tensor_scalar(both[:, v.k % 4], both[:, v.k % 4], TANH_CLIP, None, ALU.min).then_inc(clipped, 1)
                v = at(4)
                if v and v.off and v.k % GB == GB - 1:
                    dve.wait_ge(mirrored, v.offs * 2 + 2)
                    add(bass.ds(v.J * QC + v.k // GB * HALF, HALF), ps[0:F + 1, 7, :], v.adds + 1 + 2 * (v.k // GB))
                v = at(3)
                if v and v.off:
                    mirror_weights(v, 0)
                v = at(2)
                if v:
                    if v.off:
                        dve.wait_ge(atanh_made, v.offs + 1)
                    else:
                        dve.wait_ge(halves_made, v.n + 1)
                        V.tensor_tensor(near[:, v.k % 4], near[:, v.k % 4], both[:, v.k % 4],
                                        ALU.subtract).then_inc(atanh_diag, 1)
                        dve.wait_ge(atanh_diag, v.J * CB + (v.k + 1))
                    g = both[:, v.k % 4]
                    V.tensor_tensor(g, near[:, v.k % 4], scale[:, v.k % 4], ALU.mult).then_inc(g_made, 1)
                    dve.wait_ge(g_made, v.n + 1)
                    if v.k % GB == 0:
                        dve.wait_ge(loaded[v.k // GB], (32 + v.direct_load + 1) * 16)
                    edges = ring[:, v.k // GB, v.k % GB, :]
                    V.tensor_tensor(edges, edges, g, ALU.mult).then_inc(weighted, 1)
                v = at(3)
                if v and v.k == CB - 1:
                    dve.wait_ge(gathered, v.n + 1)
                    add(bass.ds(v.I * QC, QC), ps[0:F + 1, 4:6, :].rearrange("p h c -> p (h c)"),
                        v.adds + (2 if v.off else 0))

            run_units(dve, unit_step)
            dve.wait_ge(agg_turned, 1)
            for i in range(NB // GB):
                sums = ps[:, i, 0:GB * (F + 1)].rearrange("p (c f) -> p c f", f=F + 1)
                V.tensor_copy(Y[:, GB * i:GB * (i + 1), :], sums[:, :, 0:F]).then_inc(agg_read, 1)
                V.tensor_copy(stats[:, 7, GB * i:GB * (i + 1)], sums[:, :, F]).then_inc(agg_read, 1)
            dve.wait_ge(agg_read, 2 * NB // GB)
            step = steps_on(tail_steps)
            wide = [P, NB, F]
            room = near[:].rearrange("p u c -> p (u c)")[:, 0:NB * F].rearrange("p (b f) -> p b f", f=F)
            s_dot, s_own, s_b, s_kappa = (stats[:, i, :] for i in (0, 1, 2, 3))
            step(V.tensor_tensor(room, X[:], Y[:], ALU.mult))
            step(V.tensor_reduce(s_dot, room, AX_X, ALU.add))
            step(V.scalar_tensor_tensor(s_own, s_dot, 2.0, stats[:, 7, :], ALU.mult, ALU.subtract))
            step(V.tensor_scalar(s_b, norm2, -1.0, 1.0, ALU.mult, ALU.add))
            step(V.tensor_tensor(room, X[:], s_own.unsqueeze(2).broadcast_to(wide), ALU.mult))
            step(V.tensor_tensor(Y[:], Y[:], s_b.unsqueeze(2).broadcast_to(wide), ALU.mult))
            step(V.tensor_tensor(Y[:], Y[:], room, ALU.add))
            step(V.tensor_scalar(s_b, s_b, MIN_NORM, 0.5, ALU.max, ALU.mult))
            step(V.tensor_scalar(s_dot, edge_sum[:], 1e-8, None, ALU.max))
            step(V.reciprocal(s_own, s_dot))
            step(V.tensor_tensor(s_kappa, s_b, s_own, ALU.mult))
            step(V.tensor_tensor(Y[:], Y[:], s_kappa.unsqueeze(2).broadcast_to(wide), ALU.mult))
            for n in range(NQ):
                dve.wait_ge(moved_ready, n + 1)
                step(V.tensor_tensor(room[:, n * CB:(n + 1) * CB, :], ps[:, 4 + n, :].rearrange("p (c f) -> p c f", f=F),
                                     b3_sb[:].unsqueeze(1).broadcast_to([P, CB, F]), ALU.add))
            step(V.tensor_tensor(Y[:], room, room, ALU.mult))
            step(V.tensor_reduce(stats[:, 0, :], Y[:], AX_X, ALU.add))
            dve.wait_ge(tail_act, 1)
            step(V.tensor_scalar(stats[:, 2, :], stats[:, 1, :], MIN_NORM, None, ALU.max))
            dve.wait_ge(tail_act, 2)
            step(V.reciprocal(stats[:, 4, :], stats[:, 2, :]))
            step(V.tensor_tensor(stats[:, 5, :], stats[:, 3, :], stats[:, 4, :], ALU.mult))
            step(V.tensor_tensor(room, room, stats[:, 5, :].unsqueeze(2).broadcast_to(wide), ALU.mult))
            step(V.tensor_tensor(Y[:], X[:], room, ALU.add))
            norm(3)

        @block.sync
        def _(sp):
            sp.wait_ge(normed[3], 1)
            sp.dma_start(out, X[:]).then_inc(out_stored, 16)
            sp.wait_ge(out_stored, 16)


def lay_out(x, adj, L0_gnn_weight, L1_gnn_W_gat, L1_gnn_a_gat, L1_gnn_w_ih_e, L1_gnn_w_hh_e, L1_gnn_b_ih_e,
            L1_gnn_b_hh_e, L1_gnn_w_ih_n, L1_gnn_w_hh_n, L1_gnn_b_ih_n, L1_gnn_b_hh_n, L2_gnn_weight, L2_gnn_bias,
            L3_gnn_weight, L3_gnn_bias):
    def turn(a):
        return np.ascontiguousarray(np.asarray(a).T)

    def nodes(a):
        return np.ascontiguousarray(np.asarray(a).reshape(NB, P, F).transpose(1, 0, 2))

    def row(a):
        return np.ascontiguousarray(np.asarray(a).reshape(1, -1))

    return {
        "adjT": turn(adj), "x": nodes(x), "xT": turn(x),
        "cheb_w": np.ascontiguousarray(L0_gnn_weight),
        "gatWT": turn(L1_gnn_W_gat), "gat_a2": turn(np.asarray(L1_gnn_a_gat).reshape(2, F)),
        "wieT": turn(L1_gnn_w_ih_e), "wheT": turn(L1_gnn_w_hh_e), "bie": row(L1_gnn_b_ih_e), "bhe": row(L1_gnn_b_hh_e),
        "winT": turn(L1_gnn_w_ih_n), "whnT": turn(L1_gnn_w_hh_n), "bin": row(L1_gnn_b_ih_n), "bhn": row(L1_gnn_b_hh_n),
        "w2": np.ascontiguousarray(L2_gnn_weight), "b2": row(L2_gnn_bias),
        "w3": np.ascontiguousarray(L3_gnn_weight), "b3": row(L3_gnn_bias),
    }


def kernel(**inputs):
    from concourse import bacc
    from concourse.bass_utils import run_bass_kernel_spmd

    nc = bacc.Bacc("TRN2", target_bir_lowering=False, num_devices=1)
    arrays = {f"in_{k}": a for k, a in lay_out(**inputs).items()}
    aps = [nc.dram_tensor(k, a.shape, mybir.dt.from_np(a.dtype), kind="ExternalInput").ap()
           for k, a in arrays.items()]
    out = nc.dram_tensor("out_nodes", (P, NB, F), F32, kind="ExternalOutput").ap()
    adjacency_stack(nc, *aps, out)
    result = run_bass_kernel_spmd(nc, [arrays], core_ids=[0])
    return result.results[0]["out_nodes"].transpose(1, 0, 2).reshape(N, F)
```

```python
from contextlib import ExitStack

import numpy as np

import concourse.bass as bass
from concourse import mybir

ALU = mybir.AluOpType
ACT = mybir.ActivationFunctionType
AX_X = mybir.AxisListType.X
F32 = mybir.dt.float32
BF16 = mybir.dt.bfloat16
I16 = mybir.dt.int16
U8 = mybir.dt.uint8

P = 128
N = 4096
F = 64
NB = N // P
QC = 1024
NQ = N // QC
GB = 4
NS = NB // GB
HALF = 512
CB = QC // P
RING = 4
SLOTS = NQ * NS
EPS = 1e-5
LEAK = 0.2
NEG_INF = 9.0e15
MAX_NEIGH = 100
CODE_BIAS = 8192.0
CODE_SCALE = 2.0 ** 27
TINY_Q = 2.0 ** -63
MIN_NORM = 1e-15
TANH_CLIP = 1.0 - 1e-5


def adjacency_stack(nc, adjT, x, xT, cheb_w, gatWT, gat_a2, wieT, wheT, bie, bhe, winT, whnT, bin_, bhn,
                    w2, b2, w3, b3, out):
    adj_slots = adjT.rearrange("(g k p) (q c) -> p g k q c", k=GB, p=P, c=QC)
    codes_dram = nc.dram_tensor("codes", [SLOTS, P, GB * QC], U8, kind="Internal").ap()

    ctx = ExitStack()
    with ctx:
        def sb(name, shape, dt=F32):
            return ctx.enter_context(nc.sbuf_tensor(name, shape, dt))

        def sem(name):
            return ctx.enter_context(nc.semaphore(name))

        ps = ctx.enter_context(nc.psum_tensor("ps", [P, 8, HALF], F32))

        WORK = 26 * 1024

        ring = sb("ring", [P, RING, GB, QC])
        X = sb("X", [P, NB, F])
        Y = sb("Y", [P, NB, F])
        stage_f = sb("stage_f", [P, 2, GB, F + 1])
        stage_words = sb("stage_words", [P, 2 * GB * P])
        stage_b = stage_words[:, 0:2 * GB * 3 * F // 2].bitcast(BF16).rearrange("p (t k n) -> p t k n", t=2, k=GB)
        stat = stage_words[0:F + 2, :].rearrange("p (t c) -> p t c", t=2)
        turn_in = sb("turn_in", [P, QC])
        diag = sb("diag", [P, NB])
        degrees = sb("degrees", [P, NB, 2])
        edge_sum = sb("edge_sum", [P, NB])
        stats = sb("stats", [P, 10, NB])
        work = sb("work", [P, WORK])

        ident = sb("ident", [P, P])
        offdiag = sb("offdiag", [P, P])
        offdiag_b = sb("offdiag_b", [P, P], BF16)
        later_or_self = sb("later_or_self", [P, P], BF16)
        minus_ones = sb("minus_ones", [P, P], BF16)
        ones = sb("ones", [P, 32], BF16)
        ones_f = sb("ones_f", [P, 1])
        code_bias = sb("code_bias", [P, 1])
        cheb_sb = sb("cheb_sb", [P, 4, F])
        turn_w = sb("turn_w", [P, 3, 2 * F])
        w_first = sb("w_first", [F, F])
        w_edge = sb("w_edge", [P, 3 * F])
        w_score = sb("w_score", [P, 2])
        w_hid = sb("w_hid", [F + 1, 2, 4 * F])
        w_att = sb("w_att", [P, 6 * F])
        gatWT_sb = sb("gatWT_sb", [F, 2 * F])
        gat_a_sb = sb("gat_a_sb", [F, 2])
        winT_sb = sb("winT_sb", [F, 3 * F])
        w2_sb = sb("w2_sb", [F, F])
        w3_sb = sb("w3_sb", [F + 1, F])
        b2_sb = sb("b2_sb", [P, F])
        b3_sb = sb("b3_sb", [P, F])
        fold = sb("fold", [P, F])
        minus_two = sb("minus_two", [P, 1])

        at = [0]

        def carve(words, reset=None):
            if reset is not None:
                at[0] = reset
            a = at[0]
            at[0] += words
            assert at[0] <= WORK, at[0]
            return work[:, a:a + words]

        T1 = carve(NB * F, 0).rearrange("p (b f) -> p b f", f=F)
        T2 = carve(NB * F).rearrange("p (b f) -> p b f", f=F)
        mask = carve(2 * GB * QC // 2).bitcast(BF16).rearrange("p (t k c) -> p t k c", t=2, k=GB)
        later = carve(2 * GB * QC // 2).bitcast(BF16).rearrange("p (t k c) -> p t k c", t=2, k=GB)
        codes = carve(2 * GB * QC // 4).bitcast(U8).rearrange("p (t k c) -> p t k c", t=2, k=GB)
        xT_sb = carve(N)[0:F, :]
        bias_tmp = carve(4 * 3 * F)[0:F + 1, :].rearrange("p (i n) -> p i n", i=4)
        count_in = codes.rearrange("p t k c -> p (t k c)")[0:F, 0:4 * QC].bitcast(F32)

        row_out = mask[:, 1].rearrange("p k c -> p (k c)")[:, 0:2 * QC].bitcast(F32)
        row_sum = mask[:, 0].rearrange("p k c -> p (k c)")[:, 0:2 * QC].bitcast(F32)

        more = carve(2 * 2 * QC // 2, 0).bitcast(BF16).rearrange("p (t k c) -> p t k c", t=2, k=2)
        less = carve(2 * 2 * QC // 2).bitcast(BF16).rearrange("p (t k c) -> p t k c", t=2, k=2)
        negs = carve(2 * 2 * QC).rearrange("p (t k c) -> p t k c", t=2, k=2)
        hid = carve(CB * 8 * F).rearrange("p (c g n) -> p c g n", c=CB, g=2)
        att = carve(CB * (6 * F + 2)).rearrange("p (c n) -> p c n", c=CB)
        parts = carve(NB * 3 * F // 2).bitcast(BF16).rearrange("p (b n) -> p b n", n=3 * F)
        weighted_in = carve(QC)
        hT = carve(QC)[0:F + 1, :]
        x_q = carve(CB * F).rearrange("p (c f) -> p c f", f=F)
        own = carve(GB * P).rearrange("p (k c) -> p k c", k=GB)
        gate = carve(CB * 2 * F).rearrange("p (c g f) -> p c g f", c=CB, g=2)
        small = carve(16 * 2 * CB).rearrange("p (i c n) -> p i c n", i=16, c=CB)

        code_in = carve(4 * QC, 0).bitcast(U8).rearrange("p (r k c) -> p r k c", r=4, k=GB)
        decay = carve(4 * QC).bitcast(I16).rearrange("p (t k c) -> p t k c", t=2, k=GB)
        support = carve(NB * F).rearrange("p (b f) -> p b f", f=F)
        assert at[0] <= 2048 * 2 + 4096 + CB * 8 * F + CB * (6 * F + 2)
        square_room = carve(CB * F, at[0] + 4096).rearrange("p (c f) -> p c f", f=F)
        h2T = carve(2 * QC, at[0] - CB * F)[0:F, :].rearrange("p (t c) -> p t c", t=2)

        UT = carve(N, 0)[0:F + 2, :]
        VT = carve(N)[0:F + 2, :]
        aggT = carve(N)[0:F + 1, :]
        near = carve(4 * QC).rearrange("p (u c) -> p u c", u=4)
        both = carve(4 * QC).rearrange("p (u c) -> p u c", u=4)
        scale = carve(4 * QC).rearrange("p (u c) -> p u c", u=4)
        denom = carve(2 * QC).rearrange("p (u c) -> p u c", u=2)
        U = carve(NB * 98, at[0] - 14 * QC).rearrange("p (b f) -> p b f", f=98)
        moveT = carve(2 * QC, at[0])[0:F, :].rearrange("p (t c) -> p t c", t=2)
        stage_m = Y[:].rearrange("p b f -> p (b f)")[:, 0:2 * CB * (F + 1)].rearrange(
            "p (t c f) -> p t c f", t=2, c=CB)
        mirror_f = turn_in[:].rearrange("p (h c) -> p h c", h=2)

        split_rest = [Y[:], support]

        def own_blocks(slot, s):
            first = slot[:, 0, s * GB * P:(s * GB + 1) * P]
            return bass.AP(first.tensor, first.offset, [first.ap[0], (QC + P, GB), (1, P)])

        ROUND = 2 * CB
        UNITS = NQ * ROUND + 2 * CB

        class Unit:
            def __init__(self, n, J, I, k, off, direct_load, mirror_load, quad, offs, adds, free, targets_buffer=0,
                         targets_free=None):
                self.n = n
                self.J, self.I = J, I
                self.k = k
                self.off = off
                self.direct_load = direct_load
                self.mirror_load = mirror_load
                self.quad = quad
                self.offs = offs
                self.adds = adds
                self.free = free
                self.targets_buffer = targets_buffer
                self.targets_free = targets_free

            def has(self, back):
                return not isinstance(self.n, int) or self.n >= back

            def has_off(self, back):
                return not isinstance(self.offs, int) or self.offs >= back

        def round_unit(J, u):
            if u < 0:
                J, u = J - 1, u + ROUND
            off = u >= CB
            I = ((J + 1) % NQ if off else J)
            free = (J * 4 + 1, J * 4) if off else (J * 4 - 1, None)
            return Unit(J * ROUND + u, J, I, u % CB, off, J * 2 + int(off), J, J * 4 + u // GB,
                        J * CB + (u - CB) if off else None, J * 4, free, 0, J * CB)

        def tail_unit(n):
            if n < NQ * ROUND:
                return round_unit(NQ - 1, n - (NQ - 1) * ROUND)
            if n >= UNITS:
                return None
            J, k = divmod(n - NQ * ROUND, CB)
            adds = 4 * NQ - 1 + 3 * J
            return Unit(n, J, J + 2, k, True, 2 * NQ + J, NQ + J, n // GB, NQ * CB + J * CB + k, adds,
                        (adds, adds + 1), 1 - J, NQ * CB)

        ADDS = 4 * NQ + 6
        DEPTH = 4

        def run_units(eng, step):
            for t in range(ROUND):
                step(lambda lag, t=t: round_unit(0, t - lag) if t >= lag else None)
            with eng.Fori(1, NQ) as J:
                for t in range(ROUND):
                    step(lambda lag, t=t: round_unit(J, t - lag))
            for t in range(NQ * ROUND, UNITS + DEPTH):
                step(lambda lag, t=t: tail_unit(t - lag))

        def quarters(eng, work, settle=None):
            work(0, True)
            with eng.Fori(1, NQ) as q:
                work(q, False)
            if settle:
                settle()

        block = ctx.enter_context(nc.Block())

        loaded = [sem(f"loaded{r}") for r in range(RING)]
        ring_used = sem("ring_used")
        load_turns = sem("load_turns")
        stage_turns = sem("stage_turns")
        turn_turns = sem("turn_turns")
        consts_in = sem("consts_in")
        x_in = sem("x_in")
        pool_steps = sem("pool_steps")
        consts_made = sem("consts_made")
        weights_made = sem("weights_made")
        first_ready = sem("first_ready")
        first_read = sem("first_read")
        staged = sem("staged")
        signs_ready = [sem(f"signs_ready{p}") for p in range(2)]
        dve_signs = [sem(f"dve_signs{p}") for p in range(2)]
        rank_ready = sem("rank_ready")
        codes_made = sem("codes_made")
        codes_stored = [sem(f"codes_stored{t}") for t in range(2)]
        product_ready = [sem(f"product_ready{p}") for p in range(3)]
        product_copied = [sem(f"product_copied{p}") for p in range(3)]
        turned = [sem(f"turned{p}") for p in range(3)]
        turn_read = [sem(f"turn_read{p}") for p in range(3)]
        counts_copied = sem("counts_copied")
        counts_turned = sem("counts_turned")
        counts_read = sem("counts_read")
        turn_steps = [sem(f"turn_steps{p}") for p in range(3)]
        norm_steps = [sem(f"norm_steps{l}") for l in range(4)]
        norm_root = [sem(f"norm_root{l}") for l in range(4)]
        normed = [sem(f"normed{l}") for l in range(4)]
        out_stored = sem("out_stored")
        row_steps = sem("row_steps")
        row_ready = sem("row_ready")
        rows_turned = sem("rows_turned")
        rows_read = sem("rows_read")
        gat_ready = sem("gat_ready")
        part_made = [[sem(f"part{m}_made{l}") for m in range(3)] for l in (1, 2)]
        rest_made = [[sem(f"rest{m}_made{l}") for m in range(2)] for l in (1, 2)]
        staged_parts = sem("staged_parts")
        diag_cut = sem("diag_cut")
        diag_steps = sem("diag_steps")
        negs_made = sem("negs_made")
        rect_ready = sem("rect_ready")
        pair_used = sem("pair_used")
        sums_copied = sem("sums_copied")
        x_q_ready = sem("x_q_ready")
        hT_ready = sem("hT_ready")
        hT_copied = sem("hT_copied")
        hid_ready = sem("hid_ready")
        att_ready = sem("att_ready")
        hid_read = sem("hid_read")
        att_read = sem("att_read")
        gate_steps = sem("gate_steps")
        gate_act = sem("gate_act")
        layer1_sum = sem("layer1_sum")
        code_loaded = [sem(f"code_loaded{r}") for r in range(4)]
        decay_used = sem("decay_used")
        decay_dve = sem("decay_dve")
        decay_act = sem("decay_act")
        h2T_ready = sem("h2T_ready")
        h2T_copied = sem("h2T_copied")
        support_ready = sem("support_ready")
        support_read = sem("support_read")
        sum2_copied = sem("sum2_copied")
        sum2_turned = sem("sum2_turned")
        sum2_read = sem("sum2_read")
        bias_added = sem("bias_added")
        ext_steps = sem("ext_steps")
        ext_ready = sem("ext_ready")
        uv_ready = sem("uv_ready")
        ut_copied = sem("ut_copied")
        vt_copied = sem("vt_copied")
        staged_rows = sem("staged_rows")
        staged_mirror = sem("staged_mirror")
        staged_stat = sem("staged_stat")
        dist_ready = sem("dist_ready")
        clamped = sem("clamped")
        logs_made = sem("logs_made")
        log_pairs = sem("log_pairs")
        norms_made = sem("norms_made")
        clipped = sem("clipped")
        halves_made = sem("halves_made")
        atanh_made = sem("atanh_made")
        atanh_diag = sem("atanh_diag")
        g_made = sem("g_made")
        weighted = sem("weighted")
        g_turned = sem("g_turned")
        mirror_weighted = sem("mirror_weighted")
        gathered = sem("gathered")
        mirrored = sem("mirrored")
        agg_added = sem("agg_added")
        plus_made = sem("plus_made")
        agg_turned = sem("agg_turned")
        tail_steps = sem("tail_steps")
        tail_act = sem("tail_act")
        moveT_ready = sem("moveT_ready")
        moveT_copied = sem("moveT_copied")
        moved_ready = sem("moved_ready")

        N_PUTS = 19
        GATE_TURNS = ((2, 1), (3, 1), (4, 0), (5, 0), (6, 0), (6, 1))
        GATE_TURNS_ACT = ((3, 0), (4, 1), (5, 1))
        G_SCORES = 10
        G_MIXED = 20
        G_SUMS = 22
        G_NEW = 25
        GATE_STEPS = 30
        NORM_SUMS = 5
        TAIL_FIRST = 6
        TAIL_AGG = 8
        TAIL_MOVED = 3

        def quarter_of(p, q):
            return NQ - 1 - q if p == 1 else q

        def source_group(p, q, s):
            if p == 0:
                return NS - 1 - s
            if p == 1:
                return (NS - q * 2 + s) % NS
            if p == 2:
                return (s + NS - 2) % NS
            return (q * 2 + s) % NS

        def ring_slot(p, s):
            return RING - 1 - s % RING if p in (1, 2) else s % RING

        LOADED = [0]
        for p in range(4):
            LOADED.append(LOADED[-1] + SLOTS // RING - (p in (1, 2)))

        def loads(p, q, s):
            return q * 2 + (LOADED[p] + s // RING + (p not in (1, 2)))

        def block_order(p):
            return (3, 2, 1, 0) if p == 0 else (0, 1, 2, 3)

        @block.sync
        def _(sp):
            for credited in (*turn_read, *turned, counts_turned, layer1_sum, att_ready, sum2_turned, sum2_read):
                sp.sem_inc(credited, 1)

            def load(p, q, s):
                r = ring_slot(p, s)
                g = source_group(p, q, s)
                src = adj_slots[:, bass.ds(g, 1), :, bass.ds(quarter_of(p, q), 1), :].rearrange(
                    "p a k b c -> p (a k) (b c)")
                sp.dma_start(ring[:, r], src).then_inc(loaded[r], 16)

            def wait_then_load(p, q, s, used, value):
                sp.wait_ge(used, value)
                if not isinstance(q, int):
                    sp.sem_inc(load_turns, 1)
                load(p, q, s)

            load(0, 0, 0)
            sp.dma_start(xT_sb, xT).then_inc(x_in, 16)
            sp.wait_ge(x_in, 32)
            sp.wait_ge(consts_in, N_PUTS * 16)
            for s in range(1, RING):
                load(0, 0, s)
            for s in range(RING, NS):
                wait_then_load(0, 0, s, ring_used, s - RING + 1)
            with sp.Fori(1, NQ) as q:
                for s in range(NS):
                    wait_then_load(0, q, s, ring_used, q * NS + (s - RING + 1))
            for p in (1, 2):
                for s in range(RING, NS):
                    wait_then_load(p, 0, s, ring_used, p * SLOTS + s - RING + 1)
                with sp.Fori(1, NQ) as q:
                    for s in range(NS):
                        wait_then_load(p, q, s, ring_used, q * NS + (p * SLOTS + s - RING + 1))
            for s in range(NS):
                if s < RING:
                    wait_then_load(3, 0, s, ring_used, 3 * SLOTS - s)
                else:
                    wait_then_load(3, 0, s, pair_used, 2 + 2 * (s - RING + 1))
            with sp.Fori(1, NQ) as q:
                for s in range(NS):
                    wait_then_load(3, q, s, pair_used, q * (2 * NS) + (2 + 2 * (s - RING + 1)))
            for t in range(2):
                sp.wait_ge(codes_stored[t], NQ * NS // 2 * 16)
            sp.wait_ge(pair_used, 2 + 2 * SLOTS)

            def load_codes(q, s):
                r = s % RING
                src = codes_dram[bass.ds(q * NS + s, 1)].rearrange("a p n -> p (a n)")
                sp.dma_start(code_in[:, r].rearrange("p k c -> p (k c)"), src).then_inc(code_loaded[r], 16)

            for s in range(NS):
                if s >= RING:
                    sp.wait_ge(decay_dve, s - RING + 1)
                    sp.wait_ge(decay_act, s - RING + 1)
                load_codes(0, s)
            with sp.Fori(1, NQ) as q:
                for s in range(NS):
                    sp.wait_ge(decay_dve, q * NS + (s - RING + 1))
                    sp.wait_ge(decay_act, q * NS + (s - RING + 1))
                    sp.sem_inc(load_turns, 1)
                    load_codes(q, s)
            def load_pair(J, I, r):
                rows, cols = (J, I) if r < 2 else (I, J)
                src = adj_slots[:, bass.ds(rows * 2 + r % 2, 1), :, bass.ds(cols, 1), :].rearrange(
                    "p a k b c -> p (a k) (b c)")
                sp.dma_start(ring[:, r], src).then_inc(loaded[r], 16)

            for r in (0, 1):
                sp.wait_ge(pair_used, 2 + 2 * (SLOTS - RING + r + 1))
                load_pair(0, 0, r)
            for r in (2, 3):
                sp.wait_ge(pair_used, 2 + 2 * (SLOTS - RING + r + 1))
                load_pair(0, 1, r)
            for r in (0, 1):
                sp.wait_ge(gathered, GB * (r + 1))
                load_pair(0, 1, r)
            with sp.Fori(1, NQ) as J:
                for r in (0, 1):
                    sp.wait_ge(gathered, J * ROUND + (GB * (r + 1) - CB))
                    sp.sem_inc(load_turns, 1)
                    load_pair(J, J, r)
                for r in (2, 3):
                    sp.wait_ge(mirror_weighted, J * (2 * CB) + (r - 3))
                    sp.sem_inc(load_turns, 1)
                    load_pair(J, (J + 1) % NQ, r)
                for r in (0, 1):
                    sp.wait_ge(gathered, J * ROUND + GB * (r + 1))
                    sp.sem_inc(load_turns, 1)
                    load_pair(J, (J + 1) % NQ, r)
            for J in range(2):
                base = NQ * ROUND + J * CB
                for r in (0, 2, 3, 1):
                    if r < 2:
                        sp.wait_ge(gathered, base - CB + GB * (r + 1))
                    else:
                        sp.wait_ge(mirror_weighted, (NQ + J) * 2 * CB + (r - 3))
                    load_pair(J, J + 2, r)

        @block.gpsimd
        def _(pool):
            steps = [0]

            def step(ins):
                steps[0] += 1
                ins.then_inc(pool_steps, 1)
                pool.wait_ge(pool_steps, steps[0])

            def diagonal(ap, base, fill, width):
                step(nc.gpsimd.affine_select(out=ap, in_=ap, compare_op=ALU.not_equal, fill=fill, base=base,
                                             pattern=[[-1, width]], channel_multiplier=1))

            step(nc.gpsimd.memset(ident[:], 0.0))
            diagonal(ident[:], 0, 1.0, P)
            step(nc.gpsimd.memset(offdiag[:], 1.0))
            diagonal(offdiag[:], 0, 0.0, P)
            step(nc.gpsimd.memset(offdiag_b[:], 1.0))
            diagonal(offdiag_b[:], 0, 0.0, P)
            step(nc.gpsimd.memset(fold[:], 0.0))
            diagonal(fold[:], 0, 1.0, F)
            diagonal(fold[:], -F, 1.0, F)
            step(nc.gpsimd.memset(minus_ones[:], -1.0))
            step(nc.gpsimd.memset(ones[:], 1.0))
            step(nc.gpsimd.memset(ones_f[:], 1.0))
            step(nc.gpsimd.memset(code_bias[:], MAX_NEIGH - CODE_BIAS))
            step(nc.gpsimd.memset(later_or_self[:], -1.0))
            step(nc.gpsimd.affine_select(out=later_or_self[:], in_=later_or_self[:], compare_op=ALU.is_gt, fill=0.0,
                                         base=0, pattern=[[-1, P]], channel_multiplier=1))
            diagonal(later_or_self[:], 0, CODE_BIAS, P)
            step(nc.gpsimd.memset(minus_two[0:F], -2.0))
            step(nc.gpsimd.memset(minus_two[F:P], 1.0))
            pool.sem_inc(consts_made, 1)

            pool.wait_ge(turn_read[0], NQ + 1)

            def work(q, first):
                for s in range(NS):
                    pool.wait_ge(ring_used, SLOTS + q * NS + s - 1)
                    pool.sem_inc(stage_turns, 1)
                    nc.gpsimd.tensor_copy(stage_f[:, s % 2, :, 0:F],
                                          T1[:, bass.ds(source_group(1, q, s) * GB, GB), :]).then_inc(staged, 1)
            quarters(pool, work)

            def stage_x(n):
                pool.wait_ge(layer1_sum, n)
                pool.sem_inc(stage_turns, 1)
                nc.gpsimd.tensor_copy(x_q, X[:, bass.ds((n - 1) * CB, CB), :]).then_inc(x_q_ready, 1)

            def work(q, first):
                for s in range(NS):
                    g = source_group(3, q, s)
                    if first and s % 2 == 0:
                        pool.wait_ge(part_made[0][2], s // 2 + 1)
                    if not (first and s == 0):
                        pool.wait_ge(pair_used, q * (2 * NS) + 2 * s)
                    pool.sem_inc(stage_turns, 1)
                    nc.gpsimd.tensor_copy(stage_f[:, s % 2, :, 0:F],
                                          X[:, bass.ds(g * GB, GB), :]).then_inc(staged_parts, 1)
                    nc.gpsimd.tensor_copy(stage_b[:, s % 2], parts[:, bass.ds(g * GB, GB), :]).then_inc(
                        staged_parts, 1)
                    if s == 1 and not first:
                        stage_x(q)
            quarters(pool, work, lambda: stage_x(NQ))


            pool.wait_ge(ext_ready, NQ)
            norm_plus = stats[:, 8, :]

            def unit_step(at):
                u = at(0)
                if u:
                    if u.k % GB == 0:
                        if u.has(2 * GB):
                            pool.wait_ge(gathered, (u.quad - 1) * GB)
                            pool.sem_inc(stage_turns, 1)
                        t = u.k // GB
                        blocks = bass.ds(u.J * CB + u.k, GB)
                        nc.gpsimd.tensor_copy(stage_f[:, t, :, 0:F], X[:, blocks, :]).then_inc(staged_rows, 1)
                        nc.gpsimd.tensor_copy(stage_f[:, t, :, F], norm_plus[:, blocks]).then_inc(staged_rows, 1)
                    if u.off and u.k == 0:
                        m = u.targets_buffer
                        if not m and u.has_off(1):
                            pool.wait_ge(mirrored, 2 * u.targets_free)
                            pool.sem_inc(stage_turns, 1)
                        blocks = bass.ds(u.I * CB, CB)
                        nc.gpsimd.tensor_copy(stage_m[:, m, :, 0:F], X[:, blocks, :]).then_inc(staged_mirror, 1)
                        nc.gpsimd.tensor_copy(stage_m[:, m, :, F], norm_plus[:, blocks]).then_inc(staged_mirror, 1)
                    pool.wait_ge(logs_made, u.n + 1)
                    if u.has(4):
                        v = at(4)
                        pool.wait_ge(weighted, v.n + 1)
                        if v.off:
                            pool.wait_ge(g_turned, v.offs * 2 + 2)
                    lq, ld = near[:, u.k % 4], denom[:, u.k % 2]
                    nc.gpsimd.tensor_tensor(both[:, u.k % 4], lq, ld, ALU.subtract).then_inc(log_pairs, 1)
                    nc.gpsimd.tensor_tensor(scale[:, u.k % 4], lq, ld, ALU.add).then_inc(log_pairs, 1)
                v = at(1)
                if v and v.off:
                    pool.wait_ge(halves_made, v.n + 1)
                    nc.gpsimd.tensor_tensor(near[:, v.k % 4], near[:, v.k % 4], both[:, v.k % 4],
                                            ALU.subtract).then_inc(atanh_made, 1)

            run_units(pool, unit_step)

        @block.tensor
        def _(pe):
            pe.wait_ge(weights_made, 1)
            pe.wait_ge(x_in, 32)
            for n in range(4):
                for c in range(8):
                    b = n * 8 + c
                    mm = nc.tensor.matmul(ps[:, n, c * F:(c + 1) * F], xT_sb[:, b * P:(b + 1) * P], w_first[:],
                                          start=True, stop=True)
                mm.then_inc(first_ready, 1)
            nc.tensor.matmul(ps[:, 4, 0:2], gatWT_sb[:], gat_a_sb[:], start=True, stop=True)
            nc.tensor.matmul(ps[:, 5, 0:3 * F], gatWT_sb[:], winT_sb[:], start=True, stop=True).then_inc(gat_ready, 1)
            pe.wait_ge(first_read, 5)

            def rank(q, s, j, k):
                pe.wait_ge(signs_ready[0], q * (GB * NS) + (s * GB + j + 1))
                for h in range(2):
                    cols = slice(h * HALF, (h + 1) * HALF)
                    pe.wait_ge(codes_made, q * (2 * GB * NS) + ((s * GB + j) * 2 + h))
                    nc.tensor.matmul(ps[:, 6 + h, :], later_or_self[:], mask[:, s % 2, k, cols],
                                     start=True, stop=False)
                    nc.tensor.matmul(ps[:, 6 + h, :], minus_ones[:], later[:, s % 2, j, cols],
                                     start=False, stop=True).then_inc(rank_ready, 1)

            def count(q, s, k):
                for h in range(2):
                    cols = slice(h * HALF, (h + 1) * HALF)
                    st, sp_ = s == 0 and k == 0, s == NS - 1 and k == GB - 1
                    nc.tensor.matmul(ps[0:32, 6 + h, :], ones[:], mask[:, s % 2, k, cols], start=st, stop=sp_)
                    nc.tensor.matmul(ps[32:64, 6 + h, :], ones[:], later[:, s % 2, k, cols], start=st, stop=sp_)

            def turn(p, n):
                pe.wait_ge(product_copied[p], n * 2)
                pe.wait_ge(turn_read[p], n)
                if p:
                    pe.wait_ge(turn_read[p - 1], NQ + 1)
                for c in range(CB):
                    mm = nc.tensor.matmul(ps[:, 4 + c // 4, (c % 4) * P:(c % 4 + 1) * P],
                                          turn_in[:, c * P:(c + 1) * P], turn_w[:, p, :], start=True, stop=True)
                mm.then_inc(turned[p], 1)
                if p == 1:
                    pe.wait_ge(counts_copied, n)
                    for c in range(CB):
                        mm = nc.tensor.matmul(ps[:, 2, 2 * c:2 * c + 2], count_in[:, c * P:(c + 1) * P],
                                              ident[0:F, 0:F:32], start=True, stop=True)
                    mm.then_inc(counts_turned, 1)
                if p == 2:
                    pe.wait_ge(row_ready, n)
                    for c in range(CB):
                        mm = nc.tensor.matmul(ps[:, 2, c:c + 1], row_out[:, c * P:(c + 1) * P], ones_f[:],
                                              start=True, stop=True)
                    mm.then_inc(rows_turned, 1)

            def rows_of(p, s, k):
                if p == 1:
                    return stage_f[:, s % 2, k, 0:F]
                return (X, None, T2)[p][:, source_group(p, 0, s) * GB + k, :]

            for p in range(3):
                if p == 2:
                    pe.wait_ge(turn_read[1], NQ + 1)

                def work(q, first):
                    for s in range(NS):
                        r = ring_slot(p, s)
                        pe.wait_ge(loaded[r], loads(p, q, s) * 16)
                        if p == 1:
                            pe.wait_ge(staged, q * NS + s + 1)
                        if p == 1:
                            pe.wait_ge(signs_ready[1], q * NS + s + 1)
                            if s == 0 and not first:
                                pe.wait_ge(counts_copied, q)
                        order = block_order(p)
                        for i in range(GB):
                            if p == 0:
                                rank(q, s, i, order[i])
                            if p == 1:
                                count(q, s, i)
                            if p == 2 and i == 2:
                                pe.wait_ge(row_steps, q * (GB * NS) + GB * (s + 1))
                            if s == 0 and i == 0 and not first:
                                pe.wait_ge(product_copied[p], q * 2)
                            pair, h = i // 2, i % 2
                            ka, kb = order[2 * pair:2 * pair + 2]
                            start, stop = s == 0 and pair == 0, s == NS - 1 and pair == 1
                            cols = slice(h * HALF, (h + 1) * HALF)
                            nc.tensor.matmul(ps[0:F, h, :], rows_of(p, s, ka), ring[:, r, ka, cols],
                                             start=start, stop=stop)
                            mm = nc.tensor.matmul(ps[F:2 * F, h, :], rows_of(p, s, kb), ring[:, r, kb, cols],
                                                  start=start, stop=stop)
                        mm.then_inc(ring_used, 1)
                        if s == 1 and not first:
                            turn(p, q)
                quarters(pe, work, lambda: turn(p, NQ))

            pe.sem_inc(pair_used, 2)
            pe.wait_ge(turn_read[2], NQ + 1)
            pe.wait_ge(rows_read, NQ)

            def project(n):
                pe.wait_ge(x_q_ready, n)
                pe.wait_ge(sums_copied, n * 4)
                pe.sem_inc(turn_turns, 1)
                for c in range(CB):
                    mm = nc.tensor.transpose(ps[0:F, 4 + c // 4, (c % 4) * P:(c % 4 + 1) * P], x_q[:, c, :], ident[:])
                mm.then_inc(hT_ready, 1)
                pe.wait_ge(hT_copied, n)
                for c in range(CB):
                    a, b = 4 + 2 * (c % 2), 5 + 2 * (c % 2)
                    cols = slice(c * P, (c + 1) * P)
                    if c >= 2:
                        pe.wait_ge(hid_read, (n - 1) * CB + (c - 1))
                        pe.wait_ge(att_read, (n - 1) * CB + (c - 1))
                    nc.tensor.matmul(ps[:, a, :], hT[:, cols], w_hid[:].rearrange("p g n -> p (g n)"),
                                     start=True, stop=False)
                    nc.tensor.matmul(ps[:, a, 0:3 * F], turn_in[:, cols], w_edge[:], start=False, stop=True).then_inc(
                        hid_ready, 1)
                    nc.tensor.matmul(ps[:, b, 0:6 * F], weighted_in[:, cols], w_att[:], start=True, stop=True)
                    nc.tensor.matmul(ps[:, b, 6 * F:6 * F + 2], turn_in[:, cols], w_score[:],
                                     start=True, stop=True).then_inc(att_ready, 1)

            def work(q, first):
                for s in range(NS):
                    r, t = s % RING, s % 2
                    pe.wait_ge(staged_parts, q * (2 * NS) + 2 * (s + 1))
                    for pair in range(2):
                        pe.wait_ge(rect_ready, q * (2 * NS) + (2 * s + pair + 1))
                        if s == 0 and pair == 0 and not first:
                            pe.wait_ge(sums_copied, q * 4)
                        for i in range(2):
                            k = 2 * pair + i
                            start = s == 0 and k == 0
                            stop = s == NS - 1 and k == GB - 1
                            for h in range(2):
                                cols = slice(h * HALF, (h + 1) * HALF)
                                nc.tensor.matmul(ps[0:F, h, :], stage_f[:, t, k, 0:F], ring[:, r, k, cols],
                                                 start=start, stop=stop)
                                nc.tensor.matmul(ps[F:P, h, :], stage_f[:, t, k, 0:F], negs[:, pair, i, cols],
                                                 start=start, stop=stop)
                                for m in range(3):
                                    part = stage_b[:, t, k, m * F:(m + 1) * F]
                                    nc.tensor.matmul(ps[0:F, 2 + h, :], part, more[:, pair, i, cols],
                                                     start=start and m == 0, stop=stop and m == 2)
                                    mm = nc.tensor.matmul(ps[F:P, 2 + h, :], part, less[:, pair, i, cols],
                                                          start=start and m == 0, stop=stop and m == 2)
                        mm.then_inc(pair_used, 1)
                    if s == 1 and not first:
                        project(q)

            quarters(pe, work, lambda: project(NQ))

            pe.wait_ge(hid_read, NB)
            pe.wait_ge(att_read, NB)

            def turn_rows(n):
                pe.wait_ge(normed[1], n + 1)
                if n >= 2:
                    pe.wait_ge(h2T_copied, n - 1)
                for c in range(CB):
                    bank = 2 * (n % 2) + c // 4
                    mm = nc.tensor.transpose(ps[0:F, bank, (c % 4) * P:(c % 4 + 1) * P], X[:, n * CB + c, :], ident[:])
                mm.then_inc(h2T_ready, 1)

            turn_rows(0)
            for n in range(NQ):
                if n + 1 < NQ:
                    turn_rows(n + 1)
                pe.wait_ge(h2T_copied, n + 1)
                for c in range(CB):
                    mm = nc.tensor.matmul(ps[:, 4 + n, c * F:(c + 1) * F], h2T[:, n % 2, c * P:(c + 1) * P], w2_sb[:],
                                          start=True, stop=True)
                mm.then_inc(support_ready, 1)
            pe.wait_ge(support_read, NQ)
            def fold_sums(n):
                pe.wait_ge(sum2_copied, n * 2)
                pe.wait_ge(sum2_read, n)
                for c in range(CB):
                    mm = nc.tensor.matmul(ps[:, 4, c * F:(c + 1) * F], turn_in[:, c * P:(c + 1) * P], fold[:],
                                          start=True, stop=True)
                mm.then_inc(sum2_turned, 1)

            def work(q, first):
                for s in range(NS):
                    t = s % 2
                    if first and s % 2 == 0:
                        pe.wait_ge(part_made[1][2], s // 2 + 1)
                    pe.wait_ge(decay_dve, q * NS + s + 1)
                    pe.wait_ge(decay_act, q * NS + s + 1)
                    if s == 0 and not first:
                        pe.wait_ge(sum2_copied, q * 2)
                    for k in range(GB):
                        for h in range(2):
                            w = decay[:, t, k, h * HALF:(h + 1) * HALF].bitcast(BF16)
                            nc.tensor.matmul(ps[:, h, :], parts[:, s * GB + k, 0:2 * F], w,
                                             start=s == 0 and k == 0, stop=False)
                    for k in (0, 2):
                        for h in range(2):
                            for i in range(2):
                                w = decay[:, t, k + i, h * HALF:(h + 1) * HALF].bitcast(BF16)
                                mm = nc.tensor.matmul(ps[i * F:(i + 1) * F, h, :], parts[:, s * GB + k + i, 2 * F:3 * F], w,
                                                      start=False, stop=s == NS - 1 and k == 2)
                    mm.then_inc(decay_used, 1)
                    if s == 1 and not first:
                        fold_sums(q)

            quarters(pe, work, lambda: fold_sums(NQ))

            pe.wait_ge(sum2_read, NQ + 1)
            for n in range(NQ):
                pe.wait_ge(ext_ready, n + 1)
                if n >= 2:
                    pe.wait_ge(ut_copied, n - 1)
                    pe.wait_ge(vt_copied, n - 1)
                for c in range(CB):
                    bank = 2 * (n % 2) + c // 4
                    mm = nc.tensor.transpose(ps[0:98, bank, (c % 4) * P:(c % 4 + 1) * P], U[:, n * CB + c, :], ident[:])
                mm.then_inc(uv_ready, 1)
            pe.wait_ge(ut_copied, NQ)
            pe.wait_ge(vt_copied, NQ)

            def mirror_products(v, h):
                for c in range(GB):
                    mm = nc.tensor.matmul(ps[0:F + 1, 7, v.k % GB * P:(v.k % GB + 1) * P],
                                          stage_m[:, v.targets_buffer, h * GB + c, :],
                                          mirror_f[:, h, c * P:(c + 1) * P],
                                          start=h == 0 and c == 0, stop=h == 1 and c == GB - 1)
                mm.then_inc(mirrored, 1)

            def turn_g(v, h):
                pe.sem_inc(turn_turns, 1)
                for c in range(GB):
                    mm = nc.tensor.transpose(ps[:, 6, c * P:(c + 1) * P],
                                             both[:, v.k % 4, (h * GB + c) * P:(h * GB + c + 1) * P], ident[:])
                mm.then_inc(g_turned, 1)

            def unit_step(at):
                u = at(0)
                if u:
                    if u.k % GB == 0:
                        pe.wait_ge(staged_stat, u.quad + 1)
                    t = u.k // GB
                    for h in range(2):
                        cols = bass.ds(u.I * QC + h * HALF, HALF)
                        if h == 0 and u.has(1):
                            pe.wait_ge(clamped, 2 * u.n - 1)
                        mm = nc.tensor.matmul(ps[:, h, :], stat[:, t, u.k % GB * P:(u.k % GB + 1) * P], VT[:, cols],
                                              start=True, stop=True)
                    mm.then_inc(dist_ready, 1)
                    for h in range(2):
                        cols = bass.ds(u.I * QC + h * HALF, HALF)
                        if h == 0 and u.has(1):
                            pe.wait_ge(clamped, 2 * u.n)
                        mm = nc.tensor.matmul(ps[:, 2 + h, :], stat[:, t, u.k % GB * P:(u.k % GB + 1) * P],
                                              UT[:, cols], start=True, stop=True)
                    mm.then_inc(dist_ready, 1)
                v = at(4)
                if v and v.off:
                    pe.wait_ge(mirror_weighted, v.offs * 2 + 2)
                    mirror_products(v, 1)
                v = at(3)
                if v and v.off:
                    pe.wait_ge(g_made, v.n + 1)
                    if v.has_off(1):
                        pe.wait_ge(mirror_weighted, v.offs * 2)
                    turn_g(v, 0)
                if v:
                    pe.wait_ge(weighted, v.n + 1)
                    if v.k % GB == 0:
                        pe.wait_ge(staged_rows, 2 * (v.quad + 1))
                    if v.k == 0 and v.has(1):
                        pe.wait_ge(agg_added, v.free[0])
                    for h in range(2):
                        mm = nc.tensor.matmul(ps[0:F + 1, 4 + h, :], stage_f[:, v.k // GB, v.k % GB, :],
                                              ring[:, v.k // GB, v.k % GB, h * HALF:(h + 1) * HALF],
                                              start=v.k == 0, stop=v.k == CB - 1)
                    mm.then_inc(gathered, 1)
                if v and v.off:
                    pe.wait_ge(mirror_weighted, v.offs * 2 + 1)
                    turn_g(v, 1)
                    if v.k == 0:
                        pe.wait_ge(staged_mirror, 2 * (v.mirror_load + 1))
                        if v.has_off(1):
                            pe.wait_ge(agg_added, v.free[1])
                    elif v.k == GB:
                        pe.wait_ge(agg_added, v.adds + 2)
                    mirror_products(v, 0)

            run_units(pe, unit_step)
            pe.wait_ge(agg_added, ADDS)
            for n in range(NQ):
                for b in range(n * CB, (n + 1) * CB):
                    mm = nc.tensor.matmul(ps[:, b // GB, b % GB * (F + 1):(b % GB + 1) * (F + 1)],
                                          aggT[:, b * P:(b + 1) * P], ident[0:F + 1, 0:F + 1], start=True, stop=True)
                mm.then_inc(agg_turned, 1)

            def turn_agg(n):
                pe.wait_ge(tail_steps, TAIL_FIRST + (n + 1) * TAIL_AGG)
                for c in range(CB):
                    mm = nc.tensor.transpose(ps[0:F, 2 * n + c // 4, (c % 4) * P:(c % 4 + 1) * P],
                                             Y[:, n * CB + c, :], ident[:])
                mm.then_inc(moveT_ready, 1)

            turn_agg(0)
            for n in range(NQ):
                if n + 1 < NQ:
                    turn_agg(n + 1)
                pe.wait_ge(moveT_copied, n + 1)
                for c in range(CB):
                    mm = nc.tensor.matmul(ps[:, 2 * n, c * F:(c + 1) * F], moveT[:, n % 2, c * P:(c + 1) * P],
                                          w3_sb[0:F, :], start=True, stop=True)
                mm.then_inc(moved_ready, 1)

        def copy_product(act, p, n):
            act.wait_ge(ring_used, n * NS + p * SLOTS)
            act.wait_ge(turned[p], n)
            nc.scalar.activation(turn_in[:, HALF:QC], ps[:, 1, :], ACT.Copy).then_inc(product_copied[p], 1)

        def split_act(act, i, src, ready):
            for t in range(NQ + 2):
                for m in range(3):
                    n = t - m
                    if 0 <= n < NQ:
                        blocks = slice(n * CB, (n + 1) * CB)
                        if m == 0:
                            act.wait_ge(ready, n + 1)
                        else:
                            act.wait_ge(rest_made[i][m - 1], n + 1)
                        rest = (split_rest[i] if m else src)[:, blocks, :]
                        nc.scalar.activation(parts[:, blocks, m * F:(m + 1) * F], rest, ACT.Copy).then_inc(
                            part_made[i][m], 1)

        def norm_act(act, l):
            act.wait_ge(norm_steps[l], NQ * NORM_SUMS + 1)
            nc.scalar.activation(stats[:, 4, :], stats[:, 3, :], ACT.Sqrt).then_inc(norm_root[l], 1)

        @block.scalar
        def _(act):
            def put(dst, src):
                act.dma_start(dst, src).then_inc(consts_in, 16)

            act.dma_start(X[:], x).then_inc(x_in, 16)
            cheb = cheb_w.rearrange("k i o -> i k o")
            put(cheb_sb[0:F], cheb)
            put(cheb_sb[F:P], cheb)
            put(gatWT_sb[:, 0:F], gatWT)
            put(gatWT_sb[:, F:2 * F], gatWT)
            put(gat_a_sb[:], gat_a2)
            put(winT_sb[:], winT)
            put(w_edge[:], wieT)
            for g, (wT, b_in, b_hid) in enumerate(((wheT, bie, bhe), (whnT, bin_, bhn))):
                put(w_hid[0:F, g, 0:2 * F], wT[:, 0:2 * F])
                put(w_hid[0:F, g, 3 * F:4 * F], wT[:, 2 * F:3 * F])
                put(bias_tmp[F:F + 1, 2 * g, :], b_in)
                put(bias_tmp[F:F + 1, 2 * g + 1, :], b_hid)
            put(w2_sb[:], w2)
            put(w3_sb[0:F, :], w3)
            put(b2_sb[:], b2.broadcast_to([P, F]))
            put(b3_sb[:], b3.broadcast_to([P, F]))
            act.sem_inc(codes_made, 1)

            def code_work(q, first):
                for s in range(NS):
                    t = s % 2
                    if not (first and s < 2):
                        act.wait_ge(codes_stored[t], (q * (NS // 2) + s // 2) * 16)
                    for j, k in enumerate(block_order(0)):
                        if s == 0 and j == 1 and not first:
                            copy_product(act, 0, q)
                        for h in range(2):
                            act.wait_ge(rank_ready, q * (2 * GB * NS) + ((s * GB + j) * 2 + h + 1))
                            nc.scalar.activation(codes[:, t, k, h * HALF:(h + 1) * HALF], ps[:, 6 + h, :], ACT.Relu,
                                                 bias=code_bias[:], scale=1.0).then_inc(codes_made, 1)
                    act.wait_ge(codes_made, q * (2 * GB * NS) + ((s + 1) * GB * 2 + 1))
                    act.dma_start(codes_dram[bass.ds(q * NS + (NS - 1 - s), 1)].rearrange("a p n -> p (a n)"),
                                  codes[:, t].rearrange("p k c -> p (k c)")).then_inc(codes_stored[t], 16)

            quarters(act, code_work, lambda: copy_product(act, 0, NQ))
            act.wait_ge(codes_stored[0], NQ * NS // 2 * 16)
            act.wait_ge(codes_stored[1], NQ * NS // 2 * 16)
            with act.Fori(1, NQ + 1) as n:
                act.wait_ge(ring_used, n * NS + SLOTS)
                act.wait_ge(counts_turned, n)
                nc.scalar.activation(count_in, ps[0:F, 6:8, :], ACT.Copy).then_inc(counts_copied, 1)
                copy_product(act, 1, n)
            with act.Fori(1, NQ + 1) as n:
                copy_product(act, 2, n)
            norm_act(act, 0)

            split_act(act, 0, X[:], normed[0])
            act.preload_act_table_set("exp_and_others")

            def copy_sums(n):
                act.wait_ge(pair_used, n * (2 * NS) + 2)
                act.wait_ge(att_ready, (n - 1) * CB + 1)
                nc.scalar.activation(turn_in[:, HALF:QC], ps[:, 3, :], ACT.Copy).then_inc(sums_copied, 1)
                nc.scalar.activation(weighted_in[:, HALF:QC], ps[:, 1, :], ACT.Copy).then_inc(sums_copied, 1)

            def copy_hidden(n):
                act.wait_ge(hT_ready, n)
                nc.scalar.activation(hT[0:F, :], ps[0:F, 4:6, :], ACT.Copy).then_inc(hT_copied, 1)
                for c in range(CB):
                    act.wait_ge(hid_ready, (n - 1) * CB + (c + 1))
                    if c == 0:
                        act.wait_ge(layer1_sum, n)
                    nc.scalar.activation(hid[:, c].rearrange("p g n -> p (g n)"), ps[:, 4 + 2 * (c % 2), :],
                                         ACT.Copy).then_inc(hid_read, 1)

            def gate_part(n, i):
                if i == 0:
                    act.wait_ge(gate_steps, (n - 1) * GATE_STEPS + G_SCORES)
                    nc.scalar.activation(small[:, 4], small[:, 2], ACT.Exp).then_inc(gate_act, 1)
                    nc.scalar.activation(small[:, 5, :, 0], small[:, 3, :, 1], ACT.Exp).then_inc(gate_act, 1)
                if i == 1:
                    act.wait_ge(gate_steps, (n - 1) * GATE_STEPS + G_SUMS)
                    act.wait_ge(hid_read, n * CB)
                    rz = hid[:, :, :, 0:2 * F].rearrange("p c g n -> p (c g) n")
                    nc.scalar.activation(rz, rz, ACT.Tanh, scale=0.5).then_inc(gate_act, 1)
                if i == 2:
                    act.wait_ge(gate_steps, (n - 1) * GATE_STEPS + G_NEW)
                    nc.scalar.activation(gate[:], gate[:], ACT.Tanh).then_inc(gate_act, 1)

            def sign_work(q, first):
                for s in range(NS):
                    act.wait_ge(loaded[s % RING], loads(3, q, s) * 16)
                    if s < 2:
                        act.wait_ge(diag_cut, q * 2 + s + 1)
                    for pair in range(2):
                        act.wait_ge(pair_used, q * (2 * NS) + (2 * s + pair + 1))
                        nc.scalar.activation(negs[:, pair], ring[:, s % RING, 2 * pair:2 * pair + 2, :], ACT.Relu,
                                             scale=-1.0).then_inc(negs_made, 1)
                        if s == 0 and pair == 0 and not first:
                            copy_sums(q)
                        if s == 2 and pair == 0 and not first:
                            copy_hidden(q)
                        if (s, pair) in GATE_TURNS_ACT and not first:
                            gate_part(q, GATE_TURNS_ACT.index((s, pair)))

            def settle():
                copy_sums(NQ)
                copy_hidden(NQ)
                for i in range(3):
                    gate_part(NQ, i)

            quarters(act, sign_work, settle)
            norm_act(act, 1)

            def copy_rows(n):
                act.wait_ge(h2T_ready, n + 1)
                if n >= 2:
                    act.wait_ge(support_ready, n - 1)
                nc.scalar.activation(h2T[:, n % 2, :], ps[0:F, 2 * (n % 2):2 * (n % 2) + 2, :], ACT.Copy).then_inc(
                    h2T_copied, 1)

            copy_rows(0)
            for n in range(NQ):
                if n + 1 < NQ:
                    copy_rows(n + 1)
                act.wait_ge(support_ready, n + 1)
                nc.scalar.activation(support[:, n * CB:(n + 1) * CB, :].rearrange("p c f -> p (c f)"), ps[:, 4 + n, :],
                                     ACT.Copy, scale=CODE_SCALE).then_inc(support_read, 1)
            split_act(act, 1, support, support_read)

            def copy_sums2(n):
                act.wait_ge(decay_used, n * NS)
                act.wait_ge(sum2_turned, n)
                nc.scalar.activation(turn_in[:, HALF:QC], ps[:, 1, :], ACT.Copy).then_inc(sum2_copied, 1)

            def decay_work(q, first):
                for s in range(NS):
                    act.wait_ge(code_loaded[s % RING], (q * 2 + (s // RING + 1)) * 16)
                    if not (first and s < 2):
                        act.wait_ge(decay_used, q * NS + s - 1)
                    nc.scalar.activation(decay[:, s % 2, 3, :], code_in[:, s % RING, 3, :], ACT.Copy,
                                         scale=128.0).then_inc(decay_act, 1)
                    if s == 0 and not first:
                        copy_sums2(q)

            quarters(act, decay_work, lambda: copy_sums2(NQ))
            norm_act(act, 2)

            for n in range(NQ):
                act.wait_ge(uv_ready, n + 1)
                nc.scalar.activation(UT[:, n * QC:(n + 1) * QC], ps[0:F + 2, 2 * (n % 2):2 * (n % 2) + 2, :],
                                     ACT.Copy).then_inc(ut_copied, 1)
            act.wait_ge(ut_copied, NQ)
            act.wait_ge(vt_copied, NQ)
            act.preload_act_table_set("natural_log_exp_and_others")

            def stage_stat(J, k):
                nc.scalar.activation(stat[:, k // GB, :], UT[:, bass.ds(J * QC + k * P, GB * P)], ACT.Copy,
                                     scale=minus_two[0:F + 2, :]).then_inc(staged_stat, 1)

            def unit_step(at):
                v = at(1)
                if v:
                    act.wait_ge(log_pairs, 2 * v.n + 1)
                    size, rest, a = both[:, v.k % 4], scale[:, v.k % 4], near[:, v.k % 4]
                    nc.scalar.activation(size, size, ACT.Exp, scale=0.5).then_inc(norms_made, 1)
                u = at(0)
                if u:
                    act.wait_ge(clamped, 2 * u.n + 1)
                    nc.scalar.activation(near[:, u.k % 4], near[:, u.k % 4], ACT.Ln)
                    act.wait_ge(clamped, 2 * u.n + 2)
                    nc.scalar.activation(denom[:, u.k % 2], denom[:, u.k % 2], ACT.Ln).then_inc(logs_made, 1)
                if v:
                    act.wait_ge(clipped, v.n + 1)
                    act.wait_ge(log_pairs, 2 * v.n + 2)
                    nc.scalar.activation(a, size, ACT.Ln, bias=1.0, scale=1.0).then_inc(plus_made, 1)
                    nc.scalar.activation(rest, rest, ACT.Exp, scale=-0.5)
                    act.wait_ge(plus_made, v.n + 1)
                    nc.scalar.activation(size, size, ACT.Ln, bias=1.0, scale=-1.0).then_inc(halves_made, 1)
                if u and u.k % GB == 1 and (u.k == 1 or not (isinstance(u.n, int) and u.n > UNITS - CB)):
                    if u.has(GB):
                        act.wait_ge(dist_ready, 2 * GB * u.quad)
                        act.sem_inc(stage_turns, 1)
                    if u.k == 1:
                        stage_stat(u.J, GB)
                    elif not u.off:
                        stage_stat(u.J, 0)
                    else:
                        stage_stat((u.J + 1) % NQ, 0)

            stage_stat(0, 0)
            run_units(act, unit_step)
            for n in range(NQ):
                act.wait_ge(moveT_ready, n + 1)
                if n >= 2:
                    act.wait_ge(moved_ready, n - 1)
                nc.scalar.activation(moveT[:, n % 2, :], ps[0:F, 2 * n:2 * n + 2, :], ACT.Copy).then_inc(
                    moveT_copied, 1)
            act.wait_ge(tail_steps, TAIL_FIRST + NQ * (TAIL_AGG + TAIL_MOVED))
            nc.scalar.activation(stats[:, 1, :], stats[:, 0, :], ACT.Sqrt).then_inc(tail_act, 1)
            act.wait_ge(tail_steps, TAIL_FIRST + NQ * (TAIL_AGG + TAIL_MOVED) + 1)
            nc.scalar.activation(stats[:, 3, :], stats[:, 2, :], ACT.Tanh).then_inc(tail_act, 1)
            norm_act(act, 3)

        @block.vector
        def _(dve):
            V = nc.vector

            def steps_on(s, base=0):
                n = [0]

                def step(ins):
                    n[0] += 1
                    ins.then_inc(s, 1)
                    dve.wait_ge(s, base + n[0])
                return step

            def norm_sums(l, n, squares):
                count = [0]

                def step(ins):
                    count[0] += 1
                    ins.then_inc(norm_steps[l], 1)
                    dve.wait_ge(norm_steps[l], (n - 1) * NORM_SUMS + count[0])

                blocks = bass.ds((n - 1) * CB, CB)
                rows = Y[:, blocks, :]
                step(V.tensor_reduce(stats[:, 0, blocks], rows, AX_X, ALU.add))
                step(V.tensor_scalar(stats[:, 1, blocks], stats[:, 0, blocks], 1.0 / F, None, ALU.mult))
                step(V.tensor_tensor(rows, rows, stats[:, 1, blocks].unsqueeze(2).broadcast_to([P, CB, F]),
                                     ALU.subtract))
                step(V.tensor_tensor(squares, rows, rows, ALU.mult))
                step(V.tensor_reduce(stats[:, 2, blocks], squares, AX_X, ALU.add))
                assert count[0] == NORM_SUMS

            def norm(l):
                step = steps_on(norm_steps[l], NQ * NORM_SUMS)
                step(V.tensor_scalar(stats[:, 3, :], stats[:, 2, :], 1.0 / F, EPS, ALU.mult, ALU.add))
                dve.wait_ge(norm_root[l], 1)
                step(V.reciprocal(stats[:, 5, :], stats[:, 4, :]))
                for n in range(NQ):
                    blocks = slice(n * CB, (n + 1) * CB)
                    V.tensor_tensor(X[:, blocks, :], Y[:, blocks, :],
                                    stats[:, 5, blocks].unsqueeze(2).broadcast_to([P, CB, F]),
                                    ALU.mult).then_inc(normed[l], 1)

            dve.wait_ge(consts_in, N_PUTS * 16)
            dve.wait_ge(consts_made, 1)
            for p in range(3):
                V.tensor_copy(turn_w[:, p, 0:F], fold[:])
            V.tensor_tensor(w_first[:], cheb_sb[0:F, 0, :], cheb_sb[0:F, 2, :], ALU.subtract)
            V.tensor_tensor(turn_w[:, 0, F:P], cheb_sb[:, 1, :], cheb_sb[:, 3, :], ALU.subtract)
            V.tensor_scalar(turn_w[:, 1, F:P], cheb_sb[:, 2, :], 2.0, None, ALU.mult)
            V.tensor_scalar(turn_w[:, 2, F:P], cheb_sb[:, 3, :], 2.0, None, ALU.mult)
            for g in range(2):
                V.memset(w_hid[0:F, g, 2 * F:3 * F], 0.0)
                b_in, b_hid = bias_tmp[F:F + 1, 2 * g, :], bias_tmp[F:F + 1, 2 * g + 1, :]
                V.tensor_tensor(w_hid[F:F + 1, g, 0:2 * F], b_in[:, 0:2 * F], b_hid[:, 0:2 * F], ALU.add)
                V.tensor_copy(w_hid[F:F + 1, g, 2 * F:3 * F], b_in[:, 2 * F:3 * F])
                V.tensor_copy(w_hid[F:F + 1, g, 3 * F:4 * F], b_hid[:, 2 * F:3 * F])
            V.memset(w_att[0:F, 3 * F:6 * F], 0.0)
            V.memset(w_att[F:P, 0:3 * F], 0.0)
            dve.drain().then_inc(weights_made, 1)

            dve.wait_ge(x_in, 32)
            for n in range(4):
                dve.wait_ge(first_ready, n + 1)
                V.tensor_tensor(Y[:, n * 8:(n + 1) * 8, :], ps[:, n, :].rearrange("p (c f) -> p c f", f=F),
                                X[:, n * 8:(n + 1) * 8, :], ALU.add).then_inc(first_read, 1)
            dve.wait_ge(gat_ready, 1)
            V.tensor_copy(w_score[0:F, :], ps[0:F, 4, 0:2])
            V.tensor_copy(w_score[F:P, 0:1], ps[F:P, 4, 1:2])
            V.tensor_copy(w_score[F:P, 1:2], ps[F:P, 4, 0:1])
            V.tensor_copy(w_att[0:F, 0:3 * F], ps[0:F, 5, 0:3 * F])
            V.tensor_scalar(w_att[F:P, 3 * F:6 * F], ps[F:P, 5, 0:3 * F], -1.0, None, ALU.mult)
            dve.drain().then_inc(first_read, 1)
            dve.wait_ge(first_read, 5)

            def copy_product_dve(p, n):
                dve.wait_ge(ring_used, n * NS + p * SLOTS)
                dve.wait_ge(turned[p], n)
                V.tensor_copy(turn_in[:, 0:HALF], ps[:, 0, :]).then_inc(product_copied[p], 1)

            def read_turned(p, n):
                dve.wait_ge(turned[p], n + 1)
                turned_rows = ps[:, 4:6, :].rearrange("p a (c f) -> p (a c) f", f=2 * F)
                blocks = bass.ds(quarter_of(p, n - 1) * CB, CB)
                if p == 0:
                    V.tensor_copy(T1[:, blocks, :], turned_rows[:, :, 0:F])
                if p == 1:
                    V.scalar_tensor_tensor(T2[:, blocks, :], turned_rows[:, :, 0:F], 2.0, X[:, blocks, :],
                                           ALU.mult, ALU.subtract)
                V.tensor_tensor(Y[:, blocks, :], turned_rows[:, :, F:2 * F], Y[:, blocks, :],
                                ALU.add).then_inc(turn_read[p], 1)
                if p == 1:
                    dve.wait_ge(counts_turned, n + 1)
                    V.tensor_copy(degrees[:, blocks, :],
                                  ps[:, 2, 0:2 * CB].rearrange("p (c n) -> p c n", n=2)).then_inc(counts_read, 1)
                if p == 2:
                    dve.wait_ge(rows_turned, n)
                    V.tensor_copy(edge_sum[:, blocks], ps[:, 2, 0:CB]).then_inc(rows_read, 1)
                    dve.wait_ge(turn_read[2], n + 1)
                    norm_sums(0, n, T1[:, blocks, :])

            def settle(p):
                copy_product_dve(p, NQ)
                read_turned(p, NQ)

            def rank_work(q, first):
                for s in range(NS):
                    r, t = s % RING, s % 2
                    dve.wait_ge(loaded[r], loads(0, q, s) * 16)
                    if not (first and s < 2):
                        dve.wait_ge(ring_used, q * NS + s - 1)
                    V.tensor_scalar(mask[:, t], ring[:, r], 0.0, None, ALU.not_equal).then_inc(dve_signs[0], 1)
                    for j in range(GB):
                        if s == 0 and j == 0:
                            V.memset(later[:, t, 0], 0.0).then_inc(signs_ready[0], 1)
                            dve.wait_ge(dve_signs[0], q * NS + s + 1)
                            continue
                        k_seen = block_order(0)[(j - 1) % GB]
                        t_seen = t if j else 1 - t
                        dve.wait_ge(dve_signs[0], q * NS + s + 1)
                        dve.wait_ge(signs_ready[0], q * (GB * NS) + (s * GB + j))
                        V.tensor_tensor(later[:, t, j], later[:, t_seen, (j - 1) % GB], mask[:, t_seen, k_seen],
                                        ALU.add).then_inc(signs_ready[0], 1)
                        if s == 0 and j == 1 and not first:
                            copy_product_dve(0, q)
                    if s == 2 and not first:
                        read_turned(0, q)

            def sign_work(q, first):
                for s in range(NS):
                    r, t = ring_slot(1, s), s % 2
                    dve.wait_ge(loaded[r], loads(1, q, s) * 16)
                    dve.wait_ge(ring_used, q * NS + (SLOTS + s - 1))
                    above = V.tensor_scalar(mask[:, t], ring[:, r], 0.0, None, ALU.is_gt)
                    below = V.tensor_scalar(later[:, t], ring[:, r], 0.0, None, ALU.is_lt)
                    if s >= NS - 2:
                        above.then_inc(dve_signs[1], 1)
                        below.then_inc(dve_signs[1], 1)
                        dve.wait_ge(dve_signs[1], q * 4 + 2 * (s - (NS - 2) + 1))
                        cut = offdiag_b[:].unsqueeze(1).broadcast_to([P, GB, P])
                        for part in (mask, later):
                            mine = own_blocks(part[:, t], s - (NS - 2))
                            below = V.tensor_tensor(mine, mine, cut, ALU.mult)
                    below.then_inc(signs_ready[1], 1)
                    if s == 0 and not first:
                        copy_product_dve(1, q)
                    if s == 2 and not first:
                        read_turned(1, q)

            def row_work(q, first):
                for s in range(NS):
                    dve.wait_ge(loaded[ring_slot(2, s)], loads(2, q, s) * 16)
                    if s == 0 and not first:
                        dve.wait_ge(row_ready, q)
                    for k in range(GB):
                        edges = ring[:, ring_slot(2, s), k, :]
                        if s == 0 and k == 0:
                            V.tensor_copy(row_sum, edges).then_inc(row_steps, 1)
                            if not first:
                                copy_product_dve(2, q)
                        else:
                            dve.wait_ge(row_steps, q * (GB * NS) + (s * GB + k))
                            V.tensor_tensor(row_sum, row_sum, edges, ALU.add).then_inc(row_steps, 1)
                    if s == 2 and not first:
                        read_turned(2, q)
                dve.wait_ge(row_steps, (q + 1) * (GB * NS))
                if not first:
                    dve.wait_ge(rows_turned, q)
                V.tensor_copy(row_out, row_sum).then_inc(row_ready, 1)

            for p, work in enumerate((rank_work, sign_work, row_work)):
                quarters(dve, work, lambda: settle(p))
                dve.wait_ge(turn_read[p], NQ + 1)
            norm(0)

            def split(i, src):
                for t in range(NQ + 1):
                    for m in range(2):
                        n = t - m
                        if 0 <= n < NQ:
                            blocks = slice(n * CB, (n + 1) * CB)
                            dve.wait_ge(part_made[i][m], n + 1)
                            if m:
                                dve.wait_ge(rest_made[i][0], n + 1)
                            rest = (split_rest[i] if m else src)[:, blocks, :]
                            V.tensor_tensor(split_rest[i][:, blocks, :], rest, parts[:, blocks, m * F:(m + 1) * F],
                                            ALU.subtract).then_inc(rest_made[i][m], 1)

            split(0, X[:])
            V.memset(hT[F:F + 1, :], 1.0)

            def copy_sums(n):
                dve.wait_ge(pair_used, n * (2 * NS) + 2)
                dve.wait_ge(att_ready, (n - 1) * CB + 1)
                V.tensor_copy(turn_in[:, 0:HALF], ps[:, 2, :]).then_inc(sums_copied, 1)
                V.tensor_copy(weighted_in[:, 0:HALF], ps[:, 0, :]).then_inc(sums_copied, 1)

            def copy_attention(n):
                for c in range(CB):
                    dve.wait_ge(att_ready, (n - 1) * CB + (c + 1) + 1)
                    V.tensor_copy(att[:, c, :], ps[:, 5 + 2 * (c % 2), 0:6 * F + 2]).then_inc(att_read, 1)
                dve.wait_ge(att_read, n * CB)

            def gate_part(n, i):
                count = [(0, G_SCORES, G_MIXED, G_SUMS, G_NEW, GATE_STEPS)[i]]

                def step(ins):
                    count[0] += 1
                    ins.then_inc(gate_steps, 1)
                    dve.wait_ge(gate_steps, (n - 1) * GATE_STEPS + count[0])

                blocks = bass.ds((n - 1) * CB, CB)
                pairs = [P, CB, 2]
                scores = att[:, :, 6 * F:6 * F + 2]
                num, present, e, top, ex, ex0, z, wt = (small[:, i] for i in (0, 1, 2, 3, 4, 5, 6, 7))
                rz = hid[:, :, :, 0:2 * F].rearrange("p c g n -> p (c g) n")
                reset, update, new_in, new_hid = (hid[:, :, :, i * F:(i + 1) * F] for i in range(4))
                if i == 0:
                    step(V.tensor_copy(num, degrees[:, blocks, :]))
                    step(V.tensor_scalar(present, num, 0.0, None, ALU.is_gt))
                    step(V.scalar_tensor_tensor(e, scores, LEAK, scores, ALU.mult, ALU.max))
                    step(V.tensor_tensor(e, e, present, ALU.mult))
                    step(V.tensor_scalar(present, present, NEG_INF, -NEG_INF, ALU.mult, ALU.add))
                    step(V.tensor_tensor(e, e, present, ALU.add))
                    step(V.tensor_reduce(top[:, :, 0], e, AX_X, ALU.max))
                    step(V.tensor_scalar(top[:, :, 0], top[:, :, 0], -NEG_INF, None, ALU.max))
                    step(V.tensor_tensor(e, e, top[:, :, 0:1].broadcast_to(pairs), ALU.subtract))
                    step(V.tensor_scalar(top[:, :, 1], top[:, :, 0], -1.0, -NEG_INF, ALU.mult, ALU.add))
                    assert count[0] == G_SCORES
                if i == 1:
                    step(V.tensor_reduce(z[:, :, 0], num, AX_X, ALU.add))
                    step(V.tensor_scalar(z[:, :, 0], z[:, :, 0], -1.0, float(N), ALU.mult, ALU.add))
                    dve.wait_ge(gate_act, (n - 1) * 4 + 2)
                    step(V.tensor_tensor(z[:, :, 0], z[:, :, 0], ex0[:, :, 0], ALU.mult))
                    step(V.tensor_tensor(wt, ex, num, ALU.mult))
                    step(V.tensor_reduce(z[:, :, 1], wt, AX_X, ALU.add))
                    step(V.tensor_tensor(z[:, :, 0], z[:, :, 0], z[:, :, 1], ALU.add))
                    step(V.reciprocal(z[:, :, 1], z[:, :, 0]))
                    step(V.tensor_tensor(wt, ex, z[:, :, 1:2].broadcast_to(pairs), ALU.mult))
                    third = [P, CB, 3 * F]
                    step(V.tensor_tensor(att[:, :, 0:3 * F], att[:, :, 0:3 * F], wt[:, :, 0:1].broadcast_to(third),
                                         ALU.mult))
                    step(V.tensor_tensor(att[:, :, 3 * F:6 * F], att[:, :, 3 * F:6 * F], wt[:, :, 1:2].broadcast_to(third),
                                         ALU.mult))
                    assert count[0] == G_MIXED
                if i == 2:
                    step(V.tensor_tensor(att[:, :, 0:3 * F], att[:, :, 0:3 * F], att[:, :, 3 * F:6 * F], ALU.add))
                    dve.wait_ge(hid_read, n * CB)
                    step(V.tensor_tensor(hid[:, :, 1, 0:3 * F], hid[:, :, 1, 0:3 * F], att[:, :, 0:3 * F], ALU.add))
                    assert count[0] == G_SUMS
                if i == 3:
                    dve.wait_ge(gate_act, (n - 1) * 4 + 3)
                    step(V.tensor_scalar(rz, rz, 0.5, 0.5, ALU.mult, ALU.add))
                    step(V.tensor_tensor(gate, reset, new_hid, ALU.mult))
                    step(V.tensor_tensor(gate, gate, new_in, ALU.add))
                    assert count[0] == G_NEW
                if i == 4:
                    dve.wait_ge(gate_act, (n - 1) * 4 + 4)
                    hidden = x_q.unsqueeze(2).broadcast_to([P, CB, 2, F])
                    step(V.tensor_tensor(new_hid, hidden, gate, ALU.subtract))
                    step(V.tensor_tensor(new_hid, new_hid, update, ALU.mult))
                    step(V.tensor_tensor(gate, gate, new_hid, ALU.add))
                    step(V.tensor_tensor(gate[:, :, 0, :], gate[:, :, 0, :], gate[:, :, 1, :], ALU.add))
                    step(V.tensor_tensor(gate[:, :, 0, :], gate[:, :, 0, :],
                                         diag[:, blocks].unsqueeze(2).broadcast_to([P, CB, F]), ALU.mult))
                    assert count[0] == GATE_STEPS
                    V.tensor_tensor(Y[:, blocks, :], gate[:, :, 0, :], x_q, ALU.add).then_inc(layer1_sum, 1)
                if i == 5:
                    dve.wait_ge(layer1_sum, n + 1)
                    norm_sums(1, n, own.rearrange("p k (g f) -> p (k g) f", f=F))

            def sign_work(q, first):
                for s in range(NS):
                    r = s % RING
                    dve.wait_ge(loaded[r], loads(3, q, s) * 16)
                    if s < 2:
                        mine = own_blocks(ring[:, r], s)
                        base = q * 4 + 2 * s
                        V.tensor_tensor(own, mine, ident[:].unsqueeze(1).broadcast_to([P, GB, P]),
                                        ALU.mult).then_inc(diag_steps, 1)
                        dve.wait_ge(diag_steps, base + 1)
                        V.tensor_reduce(diag[:, bass.ds(q * CB + s * GB, GB)], own, AX_X, ALU.add).then_inc(
                            diag_steps, 1)
                        V.tensor_tensor(mine, mine, offdiag[:].unsqueeze(1).broadcast_to([P, GB, P]),
                                        ALU.mult).then_inc(diag_cut, 1)
                        dve.wait_ge(diag_cut, q * 2 + s + 1)
                        dve.wait_ge(diag_steps, base + 2)
                    for pair in range(2):
                        m = 2 * s + pair
                        edges = ring[:, r, 2 * pair:2 * pair + 2, :]
                        dve.wait_ge(pair_used, q * (2 * NS) + (m + 1))
                        V.tensor_scalar(more[:, pair], edges, 0.0, None, ALU.is_gt)
                        V.tensor_scalar(less[:, pair], edges, 0.0, None, ALU.is_lt)
                        dve.wait_ge(negs_made, q * (2 * NS) + (m + 1))
                        V.tensor_scalar(edges, edges, 0.0, None, ALU.max).then_inc(rect_ready, 1)
                        if s == 0 and pair == 0 and not first:
                            copy_sums(q)
                        if s == 2 and pair == 0 and not first:
                            copy_attention(q)
                        if (s, pair) in GATE_TURNS and not first:
                            gate_part(q, GATE_TURNS.index((s, pair)))

            def settle():
                copy_sums(NQ)
                copy_attention(NQ)
                for i in range(6):
                    gate_part(NQ, i)

            quarters(dve, sign_work, settle)
            norm(1)

            split(1, support)

            def copy_sums2(n):
                dve.wait_ge(decay_used, n * NS)
                dve.wait_ge(sum2_turned, n)
                V.tensor_copy(turn_in[:, 0:HALF], ps[:, 0, :]).then_inc(sum2_copied, 1)

            def read_sums2(n):
                dve.wait_ge(sum2_turned, n + 1)
                blocks = bass.ds((n - 1) * CB, CB)
                V.tensor_tensor(Y[:, blocks, :], ps[:, 4, :].rearrange("p (c f) -> p c f", f=F), X[:, blocks, :],
                                ALU.add).then_inc(sum2_read, 1)
                dve.wait_ge(sum2_read, n + 1)
                V.tensor_tensor(Y[:, blocks, :], Y[:, blocks, :], b2_sb[:].unsqueeze(1).broadcast_to([P, CB, F]),
                                ALU.add).then_inc(bias_added, 1)
                dve.wait_ge(bias_added, n)
                norm_sums(2, n, square_room)

            def decay_work(q, first):
                for s in range(NS):
                    dve.wait_ge(code_loaded[s % RING], (q * 2 + (s // RING + 1)) * 16)
                    if not (first and s < 2):
                        dve.wait_ge(decay_used, q * NS + s - 1)
                    V.tensor_scalar(decay[:, s % 2, 0:3, :], code_in[:, s % RING, 0:3, :], 128.0, None,
                                    ALU.mult).then_inc(decay_dve, 1)
                    if s == 0 and not first:
                        copy_sums2(q)
                    if s == 3 and not first:
                        read_sums2(q)

            def settle2():
                copy_sums2(NQ)
                read_sums2(NQ)

            quarters(dve, decay_work, settle2)
            norm(2)

            step = steps_on(ext_steps)
            norm2 = stats[:, 6, :]
            step(V.memset(U[:, :, F:98], 0.0))
            step(V.memset(U[:, :, F + 1:F + 2], 1.0))
            step(V.memset(U[:, :, 96:97], 1.0))
            dve.wait_ge(normed[2], NQ)
            for n in range(NQ):
                blocks = slice(n * CB, (n + 1) * CB)
                step(V.tensor_tensor(Y[:, blocks, :], X[:, blocks, :], X[:, blocks, :], ALU.mult))
                step(V.tensor_reduce(norm2[:, blocks], Y[:, blocks, :], AX_X, ALU.add))
                step(V.tensor_copy(U[:, blocks, 0:F], X[:, blocks, :]))
                step(V.tensor_copy(U[:, blocks, F:F + 1], norm2[:, blocks].unsqueeze(2)))
                step(V.tensor_copy(U[:, blocks, 97:98], norm2[:, blocks].unsqueeze(2)))
                step(V.tensor_scalar(stats[:, 8, blocks], norm2[:, blocks], 1.0, None, ALU.add))
                dve.sem_inc(ext_ready, 1)
            step(V.memset(aggT, 0.0))
            for n in range(NQ):
                dve.wait_ge(ut_copied, n + 1)
                banks = ps[:, 2 * (n % 2):2 * (n % 2) + 2, :]
                V.tensor_copy(VT[0:F, n * QC:(n + 1) * QC], banks[0:F])
                V.tensor_copy(VT[F:F + 2, n * QC:(n + 1) * QC], banks[96:98]).then_inc(vt_copied, 1)
            dve.wait_ge(ut_copied, NQ)
            dve.wait_ge(vt_copied, NQ)

            def mirror_weights(v, h):
                dve.wait_ge(g_turned, v.offs * 2 + h + 1)
                if v.has_off(1):
                    dve.wait_ge(mirrored, v.offs * 2 + h - 1)
                if v.k == 0:
                    dve.wait_ge(loaded[2 + h], (LOADED[4] + v.mirror_load + 1) * 16)
                V.tensor_tensor(mirror_f[:, h, :].rearrange("p (b c) -> p b c", c=P),
                                ps[:, 6, :].rearrange("p (b c) -> p b c", c=P),
                                ring[:, 2 + h, :, v.k * P:(v.k + 1) * P], ALU.mult).then_inc(mirror_weighted, 1)

            def add(cols, sums, before):
                if not (isinstance(before, int) and before == 0):
                    dve.wait_ge(agg_added, before)
                V.tensor_tensor(aggT[:, cols], aggT[:, cols], sums, ALU.add).then_inc(agg_added, 1)

            def unit_step(at):
                v = at(4)
                if v and v.off:
                    mirror_weights(v, 1)
                u = at(0)
                if u:
                    if u.has(4):
                        dve.wait_ge(g_made, u.n - 3)
                    dve.wait_ge(dist_ready, 2 * u.n + 1)
                    V.tensor_scalar(near[:, u.k % 4], ps[:, 0:2, :].rearrange("p h c -> p (h c)"), TINY_Q, None,
                                    ALU.max).then_inc(clamped, 1)
                    if u.has(2):
                        dve.wait_ge(log_pairs, 2 * u.n - 2)
                    dve.wait_ge(dist_ready, 2 * u.n + 2)
                    V.tensor_scalar(denom[:, u.k % 2], ps[:, 2:4, :].rearrange("p h c -> p (h c)"), MIN_NORM, None,
                                    ALU.max).then_inc(clamped, 1)
                v = at(1)
                if v:
                    dve.wait_ge(norms_made, v.n + 1)
                    V.tensor_scalar(both[:, v.k % 4], both[:, v.k % 4], TANH_CLIP, None, ALU.min).then_inc(clipped, 1)
                v = at(4)
                if v and v.off and v.k % GB == GB - 1:
                    dve.wait_ge(mirrored, v.offs * 2 + 2)
                    add(bass.ds(v.J * QC + v.k // GB * HALF, HALF), ps[0:F + 1, 7, :], v.adds + 1 + 2 * (v.k // GB))
                v = at(3)
                if v and v.off:
                    mirror_weights(v, 0)
                v = at(2)
                if v:
                    if v.off:
                        dve.wait_ge(atanh_made, v.offs + 1)
                    else:
                        dve.wait_ge(halves_made, v.n + 1)
                        V.tensor_tensor(near[:, v.k % 4], near[:, v.k % 4], both[:, v.k % 4],
                                        ALU.subtract).then_inc(atanh_diag, 1)
                        dve.wait_ge(atanh_diag, v.J * CB + (v.k + 1))
                    g = both[:, v.k % 4]
                    V.tensor_tensor(g, near[:, v.k % 4], scale[:, v.k % 4], ALU.mult).then_inc(g_made, 1)
                    dve.wait_ge(g_made, v.n + 1)
                    if v.k % GB == 0:
                        dve.wait_ge(loaded[v.k // GB], (LOADED[4] + v.direct_load + 1) * 16)
                    edges = ring[:, v.k // GB, v.k % GB, :]
                    V.tensor_tensor(edges, edges, g, ALU.mult).then_inc(weighted, 1)
                v = at(3)
                if v and v.k == CB - 1:
                    dve.wait_ge(gathered, v.n + 1)
                    add(bass.ds(v.I * QC, QC), ps[0:F + 1, 4:6, :].rearrange("p h c -> p (h c)"),
                        v.adds + (2 if v.off else 0))

            run_units(dve, unit_step)
            step = steps_on(tail_steps)
            wide = [P, CB, F]
            rooms = [t[:].rearrange("p u c -> p (u c)")[:, 0:NB * F].rearrange("p (b f) -> p b f", f=F)
                     for t in (near, scale)]
            room, squares = rooms
            s_dot, s_own, s_b, s_kappa = (stats[:, i, :] for i in (0, 1, 2, 3))
            step(V.tensor_scalar(s_b, norm2, -1.0, 1.0, ALU.mult, ALU.add))
            step(V.tensor_scalar(s_kappa, s_b, MIN_NORM, 0.5, ALU.max, ALU.mult))
            step(V.tensor_scalar(s_dot, edge_sum[:], 1e-8, None, ALU.max))
            step(V.reciprocal(s_own, s_dot))
            step(V.tensor_tensor(s_kappa, s_kappa, s_own, ALU.mult))
            step(V.tensor_tensor(s_b, s_b, s_kappa, ALU.mult))
            for n in range(NQ):
                blocks = slice(n * CB, (n + 1) * CB)
                rows, mine = Y[:, blocks, :], room[:, blocks, :]
                dve.wait_ge(agg_turned, n + 1)
                for b in (n * CB, n * CB + GB):
                    sums = ps[:, b // GB, 0:GB * (F + 1)].rearrange("p (c f) -> p c f", f=F + 1)
                    V.tensor_copy(Y[:, b:b + GB, :], sums[:, :, 0:F])
                    mm = V.tensor_copy(stats[:, 7, b:b + GB], sums[:, :, F])
                step(mm)
                step(V.tensor_tensor(mine, X[:, blocks, :], rows, ALU.mult))
                step(V.tensor_reduce(s_dot[:, blocks], mine, AX_X, ALU.add))
                step(V.scalar_tensor_tensor(s_own[:, blocks], s_dot[:, blocks], 2.0, stats[:, 7, blocks],
                                            ALU.mult, ALU.subtract))
                step(V.tensor_tensor(s_own[:, blocks], s_own[:, blocks], s_kappa[:, blocks], ALU.mult))
                step(V.tensor_tensor(mine, X[:, blocks, :], s_own[:, blocks].unsqueeze(2).broadcast_to(wide),
                                     ALU.mult))
                step(V.tensor_tensor(rows, rows, s_b[:, blocks].unsqueeze(2).broadcast_to(wide), ALU.mult))
                step(V.tensor_tensor(rows, rows, mine, ALU.add))
            for n in range(NQ):
                blocks = slice(n * CB, (n + 1) * CB)
                mine = room[:, blocks, :]
                dve.wait_ge(moved_ready, n + 1)
                step(V.tensor_tensor(mine, ps[:, 2 * n, :].rearrange("p (c f) -> p c f", f=F),
                                     b3_sb[:].unsqueeze(1).broadcast_to(wide), ALU.add))
                step(V.tensor_tensor(squares[:, blocks, :], mine, mine, ALU.mult))
                step(V.tensor_reduce(stats[:, 0, blocks], squares[:, blocks, :], AX_X, ALU.add))
            dve.wait_ge(tail_act, 1)
            step(V.tensor_scalar(stats[:, 2, :], stats[:, 1, :], MIN_NORM, None, ALU.max))
            dve.wait_ge(tail_act, 2)
            step(V.reciprocal(stats[:, 4, :], stats[:, 2, :]))
            step(V.tensor_tensor(stats[:, 5, :], stats[:, 3, :], stats[:, 4, :], ALU.mult))
            for n in range(NQ):
                blocks = slice(n * CB, (n + 1) * CB)
                step(V.tensor_tensor(room[:, blocks, :], room[:, blocks, :],
                                     stats[:, 5, blocks].unsqueeze(2).broadcast_to(wide), ALU.mult))
                step(V.tensor_tensor(Y[:, blocks, :], X[:, blocks, :], room[:, blocks, :], ALU.add))
                norm_sums(3, n + 1, squares[:, blocks, :])
            norm(3)

        @block.sync
        def _(sp):
            for n in range(NQ):
                blocks = slice(n * CB, (n + 1) * CB)
                sp.wait_ge(normed[3], n + 1)
                sp.dma_start(out[:, blocks, :], X[:, blocks, :]).then_inc(out_stored, 16)
            sp.wait_ge(out_stored, NQ * 16)


def lay_out(x, adj, L0_gnn_weight, L1_gnn_W_gat, L1_gnn_a_gat, L1_gnn_w_ih_e, L1_gnn_w_hh_e, L1_gnn_b_ih_e,
            L1_gnn_b_hh_e, L1_gnn_w_ih_n, L1_gnn_w_hh_n, L1_gnn_b_ih_n, L1_gnn_b_hh_n, L2_gnn_weight, L2_gnn_bias,
            L3_gnn_weight, L3_gnn_bias):
    def turn(a):
        return np.ascontiguousarray(np.asarray(a).T)

    def nodes(a):
        return np.ascontiguousarray(np.asarray(a).reshape(NB, P, F).transpose(1, 0, 2))

    def row(a):
        return np.ascontiguousarray(np.asarray(a).reshape(1, -1))

    return {
        "adjT": turn(adj), "x": nodes(x), "xT": turn(x),
        "cheb_w": np.ascontiguousarray(L0_gnn_weight),
        "gatWT": turn(L1_gnn_W_gat), "gat_a2": turn(np.asarray(L1_gnn_a_gat).reshape(2, F)),
        "wieT": turn(L1_gnn_w_ih_e), "wheT": turn(L1_gnn_w_hh_e), "bie": row(L1_gnn_b_ih_e), "bhe": row(L1_gnn_b_hh_e),
        "winT": turn(L1_gnn_w_ih_n), "whnT": turn(L1_gnn_w_hh_n), "bin": row(L1_gnn_b_ih_n), "bhn": row(L1_gnn_b_hh_n),
        "w2": np.ascontiguousarray(L2_gnn_weight), "b2": row(L2_gnn_bias),
        "w3": np.ascontiguousarray(L3_gnn_weight), "b3": row(L3_gnn_bias),
    }


def kernel(**inputs):
    from concourse import bacc
    from concourse.bass_utils import run_bass_kernel_spmd

    nc = bacc.Bacc("TRN2", target_bir_lowering=False, num_devices=1)
    arrays = {f"in_{k}": a for k, a in lay_out(**inputs).items()}
    aps = [nc.dram_tensor(k, a.shape, mybir.dt.from_np(a.dtype), kind="ExternalInput").ap()
           for k, a in arrays.items()]
    out = nc.dram_tensor("out_nodes", (P, NB, F), F32, kind="ExternalOutput").ap()
    adjacency_stack(nc, *aps, out)
    result = run_bass_kernel_spmd(nc, [arrays], core_ids=[0])
    return result.results[0]["out_nodes"].transpose(1, 0, 2).reshape(N, F)
```
